# Optimizing a Trainium2 kernel written in Bass

```python
import numpy as np
import jax
import jax.numpy as jnp

def _softmax(x, axis=-1):
    return jax.nn.softmax(x, axis=axis)

def _gelu(x):
    return jax.nn.gelu(x, approximate=True)

def _silu(x):
    return jax.nn.silu(x)

def _sigmoid(x):
    return jax.nn.sigmoid(x)

def _layernorm(x, axis=-1, eps=1e-05):
    m = jnp.mean(x, axis=axis, keepdims=True)
    v = jnp.var(x, axis=axis, keepdims=True)
    return (x - m) / jnp.sqrt(v + eps)

def _scatter_add(tgt, idx, src, axis=0):
    return tgt.at[idx].add(src)

def _segment_sum(src, seg, n):
    return jax.ops.segment_sum(src, seg, n)
kernel_name = 'mk_early_fusion_embed_d1_tok_img768_r4_2017e7'

def setup_inputs(seed: int=0):
    np.random.seed(seed)
    _w = jnp.asarray

    def _rec_inputs():
        import jax
        import jax.numpy as jnp
        _rk = jax.random.key(seed)
        x = 7.57192e-06 + 1.00007 * jax.random.normal(jax.random.fold_in(_rk, 1), (64, 224, 224, 3), jnp.float32)
        x_txt = jax.random.randint(jax.random.fold_in(_rk, 51), (64, 77), 0, 31999, jnp.int32)
        mask_BS_i2_0 = jnp.where(jnp.ones((64, 77), dtype=bool), 2, 0).astype(jnp.int32)
        return (x, x_txt, mask_BS_i2_0)
    x, x_txt, mask_BS_i2_0 = _rec_inputs()

    def _L0_tok_setup():
        import jax, jax.numpy as jnp
        import numpy as np
        IMG = 224
        P = 16
        HP = P // 2
        D = 192
        C_IN = 3
        B = 64

        def _crop_shift_pad(images, oh, ow):
            th = IMG - HP
            tw = IMG - HP
            out = jnp.zeros_like(images)
            return out.at[:, oh:oh + th, ow:ow + tw, :].set(images[:, oh:oh + th, ow:ow + tw, :])
        key = jax.random.key(seed)
        k1, k2 = jax.random.split(key, 2)
        images = jax.random.normal(k1, (B, IMG, IMG, C_IN), dtype=jnp.float32)
        pvs = P * P * C_IN * 5
        W = jax.random.normal(k2, (pvs, D), dtype=jnp.float32) * 0.02
        b = jnp.zeros((D,), dtype=jnp.float32)
        return {'images': images, 'W': W, 'b': b}
    _L0_tok_all = _L0_tok_setup()
    _L0_tok_in = {k: v for k, v in _L0_tok_all.items() if k in ('W', 'b')}
    del _L0_tok_all

    def _L0_txt_setup():
        import jax, jax.numpy as jnp
        import numpy as np
        VOCAB = 8000
        DIM = 192
        BATCH = 8
        SEQ = 512

        def _sinusoidal_pos(seq_len, dim):
            pos = jnp.arange(seq_len, dtype=jnp.float32)[:, None]
            ids = jnp.arange(dim, dtype=jnp.float32)[None, :]
            even_exp = jnp.floor(ids / 2.0) * 2.0 / dim
            angle = pos / jnp.power(10000.0, even_exp)
            return jnp.where(jnp.arange(dim) % 2 == 0, jnp.sin(angle), jnp.cos(angle))
        key = jax.random.key(seed)
        k1, k2, k3, k4 = jax.random.split(key, 4)
        input_tensor = jax.random.randint(k1, (BATCH, SEQ), 0, VOCAB)
        segment_label = jax.random.randint(k2, (BATCH, SEQ), 0, 3)
        token_table = jax.random.normal(k3, (VOCAB, DIM), dtype=jnp.float32) * 0.02
        segm_table = jax.random.normal(k4, (3, DIM), dtype=jnp.float32) * 0.02
        token_table = token_table.at[0].set(0.0)
        segm_table = segm_table.at[0].set(0.0)
        return {'input_tensor': input_tensor, 'segment_label': segment_label, 'token_table': token_table, 'segm_table': segm_table}
    _L0_txt_all = _L0_txt_setup()
    _L0_txt_in = {k: v for k, v in _L0_txt_all.items() if k in ('token_table', 'segm_table')}
    del _L0_txt_all

    def _L0_attn_setup():
        import jax, jax.numpy as jnp
        import numpy as np
        EMBED_DIM = 192
        NUM_HEADS = 12
        HEAD_DIM = EMBED_DIM // NUM_HEADS
        SCALING = HEAD_DIM ** (-0.5)
        B, N = (4, 512)
        key = jax.random.key(seed)
        k_x, k_wqkv, k_bqkv, k_wo, k_bo = jax.random.split(key, 5)
        s = EMBED_DIM ** (-0.5)
        return {'x_q': jax.random.normal(k_x, (B, N, EMBED_DIM), dtype=jnp.float32), 'w_qkv': jax.random.normal(k_wqkv, (3 * EMBED_DIM, EMBED_DIM), dtype=jnp.float32) * s, 'b_qkv': jax.random.normal(k_bqkv, (3 * EMBED_DIM,), dtype=jnp.float32) * s, 'w_out': jax.random.normal(k_wo, (EMBED_DIM, EMBED_DIM), dtype=jnp.float32) * s, 'b_out': jax.random.normal(k_bo, (EMBED_DIM,), dtype=jnp.float32) * s}
    _L0_attn_all = _L0_attn_setup()
    _L0_attn_in = {k: v for k, v in _L0_attn_all.items() if k in ('w_qkv', 'b_qkv', 'w_out', 'b_out')}
    del _L0_attn_all

    def _L0_ffn_setup():
        import jax, jax.numpy as jnp
        import numpy as np
        CAPACITY_FACTOR = 1.25
        key = jax.random.key(seed)
        ks = jax.random.split(key, 5)
        B, S, D, F, E = (8, 512, 192, 768, 8)
        return {'x': jax.random.normal(ks[0], (B, S, D), jnp.float32), 'switch_w': jax.random.normal(ks[1], (D, E), jnp.float32) * 0.02, 'switch_b': jnp.zeros((E,), jnp.float32), 'w1': jax.random.normal(ks[2], (E, D, F), jnp.float32) * 0.02, 'b1': jnp.zeros((E, F), jnp.float32), 'w2': jax.random.normal(ks[3], (E, F, D), jnp.float32) * 0.02, 'b2': jnp.zeros((E, D), jnp.float32)}
    _L0_ffn_all = _L0_ffn_setup()
    _L0_ffn_in = {k: v for k, v in _L0_ffn_all.items() if k in ('switch_w', 'switch_b', 'w1', 'b1', 'w2', 'b2')}
    del _L0_ffn_all
    return {'x': x, 'x_txt': x_txt, 'mask_BS_i2_0': mask_BS_i2_0, 'L0_tok_W': _L0_tok_in['W'], 'L0_tok_b': _L0_tok_in['b'], 'L0_txt_token_table': _L0_txt_in['token_table'], 'L0_txt_segm_table': _L0_txt_in['segm_table'], 'L0_attn_w_qkv': _L0_attn_in['w_qkv'], 'L0_attn_b_qkv': _L0_attn_in['b_qkv'], 'L0_attn_w_out': _L0_attn_in['w_out'], 'L0_attn_b_out': _L0_attn_in['b_out'], 'L0_ffn_switch_w': _L0_ffn_in['switch_w'], 'L0_ffn_switch_b': _L0_ffn_in['switch_b'], 'L0_ffn_w1': _L0_ffn_in['w1'], 'L0_ffn_b1': _L0_ffn_in['b1'], 'L0_ffn_w2': _L0_ffn_in['w2'], 'L0_ffn_b2': _L0_ffn_in['b2']}

def reference(x, x_txt, mask_BS_i2_0, L0_tok_W, L0_tok_b, L0_txt_token_table, L0_txt_segm_table, L0_attn_w_qkv, L0_attn_b_qkv, L0_attn_w_out, L0_attn_b_out, L0_ffn_switch_w, L0_ffn_switch_b, L0_ffn_w1, L0_ffn_b1, L0_ffn_w2, L0_ffn_b2):
    import jax
    import jax.numpy as jnp

    def _L0_tok_ref(images, W, b):
        import jax, jax.numpy as jnp
        import numpy as np
        IMG = 224
        P = 16
        HP = P // 2
        D = 192
        C_IN = 3
        B = 64

        def _crop_shift_pad(images, oh, ow):
            th = IMG - HP
            tw = IMG - HP
            out = jnp.zeros_like(images)
            return out.at[:, oh:oh + th, ow:ow + tw, :].set(images[:, oh:oh + th, ow:ow + tw, :])
        offsets = [(0, 0), (HP, 0), (0, HP), (HP, HP)]
        concat = jnp.concatenate([images] + [_crop_shift_pad(images, oh, ow) for oh, ow in offsets], axis=-1)
        Bn, _, _, C = concat.shape
        g = IMG // P
        x = concat.reshape(Bn, g, P, g, P, C)
        x = x.transpose(0, 1, 3, 2, 4, 5).reshape(Bn, g * g, P * P * C)
        return x @ W + b

    def _L0_txt_ref(input_tensor, segment_label, token_table, segm_table):
        import jax, jax.numpy as jnp
        import numpy as np
        VOCAB = 8000
        DIM = 192
        BATCH = 8
        SEQ = 512

        def _sinusoidal_pos(seq_len, dim):
            pos = jnp.arange(seq_len, dtype=jnp.float32)[:, None]
            ids = jnp.arange(dim, dtype=jnp.float32)[None, :]
            even_exp = jnp.floor(ids / 2.0) * 2.0 / dim
            angle = pos / jnp.power(10000.0, even_exp)
            return jnp.where(jnp.arange(dim) % 2 == 0, jnp.sin(angle), jnp.cos(angle))
        batch, seq = input_tensor.shape
        pos = _sinusoidal_pos(seq, token_table.shape[1])
        tokens_embed = token_table[input_tensor]
        segments_embed = segm_table[segment_label]
        return segments_embed + pos[None, :, :] + tokens_embed

    def _L0_attn_ref(x_q, w_qkv, b_qkv, w_out, b_out):
        import jax, jax.numpy as jnp
        import numpy as np
        EMBED_DIM = 192
        NUM_HEADS = 12
        HEAD_DIM = EMBED_DIM // NUM_HEADS
        SCALING = HEAD_DIM ** (-0.5)
        B, N = (4, 512)
        b_sz, n, _ = x_q.shape
        qkv = jnp.einsum('bne,fe->bnf', x_q, w_qkv) + b_qkv
        qkv = qkv.reshape(b_sz, n, 3, NUM_HEADS, HEAD_DIM).transpose(0, 3, 2, 1, 4)
        q, k, v = (qkv[:, :, 0], qkv[:, :, 1], qkv[:, :, 2])
        q = q * SCALING
        attn = jnp.einsum('bhqd,bhkd->bhqk', q, k) + 1.0
        attn = jax.nn.softmax(attn, axis=-1)
        out = jnp.einsum('bhqk,bhkd->bhqd', attn, v)
        out = out.transpose(0, 2, 1, 3).reshape(b_sz, n, EMBED_DIM)
        return jnp.einsum('bne,fe->bnf', out, w_out) + b_out

    def _L0_ffn_ref(x, switch_w, switch_b, w1, b1, w2, b2):
        import jax, jax.numpy as jnp
        import numpy as np
        CAPACITY_FACTOR = 1.25
        B, S, D = x.shape
        E = w1.shape[0]
        xf = x.reshape(-1, D)
        N = xf.shape[0]
        capacity = int(CAPACITY_FACTOR * N / E)
        probs = jax.nn.softmax(xf @ switch_w + switch_b, axis=-1)
        prob_max = jnp.max(probs, axis=-1)
        routes = jnp.argmax(probs, axis=-1)
        sort_idx = jnp.lexsort((-prob_max, routes))
        counts = jnp.bincount(routes, length=E)
        starts = jnp.concatenate([jnp.zeros((1,), counts.dtype), jnp.cumsum(counts)[:-1]])
        rank_sorted = jnp.arange(N) - starts[routes[sort_idx]]
        rank = jnp.zeros((N,), jnp.int32).at[sort_idx].set(rank_sorted.astype(jnp.int32))
        keep = rank < capacity
        dest_e = jnp.where(keep, routes, E)
        dest_c = jnp.where(keep, rank, 0)
        buf = jnp.zeros((E + 1, capacity, D), xf.dtype).at[dest_e, dest_c].set(xf)
        h = jax.nn.gelu(jnp.einsum('ecd,edf->ecf', buf[:E], w1) + b1[:, None, :], approximate=False)
        o = jnp.einsum('ecf,efd->ecd', h, w2) + b2[:, None, :]
        y_exp = o[routes, dest_c]
        y = jnp.where(keep[:, None], y_exp, xf)
        out = y * prob_max[:, None]
        return out.reshape(B, S, D)
    h = _L0_tok_ref(x, L0_tok_W, L0_tok_b)
    h = jnp.concatenate([h, _L0_txt_ref(x_txt, mask_BS_i2_0, L0_txt_token_table, L0_txt_segm_table)], axis=1)
    h = h + _L0_attn_ref(_layernorm(h, axis=-1), L0_attn_w_qkv, L0_attn_b_qkv, L0_attn_w_out, L0_attn_b_out)
    h = h + _L0_ffn_ref(_layernorm(h, axis=-1), L0_ffn_switch_w, L0_ffn_switch_b, L0_ffn_w1, L0_ffn_b1, L0_ffn_w2, L0_ffn_b2)
    return h

_drawn_inputs = setup_inputs


def setup_inputs(seed=0):
    import zlib

    import numpy as np

    out = dict(_drawn_inputs(seed))
    spreads = {'L0_tok_b': (0.0, 0.1),
     'L0_ffn_switch_b': (0.0, 0.1),
     'L0_ffn_b1': (0.0, 0.8),
     'L0_ffn_b2': (0.0, 0.528)}
    factors = {'L0_txt_token_table': 3.307,
     'L0_txt_segm_table': 3.12,
     'L0_ffn_w1': 4.591,
     'L0_ffn_w2': 4.236}
    for name, (base, spread) in spreads.items():
        noise = np.random.default_rng([zlib.crc32(name.encode()), seed]).standard_normal(out[name].shape)
        drawn = base * np.exp(spread * noise) if base else spread * noise
        out[name] = jnp.asarray(drawn.astype(out[name].dtype))
    for name, factor in factors.items():
        out[name] = (out[name] * factor).astype(out[name].dtype)
    return out
```

```python
import numpy as np
import concourse.bass as bass
from concourse import mybir
from contextlib import ExitStack

fp32 = mybir.dt.float32
bf16 = mybir.dt.bfloat16
i32 = mybir.dt.int32
ALU = mybir.AluOpType
ACT = mybir.ActivationFunctionType
AX = mybir.AxisListType

BATCH = 64
IMG = 224
PATCH = 16
GRID = IMG // PATCH
CH = 3
D = 192
TXT = 77
NIMG = GRID * GRID
NTOK = TXT + NIMG
GROUPS = 5
ROW = IMG * CH
SEG = PATCH * CH
KC = 6
EW = SEG // KC
D, NTOK, HEADS, HD = 192, 273, 12, 16
QT = 3
P = NTOK // QT
KH = D // 2
GRP = 3
E = 8
RW = D + 4
LEAD = 8
SLOTS = 18
Q_PART = (0, 0, 0, 1, 1, 2)
K_PART = (0, 1, 2, 0, 1, 0)
TAIL = ("OUT0", "OUT1", "X0", "X1", "LG", "RK")
PREP = ("T0", "T1", "Q0", "Q1", "K0", "K1", "V0", "V1", "MT0")
MISC = ("T0", "T1", "Q0", "OUT0", "Q1", "OUT1", "MT1", "K0", "K1", "V0", "V1", "X0", "X1", "LG", "MT2", "RK", "MT0")
D, F, E, RW = 192, 768, 8, 196
FC = F // 128
NOWHERE = 1000000


def patch_embed(nc, x, W, tok_b, idx_tok, idx_seg, tok_table, seg_table, pos, ident_in, h):
    half = 64
    tile_units = GRID
    with ExitStack() as ctx:
        def sb(name, shape, dt=fp32):
            return ctx.enter_context(nc.sbuf_tensor(name, shape, dt))

        def sem(name):
            return ctx.enter_context(nc.semaphore(name))

        img = [sb(f"img{i}", [128, PATCH * ROW]) for i in range(2)]
        wraw = sb("wraw", [128, KC, GROUPS, D])
        wv = [[sb(f"w_{r}_{c}", [128, KC, D]) for c in ("all", "off")] for r in ("mid", "top", "bottom")]
        patch = [sb(f"patch{i}", [128, KC * 128]) for i in range(2)]
        patchT = [sb(f"patchT{i}", [128, KC, 128]) for i in range(2)]
        stage = [sb(f"stage{i}", [128, GRID, D]) for i in range(2)]
        bias = sb("tok_bias", [128, D])
        ident = sb("identA", [128, 128])
        psT = [ctx.enter_context(nc.psum_tensor(f"psT{i}", [128, 2, 512], fp32)) for i in range(2)]
        psO = [ctx.enter_context(nc.psum_tensor(f"psO{i}", [128, 512], fp32)) for i in range(2)]
        idx_all = [sb(f"idx_all{i}", [TXT, BATCH], i32) for i in range(2)]
        idx_f = [sb(f"idx_f{i}", [TXT, BATCH]) for i in range(2)]
        wrap = [sb(f"idx_wrapped{i}", [TXT, BATCH]) for i in range(2)]
        idx_now = [[sb(f"idx_now{i}{j}", [TXT, 1], i32) for j in range(2)] for i in range(2)]
        tok_rows = [sb(f"tok_rows{i}", [TXT, D]) for i in range(2)]
        seg_rows = [sb(f"seg_rows{i}", [TXT, D]) for i in range(2)]
        txt_sum = [sb(f"txt_sum{i}", [TXT, D]) for i in range(2)]
        pos_sb = sb("pos_sb", [TXT, D])

        w_loaded, const_loaded, w_ready = sem("w_loaded"), sem("const_loaded"), sem("w_ready")
        img_loaded = [sem(f"img_loaded{i}") for i in range(2)]
        ordered, transposed = sem("ordered"), sem("transposed")
        copied_dve, copied_act = sem("copied_dve"), sem("copied_act")
        embedded, staged = sem("embedded"), sem("staged")
        stored = [sem(f"stored{i}") for i in range(2)]
        txt_idx, txt_got, txt_out = sem("txt_idx"), sem("txt_got"), sem("txt_out")
        block = ctx.enter_context(nc.Block())

        h_rows = h.rearrange("b t d -> b (t d)")

        def out_rows(gy):
            return h_rows[:, bass.ds((TXT + gy * GRID) * D, GRID * D)]

        x_rows = x.rearrange("b (gy r) w c -> gy b (r w c)", gy=GRID)

        @block.sync
        def _(sp):
            def load(par, gys):
                for i, gy in enumerate(gys):
                    for q in range(2):
                        n = PATCH * ROW // 2
                        src = x_rows[bass.ds(gy, 1), :, q * n:(q + 1) * n].rearrange("o b n -> (o b) n")
                        sp.dma_start(img[par][i * half:(i + 1) * half, q * n:(q + 1) * n], src)\
                          .then_inc(img_loaded[par], 16)

            def store(par, gys):
                for i, gy in enumerate(gys):
                    sp.dma_start(out_rows(gy), stage[par][i * half:(i + 1) * half, :, :]
                                 .rearrange("p g d -> p (g d)")).then_inc(stored[par], 16)

            load(0, (1, 2))
            load(1, (3, 4))
            with sp.Fori(0, 2, 1) as pair:
                k = 2 * pair
                for par in range(2):
                    sp.wait_ge(w_ready, 1)
                    sp.wait_ge(ordered, (k + par) * tile_units + tile_units)
                    load(par, (2 * k + 2 * par + 5, 2 * k + 2 * par + 6))
                    sp.wait_ge(w_ready, 1)
                    sp.wait_ge(staged, (k + par) * tile_units + tile_units + 2)
                    store(par, (2 * k + 2 * par + 1, 2 * k + 2 * par + 2))
            sp.wait_ge(ordered, 5 * tile_units)
            load(0, (0, GRID - 1))
            sp.wait_ge(staged, 5 * tile_units + 2)
            store(0, (9, 10))
            sp.wait_ge(staged, 6 * tile_units + 2)
            store(1, (11, 12))
            sp.wait_ge(staged, 7 * tile_units + 2)
            store(0, (0, GRID - 1))
            sp.wait_ge(stored[0], 4 * 32 + 32)
            sp.wait_ge(stored[1], 3 * 32 + 32)

        @block.scalar
        def _(act):
            act.dma_start(ident[:, :], ident_in).then_inc(const_loaded, 16)
            act.dma_start(bias[:, :], tok_b.rearrange("(o n) -> o n", o=1).broadcast_to([128, D]))\
               .then_inc(const_loaded, 16)
            wrows = W.rearrange("(py px g c) n -> px c py g n", px=PATCH, g=GROUPS, c=CH)
            for k in range(KC):
                for e in range(EW):
                    px, c = divmod(EW * k + e, CH)
                    act.dma_start(wraw[e:e + EW * (PATCH - 1) + 1:EW, k, :, :], wrows[px, c])\
                       .then_inc(w_loaded, 16)
            act.sem_inc(copied_act, 2)

            def copies(u0, n):
                for i in range(n):
                    act.wait_ge(transposed, u0 + i + 3)
                    act.wait_ge(embedded, u0 + i + 1)
                    nc.scalar.activation(patchT[i % 2][:, 3:6, :].rearrange("p k n -> p (k n)"),
                                         psT[i % 2][:, 1, 0:384], ACT.Copy).then_inc(copied_act, 1)
            with act.Fori(0, 3, 1) as pair:
                k = 2 * pair
                copies(k * tile_units, 2 * tile_units)
            copies(6 * tile_units, tile_units)

        @block.tensor
        def _(pe):
            pe.wait_ge(const_loaded, 32)
            pe.sem_inc(embedded, 2)
            pe.sem_inc(transposed, 2)

            def embed(par, u0, border=False):
                def transposes(g):
                    u = u0 + g
                    pe.wait_ge(ordered, u + 1)
                    pe.wait_ge(copied_dve, u + 1)
                    pe.wait_ge(copied_act, u + 1)
                    for k in range(KC):
                        last = nc.tensor.transpose(psT[g % 2][:, k // 3, (k % 3) * 128:(k % 3) * 128 + 128],
                                                   patch[g % 2][:, k * 128:(k + 1) * 128], ident[:, :])
                    last.then_inc(transposed, 1)

                def product(g):
                    u = u0 + g
                    pe.wait_ge(copied_dve, u + 3)
                    pe.wait_ge(copied_act, u + 3)
                    pe.wait_ge(staged, u + 1)
                    for rows, m0, m1 in (((1, 0, half), (2, half, 128)) if border else ((0, 0, 128),)):
                        for k in range(KC):
                            off = (g == 0 and k < 3) or (g == GRID - 1 and k >= 3)
                            last = nc.tensor.matmul(psO[g % 2][m0:m1, 0:D], patchT[g % 2][:, k, m0:m1],
                                                    wv[rows][off][:, k, :], start=(k == 0), stop=(k == KC - 1))
                    last.then_inc(embedded, 1)
                transposes(0)
                for g in range(GRID):
                    if g + 1 < GRID:
                        transposes(g + 1)
                    if g == 0:
                        pe.wait_ge(w_ready, 1)
                    product(g)

            with pe.Fori(0, 3, 1) as pair:
                k = 2 * pair
                for par in range(2):
                    embed(par, k * tile_units + par * tile_units)
            embed(0, 6 * tile_units, border=True)

        @block.vector
        def _(dve):
            dve.sem_inc(copied_dve, 2)
            dve.sem_inc(staged, 2)
            dve.sem_inc(stored[0], 32)
            dve.sem_inc(stored[1], 32)
            dve.wait_ge(w_loaded, 16 * KC * EW)

            def total(dst, groups, chunks, p0=0, p1=128):
                out = dst[p0:p1, chunks, :]
                src = [wraw[p0:p1, chunks, g, :] for g in groups]
                nc.vector.tensor_tensor(out, src[0], src[1], ALU.add)
                for s in src[2:]:
                    dve.drain()
                    nc.vector.tensor_tensor(out, out, s, ALU.add)
            every, left, right = slice(0, KC), slice(0, 3), slice(3, KC)
            (mid, mid_off), (top, top_off), (bot, bot_off) = wv
            total(mid, (0, 1, 2, 3, 4), every)
            total(top, (0, 1, 2, 3, 4), every, half, 128)
            total(top, (0, 1, 3), every, 0, half)
            total(bot, (0, 1, 2, 3, 4), every, 0, half)
            total(bot, (0, 2, 4), every, half, 128)
            for side, g_mid, g_top, g_bot in ((left, (0, 1, 2), (0, 1), (0, 2)), (right, (0, 3, 4), (0, 3), (0, 4))):
                total(mid_off, g_mid, side)
                total(top_off, g_mid, side, half, 128)
                total(top_off, g_top, side, 0, half)
                total(bot_off, g_mid, side, 0, half)
                total(bot_off, g_bot, side, half, 128)
            dve.drain().then_inc(w_ready, 1)
            dve.wait_ge(const_loaded, 32)

            def order(par, u0, g):
                dve.wait_ge(transposed, u0 + g + 1)
                src = img[par][:, :].rearrange("p (r n) -> p r n", r=PATCH)[:, :, g * SEG:(g + 1) * SEG]
                nc.vector.tensor_copy(patch[g % 2][:, :].rearrange("p (k r e) -> p k r e", k=KC, r=PATCH),
                                      src.rearrange("p r (k e) -> p k r e", k=KC)).then_inc(ordered, 1)

            def tile(par, u0, stores, loads):
                def copy(g):
                    u = u0 + g
                    dve.wait_ge(transposed, u + 3)
                    dve.wait_ge(embedded, u + 1)
                    nc.vector.tensor_copy(patchT[g % 2][:, 0:3, :].rearrange("p k n -> p (k n)"),
                                          psT[g % 2][:, 0, 0:384]).then_inc(copied_dve, 1)
                dve.wait_ge(img_loaded[par], loads)
                order(par, u0, 0)
                order(par, u0, 1)
                copy(0)
                dve.wait_ge(stored[par], stores)
                for g in range(GRID):
                    if g + 1 < GRID:
                        copy(g + 1)
                    if g + 2 < GRID:
                        order(par, u0, g + 2)
                    dve.wait_ge(embedded, u0 + g + 3)
                    nc.vector.tensor_tensor(stage[par][:, g, :], psO[g % 2][:, 0:D], bias[:, :], ALU.add)\
                      .then_inc(staged, 1)
            with dve.Fori(0, 3, 1) as pair:
                k = 2 * pair
                for par in range(2):
                    tile(par, k * tile_units + par * tile_units, k * 16 + 32, k * 32 + 64)
            tile(0, 6 * tile_units, 3 * 32 + 32, 4 * 64)

        @block.gpsimd
        def _(pool):
            pool.dma_start(idx_all[0][:, :], idx_tok).then_inc(txt_idx, 16)
            pool.dma_start(idx_all[1][:, :], idx_seg).then_inc(txt_idx, 16)
            pool.dma_start(pos_sb[:, :], pos).then_inc(txt_idx, 16)
            pool.wait_ge(txt_idx, 48)
            for i, size in enumerate((tok_table.shape[0], seg_table.shape[0])):
                nc.gpsimd.tensor_copy(idx_f[i][:, :], idx_all[i][:, :])
                pool.drain()
                nc.gpsimd.tensor_scalar(wrap[i][:, :], idx_f[i][:, :], 0.0, float(size), ALU.is_lt, ALU.mult)
                pool.drain()
                nc.gpsimd.tensor_tensor(wrap[i][:, :], wrap[i][:, :], idx_f[i][:, :], ALU.add)
                pool.drain()
                nc.gpsimd.tensor_scalar(wrap[i][:, :], wrap[i][:, :], 0.0, float(size - 1), ALU.max, ALU.min)
                pool.drain()

            def gather(b, par):
                for i, (table, rows) in enumerate(((tok_table, tok_rows), (seg_table, seg_rows))):
                    nc.gpsimd.tensor_copy(idx_now[i][par][:, :], wrap[i][:, bass.ds(b, 1)])
                pool.drain()
                for i, (table, rows) in enumerate(((tok_table, tok_rows), (seg_table, seg_rows))):
                    pool.indirect_dma_start(rows[par][:, :], None, table,
                                            bass.IndirectOffsetOnAxis(ap=idx_now[i][par][:, 0:1], axis=0))\
                        .then_inc(txt_got, 16)

            def add(b, par, got, free):
                pool.wait_ge(txt_idx, 48)
                pool.wait_ge(txt_got, got)
                if free is not None:
                    pool.wait_ge(txt_out, free)
                nc.gpsimd.tensor_tensor(txt_sum[par][:, :], seg_rows[par][:, :], pos_sb[:, :], ALU.add)
                pool.drain()
                nc.gpsimd.tensor_tensor(txt_sum[par][:, :], txt_sum[par][:, :], tok_rows[par][:, :], ALU.add)
                pool.drain()
                pool.dma_start(h[bass.ds(b, 1), 0:TXT, :].rearrange("o t d -> (o t) d"), txt_sum[par][:, :])\
                    .then_inc(txt_out, 16)
            gather(0, 0)
            for b in range(2):
                gather(b + 1, (b + 1) % 2)
                add(b, b, 32 * (b + 1), None)
            with pool.Fori(1, BATCH // 2 - 1, 1) as pair:
                b = 2 * pair
                for par in range(2):
                    gather(b + par + 1, (par + 1) % 2)
                    add(b + par, par, b * 32 + par * 32 + 32, b * 16 + par * 16 - 16)
            gather(BATCH - 1, 1)
            for b in (BATCH - 2, BATCH - 1):
                add(b, b % 2, 32 * (b + 1), 16 * (b - 1))
            pool.wait_ge(txt_out, 16 * BATCH)


def attention(nc, NB, h, wqkvT, bqkv, woT, bo, sw, swb, ident_in, sel_in, tri_in, c8_in, tok_in, run_in,
              xs, stack, p_all_d, r_all_d, cnt_d):
    FIRST = len(PREP)
    BODY0 = len(MISC) - len(TAIL)

    def misc_at(b, name, last=False, first=False):
        if isinstance(b, str):
            return PREP.index(name)
        if first:
            return FIRST + [m for m in MISC if m not in TAIL].index(name)
        base = FIRST + BODY0 + len(MISC) * (b - 1)
        if last:
            return base + [m for m in MISC if m not in PREP].index(name)
        if isinstance(b, int) and b == NB:
            return base - len(PREP) + TAIL.index(name)
        return base + MISC.index(name)

    with ExitStack() as ctx:
        def sb(name, shape, dt=fp32):
            return ctx.enter_context(nc.sbuf_tensor(name, shape, dt))

        def sem(name):
            return ctx.enter_context(nc.semaphore(name))

        ident, identb = sb("identB", [128, 128]), sb("identb", [128, 128], bf16)
        w_qkv = sb("w_qkv", [KH + 1, 2, 3 * D])
        w_out = sb("w_out", [128, GRP, D])
        w_sw = sb("w_sw", [KH + 1, 2, E])
        sel_f, sel = sb("sel_f", [12, 4, P]), sb("sel", [12, 4, P], bf16)
        tri, ones = sb("tri", [P, P]), sb("ones", [P, P])
        c8 = sb("c8", [P, QT, E])
        tok_all = sb("tok_all", [P, NB * QT])
        p_all, r_all = sb("p_all", [P, NB * QT]), sb("r_all", [P, NB * QT])
        h_in = [sb(f"h_in{i}", [P, QT, D]) for i in range(2)]
        h_res = [sb(f"h_res{i}", [P, QT, D]) for i in range(2)]
        stats, mv = sb("stats", [P, QT, 6]), sb("mv", [P, QT, 2])
        var_eps, rstd, mhalf = sb("var_eps", [P, QT]), sb("rstd", [P, QT]), sb("mhalf", [P, QT])
        xn = [sb(f"xn{i}", [P, QT, D]) for i in range(2)]
        xnT = sb("xnT", [KH + 1, 2, NTOK])
        qk_f = sb("qk_f", [KH, 4, NTOK])
        qk_r = sb("qk_r", [KH, 4, NTOK])
        parts = sb("parts", [KH, 4, 3, NTOK], bf16)
        Qs = [sb(f"Qs{i}", [KH, HEADS, NTOK], bf16) for i in range(2)]
        Ks = [sb(f"Ks{i}", [KH, HEADS, NTOK], bf16) for i in range(2)]
        V = [sb(f"V{i}", [P, QT, HEADS, 32]) for i in range(2)]
        neg_max = [sb(f"neg_max{i}", [P, QT, HEADS]) for i in range(2)]
        shift_r = sb("shift_r", [P, QT, 4])
        shift = sb("shift", [P, QT, 4, 3], bf16)
        mT = [sb(f"mT{i}", [12, NTOK], bf16) for i in range(GRP)]
        Pr = [sb(f"Pr{i}", [P, 2, NTOK]) for i in range(4)]
        rsum = sb("rsum", [128, NTOK])
        On = [sb(f"On{i}", [128, GRP, NTOK]) for i in range(2)]
        row = [sb(f"row{i}", [P, QT, RW]) for i in range(2)]
        stats2, mv2 = sb("stats2", [P, QT, 6]), sb("mv2", [P, QT, 2])
        var_eps2, rstd2 = sb("var_eps2", [P, QT]), sb("rstd2", [P, QT])
        xf = sb("xf", [P, QT, D])
        xfT = sb("xfT", [KH + 1, 2, NTOK])
        lmax, ls, ex = sb("lmax", [P, QT]), sb("ls", [P, QT, E]), sb("ex", [P, QT, E])
        esum, k8, oh = sb("esum", [P, QT]), sb("k8", [P, QT, E]), sb("oh", [P, QT, E])
        prob, r8 = sb("prob", [P, QT]), sb("r8", [P, QT])
        run = sb("run", [P, E])
        place, slotf = sb("place", [P, QT, E]), sb("slotf", [P, QT])
        slot = [sb(f"slot{i}", [P, QT], i32) for i in range(2)]

        psS = [ctx.enter_context(nc.psum_tensor(f"psS{i}", [128, 512], fp32)) for i in range(2)]
        psE = [ctx.enter_context(nc.psum_tensor(f"psE{i}", [128, 2, 512], fp32)) for i in range(2)]
        psO = ctx.enter_context(nc.psum_tensor("psAttn", [128, 512], fp32))
        psM = ctx.enter_context(nc.psum_tensor("psM", [128, 512], fp32))
        psMb = psM[:, :].bitcast(bf16)

        const_loaded, prepared = sem("const_loadedB"), sem("prepared")
        h_loaded = [sem(f"h_loaded{i}") for i in range(2)]
        hres_loaded = [sem(f"hres_loaded{i}") for i in range(2)]
        var_ready, rstd_ready, xn_ready = sem("var_ready"), sem("rstd_ready"), sem("xn_ready")
        misc_ready, misc_free = sem("misc_ready"), sem("misc_free")
        qk_hi, res_done, mid_done, parts_ready = sem("qk_hi"), sem("res_done"), sem("mid_done"), sem("parts_ready")
        stack_stored, stack_loaded = sem("stack_stored"), sem("stack_loaded")
        scored, maxed, shift_ready = sem("scored"), sem("maxed"), sem("shift_ready")
        shifted, exped, weighted = sem("shifted"), sem("exped"), sem("weighted")
        o_read, o_ready = sem("o_read"), sem("o_ready")
        var2_ready, rstd2_ready, xf_ready = sem("var2_ready"), sem("rstd2_ready"), sem("xf_ready")
        h2_ready = sem("h2_ready")
        ls_ready, ex_ready, oh_ready, row_ready = sem("ls_ready"), sem("ex_ready"), sem("oh_ready"), sem("row_ready")
        rows_free = sem("rows_free")
        scattered = [sem(f"scattered{i}") for i in range(2)]
        finished, group_seen, stacks_seen = sem("finishedB"), sem("group_seen"), sem("stacks_seen")
        block = ctx.enter_context(nc.Block())
        h_v = h.rearrange("b (t p) d -> b p t d", p=P)

        def bodies(eng, body, final):
            body(0, 0, tail=False, ln=True, prep=True)
            with eng.Fori(0, (NB - 4) // 2, 1) as pair:
                body(2 * pair + 1, 1, tail=True, ln=True, prep=True)
                body(2 * pair + 2, 0, tail=True, ln=True, prep=True)
            body(NB - 3, (NB - 3) % 2, tail=True, ln=True, prep=True)
            body(NB - 2, (NB - 2) % 2, tail=True, ln=False, prep=True)
            body(NB - 1, (NB - 1) % 2, tail=True, ln=False, prep=False)
            final(NB, NB % 2)

        def at(b, name, tail, prep):
            return misc_at(b, name, last=not prep, first=not tail)

        @block.sync
        def _(sp):
            for dst, src in ((w_qkv[0:KH, 0, :], wqkvT[0:KH, :]), (w_qkv[0:KH, 1, :], wqkvT[KH:D, :]),
                             (w_qkv[KH:KH + 1, 1, :], bqkv.rearrange("(o n) -> o n", o=1)),
                             (ident[:, :], ident_in), (sel_f[:, :, :], sel_in),
                             (tri[:, :], tri_in), (c8[:, :, :], c8_in), (tok_all[:, :], tok_in),
                             (run[:, :], run_in), (w_sw[0:KH, 0, :], sw[0:KH, :]), (w_sw[0:KH, 1, :], sw[KH:D, :]),
                             (w_sw[KH:KH + 1, 1, :], swb.rearrange("(o n) -> o n", o=1))):
                sp.dma_start(dst, src).then_inc(const_loaded, 16)
            sp.wait_ge(prepared, 1)
            for hd in range(HEADS):
                g, j = divmod(hd, 4)
                sp.dma_start(w_out[32 * j:32 * j + HD, g, :], woT[HD * hd:HD * hd + HD, :]).then_inc(const_loaded, 16)
            sp.dma_start(w_out[HD:HD + 1, 0, :], bo.rearrange("(o n) -> o n", o=1)).then_inc(const_loaded, 16)

            def load_h(b, par):
                sp.dma_start(h_in[par][:, :, :], h_v[bass.ds(b, 1)].rearrange("o p t d -> (o p) t d"))\
                  .then_inc(h_loaded[par], 16)

            def load_res(b, par):
                sp.dma_start(h_res[par][:, :, :], h_v[bass.ds(b, 1)].rearrange("o p t d -> (o p) t d"))\
                  .then_inc(hres_loaded[par], 16)

            def restack(n, par):
                for m in range(4):
                    sp.wait_ge(parts_ready, 4 * n + m + 1)
                    dst = stack[par, :, m // 2, KH * (m % 2):KH * (m % 2) + KH, :].rearrange("s r n -> r s n")
                    sp.dma_start(dst, parts[:, m, :, :]).then_inc(stack_stored, 16)
                sp.wait_ge(stack_stored, 64 * n + 64)
                for s in range(6):
                    for kind, tile, part in ((0, Qs, Q_PART), (1, Ks, K_PART)):
                        src = stack[par, part[s], kind, :, :].rearrange("(h d) n -> d h n", d=HD)
                        sp.dma_start(tile[par][HD * s:HD * s + HD, :, :], src).then_inc(stack_loaded, 16)

            load_h(0, 0)
            load_h(1, 1)
            restack(0, 0)

            def body(b, par, tail, ln, prep):
                if tail:
                    sp.wait_ge(o_ready, 3 * b)
                load_res(b, par)
                if ln:
                    sp.wait_ge(xn_ready, b + 1)
                    load_h(b + 2, par)
                if prep:
                    if tail:
                        sp.wait_ge(shifted, SLOTS * b + 2)
                        sp.sem_inc(stacks_seen, 1)
                        sp.wait_ge(stack_loaded, 192 * b)
                    restack(b + 1, 1 - par)
            bodies(sp, body, lambda b, par: None)
            sp.wait_ge(finished, 1)
            sp.dma_start(p_all_d, p_all[:, :]).then_inc(finished, 16)
            sp.dma_start(r_all_d, r_all[:, :]).then_inc(finished, 16)
            sp.dma_start(cnt_d, run[:, :]).then_inc(finished, 16)
            sp.wait_ge(finished, 49)
            sp.wait_ge(rows_free, NB + 2)

        @block.tensor
        def _(pe):
            pe.sem_inc(shifted, 2)
            pe.sem_inc(weighted, 2)
            pe.wait_ge(const_loaded, 16 * 25)
            pe.wait_ge(prepared, 3)

            def score(b, par, u):
                g, r = divmod(u, 12)
                qt, j = divmod(r, 4)
                hd = 4 * g + j
                pe.wait_ge(maxed, 36 * b + u + 1)
                nc.tensor.matmul(psS[u % 2][0:P, 0:NTOK], Qs[par][:, hd, P * qt:P * qt + P], Ks[par][:, hd, :],
                                 start=True, stop=True).then_inc(scored, 1)

            def shifted_scores(b, par, v, mt):
                g, r = divmod(v, 6)
                kt, pair = divmod(r, 2)
                if r == 0:
                    pe.wait_ge(misc_free, mt + 1)
                pe.wait_ge(exped, SLOTS * b + v + 1)
                for i in range(2):
                    j = 2 * pair + i
                    nc.tensor.matmul(psE[v % 2][0:P, i, 0:NTOK], Ks[par][:, 4 * g + j, P * kt:P * kt + P],
                                     Qs[par][:, 4 * g + j, :], start=True, stop=False)
                    last = nc.tensor.matmul(psE[v % 2][0:P, i, 0:NTOK], sel[:, j, :], mT[g][:, :],
                                            start=False, stop=True)
                last.then_inc(shifted, 1)

            def weigh(b, par, m):
                g, kt = divmod(m, 3)
                pe.wait_ge(exped, SLOTS * b + 2 * m + 4)
                if kt == 0:
                    pe.wait_ge(o_read, 3 * b + g + 1)
                for j in range(4):
                    last = nc.tensor.matmul(psO[32 * j:32 * j + 32, 0:NTOK], V[par][:, kt, 4 * g + j, :],
                                            Pr[(2 * par + 2 * m + j // 2) % 4][:, j % 2, :], start=(kt == 0), stop=(kt == 2))
                last.then_inc(weighted, 1)

            def misc(idx):
                if not (isinstance(idx, int) and idx == 0):
                    pe.wait_ge(misc_free, idx)

            def transpose_x(idx, src, c):
                misc(idx)
                for t in range(QT):
                    last = nc.tensor.transpose(psM[0:KH, P * t:P * t + P], src[:, t, KH * c:KH * c + KH], ident[0:P, 0:P])
                return last

            def prep_step(idx, n, par, name):
                if name in ("T0", "T1"):
                    if name == "T0":
                        pe.wait_ge(xn_ready, n + 1)
                    last = transpose_x(idx, xn[par], int(name[1]))
                    last.then_inc(misc_ready, 1)
                elif name[0] in "QK":
                    misc(idx)
                    f = (0 if name[0] == "Q" else D) + KH * int(name[1])
                    for c in range(2):
                        last = nc.tensor.matmul(psM[0:KH, 0:NTOK], w_qkv[0:KH + c, c, f:f + KH], xnT[0:KH + c, c, :],
                                                start=(c == 0), stop=(c == 1))
                    last.then_inc(misc_ready, 1)
                else:
                    misc(idx)
                    for i, t in enumerate(((0, 1), (2,))[int(name[1])]):
                        for c in range(2):
                            last = nc.tensor.matmul(psM[0:P, D * i:D * i + D], xnT[0:KH + c, c, P * t:P * t + P],
                                                    w_qkv[0:KH + c, c, 2 * D:3 * D], start=(c == 0), stop=(c == 1))
                    last.then_inc(misc_ready, 1)

            def shift_rows(idx, b, g):
                pe.wait_ge(shift_ready, 3 * b + g + 1)
                misc(idx)
                for t in range(QT):
                    last = nc.tensor.transpose(psMb[0:12, P * t + t:P * t + t + P],
                                               shift[:, t, :, :].rearrange("p j s -> p (j s)"), identb[0:P, 0:P])
                last.then_inc(misc_ready, 1)

            def tail_step(idx, p, par, name):
                if name in ("OUT0", "OUT1"):
                    if name == "OUT0":
                        pe.wait_ge(o_ready, 3 * p + 3)
                    misc(idx)
                    for i, t in enumerate(((0, 1), (2,))[int(name[3])]):
                        for g in range(GRP):
                            last = nc.tensor.matmul(psM[0:P, D * i:D * i + D], On[par][:, g, P * t:P * t + P],
                                                    w_out[:, g, :], start=(g == 0), stop=(g == GRP - 1))
                elif name in ("X0", "X1"):
                    pe.wait_ge(xf_ready, p + 1)
                    last = transpose_x(idx, xf, int(name[1]))
                elif name == "LG":
                    misc(idx)
                    for t in range(QT):
                        for c in range(2):
                            last = nc.tensor.matmul(psM[0:P, E * t:E * t + E], xfT[0:KH + c, c, P * t:P * t + P],
                                                    w_sw[0:KH + c, c, :], start=(c == 0), stop=(c == 1))
                else:
                    pe.wait_ge(oh_ready, p + 1)
                    misc(idx)
                    for t in range(QT + 1):
                        if t < QT:
                            last = nc.tensor.matmul(psM[0:P, E * t:E * t + E], tri[:, :], oh[:, t, :],
                                                    start=True, stop=(t == 0))
                        for before in range(t):
                            last = nc.tensor.matmul(psM[0:P, E * t:E * t + E], ones[:, :], oh[:, before, :],
                                                    start=(t == QT and before == 0), stop=(before == t - 1))
                last.then_inc(misc_ready, 1)

            for i, name in enumerate(PREP[:-1]):
                prep_step(i, 0, 0, name)
            pe.wait_ge(stack_loaded, 192)
            for k in range(LEAD):
                score(0, 0, 2 * k)
                score(0, 0, 2 * k + 1)
                if k == 6:
                    shift_rows(misc_at("prologue", "MT0"), 0, 0)

            prep_at = {0: ("T0",), 1: ("T1",), 2: ("Q0",), 3: ("Q1",), 4: ("K0",), 5: ("K1",), 6: ("V0",), 7: ("V1",)}
            tail_at = {2: ("OUT0",), 3: ("OUT1",), 7: ("X0",), 8: ("X1",), 9: ("LG",), 13: ("RK",)}

            def body(b, par, tail, ln, prep):
                n, p = b + 1, b - 1
                for i in range(SLOTS):
                    k = i + LEAD
                    if k < SLOTS:
                        score(b, par, 2 * k)
                        score(b, par, 2 * k + 1)
                    elif prep:
                        if k == SLOTS:
                            pe.wait_ge(stack_loaded, 192 * n + 192)
                        score(n, 1 - par, 2 * (k - SLOTS))
                        score(n, 1 - par, 2 * (k - SLOTS) + 1)
                    if i == 0:
                        mt = misc_at(p, "MT0") if tail else misc_at("prologue", "MT0")
                    elif i == 6:
                        mt = at(b, "MT1", tail, prep)
                    elif i == 12:
                        mt = at(b, "MT2", tail, prep)
                    shifted_scores(b, par, i, mt)
                    if i % 2 == 0:
                        if i:
                            weigh(b, par, i // 2 - 1)
                        elif tail:
                            weigh(p, 1 - par, 8)
                    if i == 4:
                        shift_rows(at(b, "MT1", tail, prep), b, 1)
                    if i == 10:
                        shift_rows(at(b, "MT2", tail, prep), b, 2)
                    if prep and i in prep_at:
                        for name in prep_at[i]:
                            prep_step(at(b, name, tail, prep), n, 1 - par, name)
                    if tail and i in tail_at:
                        for name in tail_at[i]:
                            tail_step(at(b, name, tail, prep), p, 1 - par, name)
                    if prep and i == 16:
                        shift_rows(at(b, "MT0", tail, prep), n, 0)

            def final(b, par):
                weigh(b - 1, 1 - par, 8)
                for name in TAIL:
                    tail_step(misc_at(b, name), b - 1, 1 - par, name)
            bodies(pe, body, final)

        @block.scalar
        def _(act):
            act.sem_inc(exped, 2)
            act.wait_ge(prepared, 2)

            def exponent(b, par, v):
                act.wait_ge(shifted, SLOTS * b + v + 3)
                act.wait_ge(weighted, 9 * b + v // 2 + 1)
                nc.scalar.activation(Pr[(2 * par + v) % 4][:, :, :], psE[v % 2][0:P, :, 0:NTOK], ACT.Exp).then_inc(exped, 1)

            def prep_step(idx, n, par, name):
                act.wait_ge(misc_ready, idx + 1)
                if name[0] == "T":
                    nc.scalar.activation(xnT[0:KH, int(name[1]), :], psM[0:KH, 0:NTOK], ACT.Copy).then_inc(misc_free, 1)
                elif name[0] in "QK":
                    m = (0 if name[0] == "Q" else 2) + int(name[1])
                    scale = HD ** -0.5 if name[0] == "Q" else 1.0
                    if not (isinstance(n, int) and n == 0):
                        act.wait_ge(stack_stored, 64 * n)
                    nc.scalar.activation(parts[:, m, 0, :], psM[0:KH, 0:NTOK], ACT.Copy, scale=scale)\
                      .then_inc(qk_hi, 1)
                    nc.scalar.activation(qk_f[:, m, :], psM[0:KH, 0:NTOK], ACT.Copy, scale=scale).then_inc(misc_free, 1)
                else:
                    if name == "V0":
                        act.wait_ge(weighted, 2 if isinstance(n, int) and n == 0 else 9 * n - 7)
                    for i, t in enumerate(((0, 1), (2,))[int(name[1])]):
                        last = nc.scalar.activation(V[par][:, t, :, 0:HD],
                                                    psM[0:P, D * i:D * i + D].rearrange("p (h d) -> p h d", d=HD), ACT.Copy)
                    last.then_inc(misc_free, 1)

            def shift_rows(idx, g):
                act.wait_ge(misc_ready, idx + 1)
                nc.scalar.activation(mT[g][:, :].rearrange("p (t n) -> p t n", t=QT),
                                     psMb[0:12, 0:QT * (P + 1)].rearrange("p (t n) -> p t n", t=QT)[:, :, 0:P], ACT.Copy)\
                  .then_inc(misc_free, 1)

            def tail_step(idx, p, name):
                if name in ("X0", "X1"):
                    act.wait_ge(misc_ready, idx + 1)
                    nc.scalar.activation(xfT[0:KH, int(name[1]), :], psM[0:KH, 0:NTOK], ACT.Copy).then_inc(misc_free, 1)
                elif name == "EX":
                    act.wait_ge(ls_ready, p + 1)
                    nc.scalar.activation(ex[:, :, :], ls[:, :, :], ACT.Exp).then_inc(ex_ready, 1)

            for i, name in enumerate(PREP[:-1]):
                prep_step(i, 0, 0, name)
            shift_rows(misc_at("prologue", "MT0"), 0)
            prep_at = {0: "T0", 1: "T1", 2: "Q0", 3: "Q1", 4: "K0", 5: "K1", 6: "V0", 7: "V1"}
            tail_at = {7: "X0", 8: "X1", 11: "EX"}

            def body(b, par, tail, ln, prep):
                for i in range(SLOTS):
                    exponent(b, par, i)
                    if i == 4:
                        shift_rows(at(b, "MT1", tail, prep), 1)
                    if i == 10:
                        shift_rows(at(b, "MT2", tail, prep), 2)
                    if prep and i in prep_at:
                        prep_step(at(b, prep_at[i], tail, prep), b + 1, 1 - par, prep_at[i])
                    if tail and i in tail_at:
                        name = tail_at[i]
                        tail_step(None if name == "EX" else at(b, name, tail, prep), b - 1, name)
                    if prep and i == 16:
                        shift_rows(at(b, "MT0", tail, prep), 0)

            def final(b, par):
                for name in ("X0", "X1", "EX"):
                    tail_step(None if name == "EX" else misc_at(b, name), b - 1, name)
            bodies(act, body, final)

        @block.vector
        def _(dve):
            nc.vector.memset(w_out[:, :, :], 0.0)
            dve.drain().then_inc(prepared, 1)
            nc.vector.memset(xnT[KH:KH + 1, 1, :], 1.0)
            nc.vector.memset(xfT[KH:KH + 1, 1, :], 1.0)
            nc.vector.memset(ones[:, :], 1.0)
            nc.vector.memset(mhalf[:, :], -0.5)
            for i in range(2):
                nc.vector.memset(V[i][:, :, :, :], 1.0)
            dve.drain().then_inc(prepared, 1)
            dve.sem_inc(maxed, 2)
            dve.sem_inc(o_read, 1)
            dve.wait_ge(const_loaded, 16 * 25)
            nc.vector.tensor_copy(identb[:, :], ident[:, :])
            nc.vector.tensor_copy(sel[:, :, :], sel_f[:, :, :])
            dve.drain().then_inc(prepared, 1)

            def maximum(b, par, u):
                g, r = divmod(u, 12)
                qt, j = divmod(r, 4)
                dve.wait_ge(scored, 36 * b + u + 1)
                nc.vector.reduce_max(neg_max[par][:, qt, 4 * g + j:4 * g + j + 1], psS[u % 2][0:P, 0:NTOK], AX.X,
                                     negate=True).then_inc(maxed, 1)

            def split_shift(b, par, g):
                nm = neg_max[par][:, :, 4 * g:4 * g + 4]
                dve.drain()
                nc.vector.tensor_copy(shift[:, :, :, 0], nm)
                dve.drain()
                nc.vector.tensor_tensor(shift_r[:, :, :], nm, shift[:, :, :, 0], ALU.subtract)
                dve.drain()
                nc.vector.tensor_copy(shift[:, :, :, 1], shift_r[:, :, :])
                dve.drain()
                nc.vector.tensor_tensor(shift[:, :, :, 2], shift_r[:, :, :], shift[:, :, :, 1], ALU.subtract)
                dve.drain().then_inc(shift_ready, 1)

            def ln_stats(src, st, m, ve, signal):
                for t in range(QT):
                    nc.vector.bn_stats(st[:, t, :], src[:, t, 0:D])
                dve.drain()
                for t in range(QT):
                    nc.vector.bn_aggr(m[:, t, :], st[:, t, :])
                dve.drain()
                nc.vector.tensor_scalar(ve[:, :], m[:, :, 1], 1e-5, None, ALU.add).then_inc(signal, 1)

            def ln_apply(dst, src, m, rs):
                for t in range(QT):
                    last = nc.vector.tensor_scalar(dst[:, t, :], src[:, t, 0:D], m[:, t, 0:1], rs[:, t:t + 1],
                                                   ALU.subtract, ALU.mult)
                return last

            def ln1_stats(b, par):
                dve.drain()
                dve.wait_ge(h_loaded[par], 8 * (b - par) + 16)
                ln_stats(h_in[par], stats, mv, var_eps, var_ready)

            def ln1_apply(b, par):
                dve.wait_ge(rstd_ready, b + 1)
                ln_apply(xn[par], h_in[par], mv, rstd).then_inc(xn_ready, 1)

            def normalise(b, par, g):
                dve.wait_ge(weighted, 9 * b + 3 * g + 3 + 2)
                dve.sem_inc(group_seen, 1)
                nc.vector.stream_shuffle(rsum[:, :], psO[:, 0:NTOK], [HD] * 32)
                dve.drain()
                nc.vector.reciprocal(rsum[:, :], rsum[:, :])
                dve.drain()
                nc.vector.tensor_tensor(On[par][:, g, :], psO[:, 0:NTOK], rsum[:, :], ALU.mult).then_inc(o_read, 1)
                dve.drain().then_inc(o_ready, 1)

            def residual(idx0, idx1, p, par):
                dve.wait_ge(hres_loaded[par], 8 * (p - par) + 16)
                dve.wait_ge(rows_free, p + 1)
                dve.wait_ge(misc_ready, idx0 + 1)
                nc.vector.tensor_tensor(row[par][:, 0:2, 0:D], psM[0:P, 0:2 * D].rearrange("p (t d) -> p t d", t=2),
                                        h_res[par][:, 0:2, :], ALU.add).then_inc(misc_free, 1)
                dve.wait_ge(misc_ready, idx1 + 1)
                nc.vector.tensor_tensor(row[par][:, 2, 0:D], psM[0:P, 0:D], h_res[par][:, 2, :], ALU.add)\
                  .then_inc(misc_free, 1)

            def ln2_stats(p, par):
                dve.drain()
                ln_stats(row[par], stats2, mv2, var_eps2, var2_ready)

            def ln2_apply(p, par):
                dve.wait_ge(rstd2_ready, p + 1)
                ln_apply(xf, row[par], mv2, rstd2).then_inc(xf_ready, 1)
                nc.vector.tensor_copy(row[par][:, :, D], rstd2[:, :])
                nc.vector.tensor_copy(row[par][:, :, D + 1], mv2[:, :, 0])
                nc.vector.tensor_copy(row[par][:, :, D + 3], tok_all[:, bass.ds(QT * p, QT)])

            def logits(idx, p):
                dve.wait_ge(misc_ready, idx + 1)
                lg = psM[0:P, 0:QT * E].rearrange("p (t e) -> p t e", e=E)
                nc.vector.reduce_max(lmax[:, :], lg, AX.X)
                dve.drain()
                nc.vector.tensor_tensor(ls[:, :, :], lg, lmax[:, :].rearrange("p (t o) -> p t o", o=1)
                                        .broadcast_to([P, QT, E]), ALU.subtract).then_inc(misc_free, 1)
                dve.drain().then_inc(ls_ready, 1)

            def route(p, par):
                dve.wait_ge(ex_ready, p + 1)
                nc.vector.reduce_sum(esum[:, :], ex[:, :, :], AX.X)
                nc.vector.scalar_tensor_tensor(out=k8[:, :, :], in0=ex[:, :, :], scalar=1.0, in1=c8[:, :, :],
                                               op0=ALU.is_ge, op1=ALU.mult)
                dve.drain()
                nc.vector.reciprocal(prob[:, :], esum[:, :])
                nc.vector.reduce_max(r8[:, :], k8[:, :, :], AX.X)
                dve.drain()
                nc.vector.tensor_copy(row[par][:, :, D + 2], prob[:, :])
                nc.vector.tensor_copy(p_all[:, bass.ds(QT * p, QT)], prob[:, :])
                nc.vector.tensor_copy(r_all[:, bass.ds(QT * p, QT)], r8[:, :])
                nc.vector.tensor_tensor(oh[:, :, :], c8[:, :, :], r8[:, :].rearrange("p (t o) -> p t o", o=1)
                                        .broadcast_to([P, QT, E]), ALU.is_equal)
                dve.drain().then_inc(oh_ready, 1)

            def places(idx, p, par):
                dve.wait_ge(misc_ready, idx + 1)
                nc.vector.tensor_tensor(place[:, :, :], psM[0:P, 0:QT * E].rearrange("p (t e) -> p t e", e=E),
                                        run[:, :].rearrange("p (o e) -> p o e", o=1).broadcast_to([P, QT, E]), ALU.add)
                dve.drain()
                nc.vector.tensor_tensor(run[:, :], run[:, :], psM[0:P, QT * E:QT * E + E], ALU.add).then_inc(misc_free, 1)
                nc.vector.tensor_tensor(place[:, :, :], place[:, :, :], oh[:, :, :], ALU.mult)
                dve.drain()
                nc.vector.reduce_sum(slotf[:, :], place[:, :, :], AX.X)
                dve.drain()
                nc.vector.tensor_copy(slot[par][:, :], slotf[:, :])
                dve.drain().then_inc(row_ready, 1)

            for b in range(2):
                ln1_stats(b, b)
                ln1_apply(b, b)
            for k in range(LEAD):
                maximum(0, 0, 2 * k)
                maximum(0, 0, 2 * k + 1)
                if k == 5:
                    split_shift(0, 0, 0)

            def body(b, par, tail, ln, prep):
                n, p = b + 1, b - 1
                q = 1 - par
                for i in range(SLOTS):
                    k = i + LEAD
                    if k < SLOTS:
                        maximum(b, par, 2 * k)
                        maximum(b, par, 2 * k + 1)
                    elif prep:
                        maximum(n, q, 2 * (k - SLOTS))
                        maximum(n, q, 2 * (k - SLOTS) + 1)
                    if i == 0 and tail:
                        normalise(p, q, 2)
                    if i == 3:
                        split_shift(b, par, 1)
                        if tail:
                            residual(at(b, "OUT0", tail, prep), at(b, "OUT1", tail, prep), p, q)
                    if i == 4 and tail:
                        ln2_stats(p, q)
                    if i == 5 and tail:
                        ln2_apply(p, q)
                    if i == 6:
                        normalise(b, par, 0)
                    if i == 9:
                        split_shift(b, par, 2)
                        if tail:
                            logits(at(b, "LG", tail, prep), p)
                    if i == 11 and tail:
                        route(p, q)
                    if i == 12:
                        normalise(b, par, 1)
                    if i == 13 and tail:
                        places(at(b, "RK", tail, prep), p, q)
                    if i == 14 and ln:
                        ln1_stats(b + 2, par)
                    if i == 15 and prep:
                        split_shift(n, q, 0)
                    if i == 16 and ln:
                        ln1_apply(b + 2, par)

            def final(b, par):
                p, q = b - 1, 1 - par
                normalise(p, q, 2)
                residual(misc_at(b, "OUT0"), misc_at(b, "OUT1"), p, q)
                ln2_stats(p, q)
                ln2_apply(p, q)
                logits(misc_at(b, "LG"), p)
                route(p, q)
                places(misc_at(b, "RK"), p, q)
            bodies(dve, body, final)
            dve.drain().then_inc(finished, 1)

        @block.gpsimd
        def _(pool):
            pool.wait_ge(prepared, 2)

            def root(b, ve, rs, ready, done):
                pool.wait_ge(ready, b + 1)
                nc.gpsimd.tensor_tensor(rs[:, :], ve[:, :], mhalf[:, :], ALU.pow).then_inc(done, 1)

            def split(n, idx):
                for m in range(4):
                    pool.wait_ge(qk_hi, 4 * n + m + 1)
                    pool.wait_ge(misc_free, idx(("Q0", "Q1", "K0", "K1")[m]) + 1)
                    nc.gpsimd.tensor_tensor(qk_r[:, m, :], qk_f[:, m, :], parts[:, m, 0, :], ALU.subtract)\
                      .then_inc(res_done, 1)
                    pool.wait_ge(prepared, 2)
                    pool.wait_ge(res_done, 4 * n + m + 1)
                    nc.gpsimd.tensor_copy(parts[:, m, 1, :], qk_r[:, m, :]).then_inc(mid_done, 1)
                    pool.wait_ge(mid_done, 4 * n + m + 1)
                    nc.gpsimd.tensor_tensor(parts[:, m, 2, :], qk_r[:, m, :], parts[:, m, 1, :], ALU.subtract)\
                      .then_inc(parts_ready, 1)

            pool.sem_inc(rows_free, 2)

            def release(p, par):
                pool.wait_ge(scattered[par], 24 * (p - par) + 48)
                pool.sem_inc(rows_free, 1)

            def scatter(p, par):
                pool.wait_ge(prepared, 2)
                pool.wait_ge(row_ready, p + 1)
                for t in range(QT):
                    pool.indirect_dma_start(xs, bass.IndirectOffsetOnAxis(ap=slot[par][:, t:t + 1], axis=0),
                                            row[par][:, t, :], None).then_inc(scattered[par], 16)
            root(0, var_eps, rstd, var_ready, rstd_ready)
            root(1, var_eps, rstd, var_ready, rstd_ready)
            split(0, lambda name: misc_at("prologue", name))

            def body(b, par, tail, ln, prep):
                if prep:
                    split(b + 1, lambda name: at(b, name, tail, prep))
                if tail:
                    root(b - 1, var_eps2, rstd2, var2_ready, rstd2_ready)
                    scatter(b - 1, 1 - par)
                if ln:
                    root(b + 2, var_eps, rstd, var_ready, rstd_ready)
                if tail:
                    release(b - 1, 1 - par)

            def final(b, par):
                root(b - 1, var_eps2, rstd2, var2_ready, rstd2_ready)
                scatter(b - 1, 1 - par)
                release(b - 1, 1 - par)
            bodies(pool, body, final)


def experts(nc, N, PT, CAPR, NT, xs, p_d, r_d, cnt_d, start_in, tok_in, tile_in, lane_in, neg_in, ident_in,
            w1, b1, w2, b2, out):
    PP = N // PT
    capacity = int(1.25 * N / E)
    RING = 4
    with ExitStack() as ctx:
        def sb(name, shape, dt=fp32):
            return ctx.enter_context(nc.sbuf_tensor(name, shape, dt))

        def sem(name):
            return ctx.enter_context(nc.semaphore(name))

        def ps(name, shape):
            return ctx.enter_context(nc.psum_tensor(name, shape, fp32))

        w1_sb = sb("w1_sb", [KH + 1, 2, E * F])
        w2_sb = sb("w2_sb", [128, FC, E * D])
        b2_sb = sb("b2_sb", [1, E * D])
        ident, one_row = sb("identC", [128, 128]), sb("one_row", [1, 128])
        p_all, r_all, tok = sb("p_allC", [PP, PT]), sb("r_allC", [PP, PT]), sb("tok", [PP, PT])
        mine = sb("mine", [PP, E, PT])
        hit = sb("hit", [PP, E, PT])
        part = sb("part", [PP, E])
        ones = sb("onesC", [PP, 128])
        start, cnt = sb("start", [128, E]), sb("cnt", [128, E])
        thr, step, cand, ok = sb("thr", [128, E]), sb("step", [128, 1]), sb("cand", [128, E]), sb("ok", [128, E])
        room, last_tok = sb("room", [128, E]), sb("last_tok", [128, E])
        tiles_f, tiles_i = sb("tiles_f", [128, E]), sb("tiles_i", [128, E], i32)
        first, end = sb("first", [128, E]), sb("end", [128, E])
        tile_no, lane, eno = sb("tile_no", [128, NT]), sb("lane", [128, 1]), sb("eno", [128, E])
        own, tmp, off = sb("own", [128, E, NT]), sb("tmp", [128, E, NT]), sb("off", [128, E, NT])
        t_base, t_exp, t_valid = sb("t_base", [128, NT]), sb("t_exp", [128, NT]), sb("t_valid", [128, NT])
        t_thr, t_last, t_used = sb("t_thr", [128, NT]), sb("t_last", [128, NT]), sb("t_used", [128, NT])
        base_i, exp_i = sb("base_i", [1, NT], i32), sb("exp_i", [1, NT], i32)
        zero_rows = sb("zero_rows", [128, RW])
        tail_f, tail_i = sb("tail_f", [128, E]), sb("tail_i", [128, E], i32)
        row = [sb(f"rowC{i}", [128, RW]) for i in range(RING)]
        xf = [sb(f"xfC{i}", [128, D]) for i in range(RING)]
        xfT = [sb(f"xfTC{i}", [KH + 1, 2, 128]) for i in range(2)]
        hid = [sb(f"hid{i}", [128, F]) for i in range(2)]
        hidT = [sb(f"hidT{i}", [128, F]) for i in range(2)]
        over, tie, low, keep, kp, dp, val, idm = (sb(n, [128, 1]) for n in
                                                   ("over", "tie", "low", "keep", "kp", "dp", "val", "idm"))
        pre = sb("pre", [128, D])
        res = [sb(f"res{i}", [128, D]) for i in range(RING)]
        dest = [sb(f"dest{i}", [128, 1], i32) for i in range(RING)]
        psC = ps("psC", [128, 512])
        psX, psH, psT = ps("psX", [128, 512]), ps("psH", [128, 2, 512]), ps("psTr", [128, 2, 512])
        psY = [ps(f"psY{i}", [128, 512]) for i in range(2)]

        small_loaded, weights_loaded, cleared = sem("small_loaded"), sem("weights_loaded"), sem("cleared")
        counted, totalled, tails_ready, tails_done, tables = (sem("counted"), sem("totalled"), sem("tails_ready"),
                                                               sem("tails_done"), sem("tables"))
        row_loaded = [sem(f"row_loaded{i}") for i in range(RING)]
        x_ready, x_tr, x_copied = sem("x_ready"), sem("x_tr"), sem("x_copied")
        h_ready, geluped = sem("h_ready"), sem("gelued")
        ht_ready, ht_dve, ht_act = sem("ht_ready"), sem("ht_dve"), sem("ht_act")
        y_ready, combined, dest_ready, out_free = sem("y_ready"), sem("combined"), sem("dest_ready"), sem("out_free")
        rows_seen = sem("rows_seen")
        scat = [sem(f"scat{i}") for i in range(RING)]
        block = ctx.enter_context(nc.Block())
        NSMALL = 10

        @block.sync
        def _(sp):
            for dst, src in ((p_all[:, :], p_d), (r_all[:, :], r_d), (tok[:, :], tok_in),
                             (start[:, :], start_in), (cnt[:, :], cnt_d[0:1, :].broadcast_to([128, E])),
                             (tile_no[:, :], tile_in), (lane[:, :], lane_in), (eno[:, :], neg_in),
                             (ident[:, :], ident_in), (b2_sb[:, :], b2.rearrange("e d -> (e d)").rearrange("(o n) -> o n", o=1))):
                sp.dma_start(dst, src).then_inc(small_loaded, 16)
            for c in range(2):
                sp.dma_start(w1_sb[0:KH, c, :].rearrange("k (e f) -> k e f", e=E),
                             w1[:, KH * c:KH * c + KH, :].rearrange("e k f -> k e f")).then_inc(weights_loaded, 16)
            sp.dma_start(w1_sb[KH:KH + 1, 1, :], b1.rearrange("e f -> (e f)").rearrange("(o n) -> o n", o=1))\
              .then_inc(weights_loaded, 16)
            for e in range(E):
                sp.dma_start(w2_sb[:, :, D * e:D * e + D], w2[e].rearrange("(c p) n -> p c n", p=128))\
                  .then_inc(weights_loaded, 16)
            sp.wait_ge(tables, 1)
            sp.wait_ge(tails_done, 16 * (E + 1))

            def load(t, r):
                base = sp.value_load(base_i[0:1, bass.ds(t, 1)], min_val=0, max_val=E * CAPR)
                sp.dma_start(row[r][:, :], xs[bass.ds(base, 128), :]).then_inc(row_loaded[r], 16)
            for r in range(RING):
                load(r, r)
            with sp.Fori(0, NT // RING - 1, 1) as k:
                for r in range(RING):
                    sp.wait_ge(tables, 1)
                    sp.wait_ge(combined, RING * k + r + 1)
                    load(RING * k + r + RING, r)

        @block.tensor
        def _(pe):
            pe.wait_ge(cleared, 1)
            pe.wait_ge(small_loaded, 16 * NSMALL)

            def total(i):
                pe.wait_ge(counted, i + 1)
                nc.tensor.matmul(psC[:, 0:E], ones[:, :], part[:, :], start=True, stop=True).then_inc(totalled, 1)
            with pe.Fori(0, 27, 1) as i:
                total(i)
            total(27)
            with pe.Fori(28, 43, 1) as i:
                total(i)
            pe.wait_ge(weights_loaded, 16 * 11)
            pe.wait_ge(tables, 1)

            def x_transpose(t, r):
                pe.wait_ge(x_ready, t + 1)
                pe.wait_ge(x_copied, t + 1)
                for c in range(2):
                    last = nc.tensor.transpose(psX[0:KH, 128 * c:128 * c + 128], xf[r][:, KH * c:KH * c + KH], ident[:, :])
                last.then_inc(x_tr, 1)

            def first_layer(t, r):
                e = pe.value_load(exp_i[0:1, bass.ds(t, 1)], min_val=0, max_val=E - 1)
                pe.wait_ge(x_copied, t + 2)
                pe.wait_ge(geluped, t + 1)
                for n in range(2):
                    for c in range(2):
                        last = nc.tensor.matmul(psH[:, n, 0:F // 2], xfT[r % 2][0:KH + c, c, :],
                                                w1_sb[0:KH + c, c, bass.ds(e * F + n * (F // 2), F // 2)],
                                                start=(c == 0), stop=(c == 1))
                last.then_inc(h_ready, 1)

            def hid_transpose(t, r):
                pe.wait_ge(geluped, t + 2)
                pe.wait_ge(ht_dve, t + 1)
                pe.wait_ge(ht_act, t + 1)
                for f in range(FC):
                    last = nc.tensor.transpose(psT[:, f // 3, 128 * (f % 3):128 * (f % 3) + 128],
                                               hid[r % 2][:, 128 * f:128 * f + 128], ident[:, :])
                last.then_inc(ht_ready, 1)

            def second_layer(t, r):
                e = pe.value_load(exp_i[0:1, bass.ds(t, 1)], min_val=0, max_val=E - 1)
                pe.wait_ge(ht_dve, t + 2)
                pe.wait_ge(ht_act, t + 2)
                for f in range(FC):
                    nc.tensor.matmul(psY[r % 2][:, 0:D], hidT[r % 2][:, 128 * f:128 * f + 128],
                                     w2_sb[:, f, bass.ds(e * D, D)], start=(f == 0), stop=False)
                nc.tensor.matmul(psY[r % 2][:, 0:D], one_row[:, :], b2_sb[:, bass.ds(e * D, D)], start=False, stop=True)\
                  .then_inc(y_ready, 1)
            x_transpose(0, 0)
            first_layer(0, 0)
            x_transpose(1, 1)
            with pe.Fori(0, NT // RING - 1, 1) as k:
                for r in range(RING):
                    t = RING * k + r
                    first_layer(t + 1, (r + 1) % RING)
                    hid_transpose(t, r)
                    x_transpose(t + 2, (r + 2) % RING)
                    second_layer(t, r)
            for t in range(NT - RING, NT):
                r = t % RING
                if t + 1 < NT:
                    first_layer(t + 1, (r + 1) % RING)
                hid_transpose(t, r)
                if t + 2 < NT:
                    x_transpose(t + 2, (r + 2) % RING)
                second_layer(t, r)

        @block.scalar
        def _(act):
            act.sem_inc(x_copied, 1)
            act.sem_inc(geluped, 1)
            act.sem_inc(ht_act, 1)
            act.wait_ge(cleared, 1)

            def x_copy(t, r):
                act.wait_ge(x_tr, t + 1)
                nc.scalar.activation(xfT[r % 2][0:KH, :, :], psX[0:KH, 0:256].rearrange("p (c n) -> p c n", c=2), ACT.Copy)\
                  .then_inc(x_copied, 1)

            def gelu(t, r):
                act.wait_ge(h_ready, t + 1)
                nc.scalar.activation(hid[r % 2][:, :].rearrange("p (n f) -> p n f", n=2), psH[:, :, 0:F // 2], ACT.Gelu)\
                   .then_inc(geluped, 1)

            def hid_copy(t, r):
                act.wait_ge(ht_ready, t + 1)
                nc.scalar.activation(hidT[r % 2][:, 384:768], psT[:, 1, 0:384], ACT.Copy).then_inc(ht_act, 1)
            x_copy(0, 0)
            gelu(0, 0)
            x_copy(1, 1)
            with act.Fori(0, NT // RING - 1, 1) as k:
                for r in range(RING):
                    t = RING * k + r
                    gelu(t + 1, r + 1)
                    hid_copy(t, r)
                    x_copy(t + 2, r + 2)
            for t in range(NT - RING, NT):
                if t + 1 < NT:
                    gelu(t + 1, t + 1)
                hid_copy(t, t)
                if t + 2 < NT:
                    x_copy(t + 2, t)

        @block.vector
        def _(dve):
            nc.vector.memset(one_row[:, :], 1.0)
            nc.vector.memset(ones[:, :], 1.0)
            nc.vector.memset(zero_rows[:, :], 0.0)
            nc.vector.memset(thr[:, :], 0.0)
            nc.vector.memset(last_tok[:, :], 0.0)
            nc.vector.memset(step[:, :], 0.5)
            for i in range(2):
                nc.vector.memset(xfT[i][KH:KH + 1, 1, :], 1.0)
            dve.drain().then_inc(cleared, 1)
            dve.sem_inc(ht_dve, 1)
            dve.wait_ge(small_loaded, 16 * NSMALL)

            def bc(a, n=NT):
                return a[:, :].rearrange("p (e o) -> p e o", o=1).broadcast_to([a.shape[0], E, n])

            def bt(a):
                return a[:, :].rearrange("p (o n) -> p o n", o=1).broadcast_to([128, E, NT])
            tt, ts = nc.vector.tensor_tensor, nc.vector.tensor_scalar
            ts(tail_f[:, :], cnt[:, :], lane[:, 0:1], None, ALU.add)
            tt(cnt[:, :], cnt[:, :], start[:, :], ALU.subtract)
            dve.drain()
            nc.vector.tensor_copy(tail_i[:, :], tail_f[:, :])
            dve.drain().then_inc(tails_ready, 1)
            ts(tiles_f[:, :], cnt[:, :], 1.0 / 128, 127.0 / 128 - 0.498, ALU.mult, ALU.add)
            dve.drain()
            nc.vector.tensor_copy(tiles_i[:, :], tiles_f[:, :])
            dve.drain()
            nc.vector.tensor_copy(end[:, :], tiles_i[:, :])
            dve.drain()
            for e in range(1, E):
                tt(end[:, e:e + 1], end[:, e:e + 1], end[:, e - 1:e], ALU.add)
                dve.drain()
            tt(first[:, :], end[:, :], tiles_i[:, :], ALU.subtract)
            dve.drain()
            tt(own[:, :, :], bt(tile_no), bc(first), ALU.is_ge)
            tt(tmp[:, :, :], bt(tile_no), bc(end), ALU.is_ge)
            tt(off[:, :, :], bt(tile_no), bc(first), ALU.subtract)
            dve.drain()
            tt(own[:, :, :], own[:, :, :], tmp[:, :, :], ALU.subtract)
            ts(off[:, :, :], off[:, :, :], 128.0, None, ALU.mult)
            dve.drain()

            def table(dst, value):
                tt(tmp[:, :, :], own[:, :, :], value, ALU.mult)
                dve.drain()
                nc.vector.reduce_sum(dst[:, :], tmp[:, :, :].rearrange("p e n -> p n e"), AX.X)
                dve.drain()
            nc.vector.reduce_sum(t_used[:, :], own[:, :, :].rearrange("p e n -> p n e"), AX.X)
            table(t_exp, bc(eno))
            table(t_base, bc(start))
            table(t_valid, off[:, :, :])
            tt(t_base[:, :], t_base[:, :], t_valid[:, :], ALU.add)
            ts(t_used[:, :], t_used[:, :], -float(E * CAPR), float(E * CAPR), ALU.mult, ALU.add)
            dve.drain()
            tt(t_base[:, :], t_base[:, :], t_used[:, :], ALU.add)
            dve.drain()
            nc.vector.tensor_copy(base_i[:, :], t_base[0:1, :])
            nc.vector.tensor_copy(exp_i[:, :], t_exp[0:1, :])
            dve.drain().then_inc(tables, 1)
            tt(off[:, :, :], bc(cnt), off[:, :, :], ALU.subtract)
            dve.drain()
            table(t_valid, off[:, :, :])
            for e in range(E):
                nc.vector.scalar_tensor_tensor(out=mine[:, e, :], in0=r_all[:, :], scalar=float(E - e), in1=p_all[:, :],
                                               op0=ALU.is_equal, op1=ALU.mult)
            dve.drain()

            def count(i, than, op):
                tt(hit[:, :, :], mine[:, :, :], than[0:PP, :].rearrange("p (e o) -> p e o", o=1).broadcast_to([PP, E, PT]), op)
                dve.drain()
                nc.vector.reduce_sum(part[:, :], hit[:, :, :], AX.X).then_inc(counted, 1)
                dve.wait_ge(totalled, i + 1)
            with dve.Fori(0, 27, 1) as i:
                ts(cand[:, :], thr[:, :], step[:, 0:1], None, ALU.add)
                dve.drain()
                count(i, cand, ALU.is_ge)
                ts(ok[:, :], psC[:, 0:E], float(capacity), None, ALU.is_ge)
                dve.drain()
                nc.vector.scalar_tensor_tensor(out=thr[:, :], in0=ok[:, :], scalar=step[:, 0:1], in1=thr[:, :],
                                               op0=ALU.mult, op1=ALU.add)
                dve.drain()
                ts(step[:, :], step[:, :], 0.5, None, ALU.mult)
                dve.drain()
            count(27, thr, ALU.is_gt)
            ts(room[:, :], psC[:, 0:E], -1.0, float(capacity), ALU.mult, ALU.add)
            tt(hit[:, :, :], mine[:, :, :], thr[0:PP, :].rearrange("p (e o) -> p e o", o=1).broadcast_to([PP, E, PT]),
               ALU.not_equal)
            dve.drain()
            ts(hit[:, :, :], hit[:, :, :], 2.0 ** 20, None, ALU.mult)
            nc.vector.memset(step[:, :], 2.0 ** 14)
            dve.drain()
            tt(mine[:, :, :], hit[:, :, :], tok[:, :].rearrange("p (o n) -> p o n", o=1).broadcast_to([PP, E, PT]), ALU.add)
            dve.drain()
            with dve.Fori(28, 43, 1) as i:
                ts(cand[:, :], last_tok[:, :], step[:, 0:1], None, ALU.add)
                dve.drain()
                count(i, cand, ALU.is_lt)
                tt(ok[:, :], psC[:, 0:E], room[:, :], ALU.is_le)
                dve.drain()
                nc.vector.scalar_tensor_tensor(out=last_tok[:, :], in0=ok[:, :], scalar=step[:, 0:1], in1=last_tok[:, :],
                                               op0=ALU.mult, op1=ALU.add)
                dve.drain()
                ts(step[:, :], step[:, :], 0.5, None, ALU.mult)
                dve.drain()
            table(t_thr, bc(thr))
            table(t_last, bc(last_tok))

            def normalise(t, r, rounds):
                dve.wait_ge(row_loaded[r], rounds)
                ts(xf[r][:, :], row[r][:, 0:D], row[r][:, D + 1:D + 2], row[r][:, D:D + 1], ALU.subtract, ALU.mult)\
                    .then_inc(x_ready, 1)

            def decide(t, r):
                p, tk = row[r][:, D + 2:D + 3], row[r][:, D + 3:D + 4]
                col = bass.ds(t, 1)
                tt(over[:, :], p, t_thr[:, col], ALU.is_gt)
                tt(tie[:, :], p, t_thr[:, col], ALU.is_equal)
                tt(low[:, :], tk, t_last[:, col], ALU.is_lt)
                tt(val[:, :], lane[:, :], t_valid[:, col], ALU.is_lt)
                dve.drain()
                tt(tie[:, :], tie[:, :], low[:, :], ALU.mult)
                nc.vector.scalar_tensor_tensor(out=idm[:, :], in0=tk, scalar=-float(NOWHERE), in1=val[:, :],
                                               op0=ALU.add, op1=ALU.mult)
                dve.drain()
                tt(keep[:, :], over[:, :], tie[:, :], ALU.max)
                dve.wait_ge(out_free, t + 1)
                ts(dest[r][:, :], idm[:, :], float(NOWHERE), None, ALU.add)
                dve.drain()
                tt(kp[:, :], keep[:, :], p, ALU.mult)
                dve.drain()
                tt(dp[:, :], p, kp[:, :], ALU.subtract)
                dve.drain()
                nc.vector.scalar_tensor_tensor(out=pre[:, :], in0=xf[r][:, :], scalar=dp[:, 0:1], in1=row[r][:, 0:D],
                                               op0=ALU.mult, op1=ALU.add)
                dve.drain()

            def hid_copy(t, r):
                dve.wait_ge(ht_ready, t + 1)
                nc.vector.tensor_copy(hidT[r % 2][:, 0:384], psT[:, 0, 0:384]).then_inc(ht_dve, 1)

            def combine(t, r):
                dve.wait_ge(y_ready, t + 1)
                nc.vector.scalar_tensor_tensor(out=res[r][:, :], in0=psY[r % 2][:, 0:D], scalar=kp[:, 0:1], in1=pre[:, :],
                                               op0=ALU.mult, op1=ALU.add).then_inc(combined, 1)
                dve.drain()
            for t in range(2):
                normalise(t, t, 16)
            with dve.Fori(0, NT // RING - 1, 1) as k:
                for r in range(RING):
                    t = RING * k + r
                    hid_copy(t, r)
                    normalise(t + 2, (r + 2) % RING, 16 * k + (16 if r < 2 else 32))
                    decide(t, r)
                    combine(t, r)
            for t in range(NT - RING, NT):
                r = t % RING
                hid_copy(t, r)
                if t + 2 < NT:
                    normalise(t + 2, (r + 2) % RING, 16 * (NT // RING))
                decide(t, r)
                combine(t, r)

        @block.gpsimd
        def _(pool):
            pool.sem_inc(out_free, 4)
            pool.wait_ge(tails_ready, 1)
            pool.dma_start(xs[E * CAPR:E * CAPR + 128, :], zero_rows[:, :]).then_inc(tails_done, 16)
            for e in range(E):
                pool.indirect_dma_start(xs, bass.IndirectOffsetOnAxis(ap=tail_i[:, e:e + 1], axis=0),
                                        zero_rows[:, :], None).then_inc(tails_done, 16)

            def write(t, r, done):
                pool.wait_ge(combined, t + 1)
                pool.sem_inc(rows_seen, 1)
                pool.indirect_dma_start(out, bass.IndirectOffsetOnAxis(ap=dest[r][:, 0:1], axis=0), res[r][:, :], None,
                                        bounds_check=N - 1, oob_is_err=False).then_inc(scat[r], 16)
                pool.wait_ge(scat[r], done)
                pool.sem_inc(out_free, 1)
            with pool.Fori(0, NT // RING, 1) as k:
                for r in range(RING):
                    write(RING * k + r, r, 16 * k + 16)


ROWS_PER_EXPERT = BATCH * NTOK + 128
TILES = -(-BATCH * NTOK // 128) + E
TILES += -TILES % 4


def _constants():
    place = np.arange(TXT, dtype=np.float32)[:, None]
    dim = np.arange(D, dtype=np.float32)[None, :]
    angle = place / np.power(np.float32(10000.0), np.floor(dim / 2) * 2 / np.float32(D)).astype(np.float32)
    sel = np.zeros((12, 4, P), np.float32)
    for j in range(4):
        sel[3 * j:3 * j + 3, j] = 1
    here = np.arange(NTOK).reshape(QT, P).T
    outside = np.where(here < TXT, here + NIMG, here - TXT)
    tok = outside[:, None, :] + NTOK * np.arange(BATCH)[None, :, None]
    start = np.arange(E, dtype=np.float32) * ROWS_PER_EXPERT

    def on(a, n):
        return np.ascontiguousarray(np.broadcast_to(a, (n,) + a.shape)).astype(np.float32)
    return {
        "pos": np.where(np.arange(D) % 2 == 0, np.sin(angle), np.cos(angle)).astype(np.float32),
        "ident": np.eye(128, dtype=np.float32),
        "sel": sel,
        "before": np.triu(np.ones((P, P), np.float32), 1),
        "c8": on(np.broadcast_to(E - np.arange(E, dtype=np.float32), (QT, E)), P),
        "tok": tok.reshape(P, BATCH * QT).astype(np.float32),
        "start": on(start, 128),
        "tile_no": on(np.arange(TILES), 128),
        "lane": np.arange(128, dtype=np.float32)[:, None].copy(),
        "expert_no": on(np.arange(E), 128),
    }


def build(nc, t, out):
    def scratch(name, shape, dt=fp32):
        return nc.dram_tensor(name, shape, dt, kind="Internal").ap()
    h = scratch("h_rows", (BATCH, NTOK, D))
    xs = scratch("routed_rows", (E * ROWS_PER_EXPERT + 128, RW))
    stack = scratch("qk_parts", (2, 3, 2, D, NTOK), bf16)
    p_all, r_all = scratch("p_rows", (P, BATCH * QT)), scratch("r_rows", (P, BATCH * QT))
    counts = scratch("counts", (P, E))
    patch_embed(nc, t["x"], t["L0_tok_W"], t["L0_tok_b"], t["x_txt"], t["mask_BS_i2_0"], t["L0_txt_token_table"],
                t["L0_txt_segm_table"], t["pos"], t["ident"], h)
    attention(nc, BATCH, h, t["L0_attn_w_qkv"], t["L0_attn_b_qkv"], t["L0_attn_w_out"], t["L0_attn_b_out"],
              t["L0_ffn_switch_w"], t["L0_ffn_switch_b"], t["ident"], t["sel"], t["before"], t["c8"],
              t["tok"], t["start"][0:P, :], xs, stack, p_all, r_all, counts)
    experts(nc, BATCH * NTOK, BATCH * QT, ROWS_PER_EXPERT, TILES, xs, p_all, r_all, counts, t["start"], t["tok"],
            t["tile_no"], t["lane"], t["expert_no"], t["ident"], t["L0_ffn_w1"], t["L0_ffn_b1"], t["L0_ffn_w2"],
            t["L0_ffn_b2"], out)


def kernel(**inputs):
    import concourse.bacc as bacc
    from concourse.bass_utils import run_bass_kernel_spmd

    nc = bacc.Bacc("TRN2", target_bir_lowering=False, num_devices=1)
    laid = dict(inputs)
    for name in ("x_txt", "mask_BS_i2_0", "L0_attn_w_qkv", "L0_attn_w_out"):
        laid[name] = np.asarray(inputs[name]).T
    laid.update(_constants())
    arrays, tensors = {}, {}
    for name, a in laid.items():
        a = np.ascontiguousarray(a)
        arrays["in_" + name] = a
        tensors[name] = nc.dram_tensor("in_" + name, a.shape, mybir.dt.from_np(a.dtype), kind="ExternalInput").ap()
    out = nc.dram_tensor("out_rows", (BATCH * NTOK, D), fp32, kind="ExternalOutput").ap()
    build(nc, tensors, out)
    r = run_bass_kernel_spmd(nc, [arrays], core_ids=[0])
    return r.results[0]["out_rows"].reshape(BATCH, NTOK, D)
```

```python
import numpy as np
import concourse.bass as bass
from concourse import mybir
from contextlib import ExitStack

fp32 = mybir.dt.float32
bf16 = mybir.dt.bfloat16
i32 = mybir.dt.int32
ALU = mybir.AluOpType
ACT = mybir.ActivationFunctionType
AX = mybir.AxisListType

BATCH = 64
IMG = 224
PATCH = 16
GRID = IMG // PATCH
CH = 3
D = 192
TXT = 77
NIMG = GRID * GRID
NTOK = TXT + NIMG
GROUPS = 5
ROW = IMG * CH
SEG = PATCH * CH
KC = 6
EW = SEG // KC
TB = 4
D, NTOK, HEADS, HD = 192, 273, 12, 16
QT = 3
P = NTOK // QT
KH = D // 2
GRP = 3
E = 8
RW = D + 4
LEAD = 10
SLOTS = 18
Q_PART = (0, 0, 0, 1, 1, 2)
K_PART = (0, 1, 2, 0, 1, 0)
TAIL = ("N2", "ON0", "ON1", "OUT0", "OUT1", "X0", "X1", "LG", "RK")
NEXT = ("V0", "V1", "MT0")
AFTER = ("T0", "T1", "Q0", "Q1", "K0", "K1")
USES = {0: ("V0",), 1: ("N2",), 2: ("MT1", "V1"), 3: ("ON0",), 4: ("ON1",), 5: ("OUT0",), 6: ("OUT1",), 7: ("N0",),
        8: ("MT2",), 10: ("X0",), 11: ("X1", "T0"), 12: ("LG", "T1"), 13: ("N1",), 14: ("MT0", "Q0"), 15: ("Q1",),
        16: ("RK", "K0"), 17: ("K1",)}
MISC = tuple(name for i in sorted(USES) for name in USES[i])
START = AFTER + ("V0", "V1") + AFTER + ("MT0",)
D, F, E, RW = 192, 768, 8, 196
FC = F // 128
NOWHERE = 1000000


def patch_embed(nc, x, W, tok_b, idx_tok, idx_seg, tok_table, seg_table, pos, ident_in, h):
    half = 64
    tile_units = GRID
    with ExitStack() as ctx:
        def sb(name, shape, dt=fp32):
            return ctx.enter_context(nc.sbuf_tensor(name, shape, dt))

        def sem(name):
            return ctx.enter_context(nc.semaphore(name))

        img = [sb(f"img{i}", [128, PATCH * ROW]) for i in range(2)]
        wraw = sb("wraw", [128, KC, GROUPS, D])
        wv = [[sb(f"w_{r}_{c}", [128, KC, D]) for c in ("all", "off")] for r in ("mid", "top", "bottom")]
        patch = [sb(f"patch{i}", [128, KC * 128]) for i in range(2)]
        patchT = [sb(f"patchT{i}", [128, KC, 128]) for i in range(2)]
        stage = [sb(f"stage{i}", [128, GRID, D]) for i in range(2)]
        bias = sb("tok_bias", [128, D])
        ident = sb("identA", [128, 128])
        psT = [ctx.enter_context(nc.psum_tensor(f"psT{i}", [128, 2, 512], fp32)) for i in range(2)]
        psO = [ctx.enter_context(nc.psum_tensor(f"psO{i}", [128, 512], fp32)) for i in range(2)]
        idx_all = [sb(f"idx_all{i}", [TXT, BATCH], i32) for i in range(2)]
        idx_f = [sb(f"idx_f{i}", [TXT, BATCH]) for i in range(2)]
        wrap = [sb(f"idx_wrapped{i}", [TXT, BATCH]) for i in range(2)]
        idx_now = [[sb(f"idx_now{i}{j}", [TXT, TB], i32) for j in range(2)] for i in range(2)]
        tok_rows = [sb(f"tok_rows{i}", [TXT, TB, D]) for i in range(2)]
        seg_rows = [sb(f"seg_rows{i}", [TXT, TB, D]) for i in range(2)]
        txt_sum = [sb(f"txt_sum{i}", [TXT, TB, D]) for i in range(2)]
        pos_sb = sb("pos_sb", [TXT, D])

        w_loaded, const_loaded, w_ready = sem("w_loaded"), sem("const_loaded"), sem("w_ready")
        img_loaded = [sem(f"img_loaded{i}") for i in range(2)]
        ordered, transposed = sem("ordered"), sem("transposed")
        copied_dve, copied_act = sem("copied_dve"), sem("copied_act")
        embedded, staged = sem("embedded"), sem("staged")
        stored = [sem(f"stored{i}") for i in range(2)]
        txt_idx, idx_ready, with_pos, summed = sem("txt_idx"), sem("idx_ready"), sem("with_pos"), sem("summed")
        txt_got = [sem(f"txt_got{i}") for i in range(2)]
        txt_out = [sem(f"txt_out{i}") for i in range(2)]
        border_ready, idx_seen = sem("border_ready"), sem("idx_seen")
        block = ctx.enter_context(nc.Block())

        h_rows = h.rearrange("b t d -> b (t d)")

        def out_rows(gy):
            return h_rows[:, bass.ds((TXT + gy * GRID) * D, GRID * D)]

        x_rows = x.rearrange("b (gy r) w c -> gy b (r w c)", gy=GRID)

        @block.sync
        def _(sp):
            def load(par, gys):
                for i, gy in enumerate(gys):
                    for q in range(2):
                        n = PATCH * ROW // 2
                        src = x_rows[bass.ds(gy, 1), :, q * n:(q + 1) * n].rearrange("o b n -> (o b) n")
                        sp.dma_start(img[par][i * half:(i + 1) * half, q * n:(q + 1) * n], src)\
                          .then_inc(img_loaded[par], 16)

            def store(par, gys):
                for i, gy in enumerate(gys):
                    sp.dma_start(out_rows(gy), stage[par][i * half:(i + 1) * half, :, :]
                                 .rearrange("p g d -> p (g d)")).then_inc(stored[par], 16)

            load(0, (1, 2))
            load(1, (3, 4))
            with sp.Fori(0, 2, 1) as pair:
                k = 2 * pair
                for par in range(2):
                    sp.wait_ge(w_ready, 1)
                    sp.wait_ge(ordered, (k + par) * tile_units + tile_units)
                    load(par, (2 * k + 2 * par + 5, 2 * k + 2 * par + 6))
                    sp.wait_ge(w_ready, 1)
                    sp.wait_ge(staged, (k + par) * tile_units + tile_units + 2)
                    store(par, (2 * k + 2 * par + 1, 2 * k + 2 * par + 2))
            sp.wait_ge(ordered, 5 * tile_units)
            load(0, (0, GRID - 1))
            sp.wait_ge(staged, 5 * tile_units + 2)
            store(0, (9, 10))
            sp.wait_ge(staged, 6 * tile_units + 2)
            store(1, (11, 12))
            sp.wait_ge(staged, 7 * tile_units + 2)
            store(0, (0, GRID - 1))
            sp.wait_ge(stored[0], 4 * 32 + 32)
            sp.wait_ge(stored[1], 3 * 32 + 32)

        @block.scalar
        def _(act):
            act.dma_start(ident[:, :], ident_in).then_inc(const_loaded, 16)
            act.dma_start(bias[:, :], tok_b.rearrange("(o n) -> o n", o=1).broadcast_to([128, D]))\
               .then_inc(const_loaded, 16)
            wrows = W.rearrange("(py s e g c) n -> s c py e g n", py=PATCH, s=2, g=GROUPS, c=CH)
            for k in range(KC):
                act.dma_start(wraw[:, k, :, :], wrows[k // CH, k % CH]).then_inc(w_loaded, 16)
            act.sem_inc(copied_act, 2)

            def copies(u0, n):
                for i in range(n):
                    act.wait_ge(transposed, u0 + i + 3)
                    act.wait_ge(embedded, u0 + i + 1)
                    nc.scalar.activation(patchT[i % 2][:, 3:6, :].rearrange("p k n -> p (k n)"),
                                         psT[i % 2][:, 1, 0:384], ACT.Copy).then_inc(copied_act, 1)
            with act.Fori(0, 3, 1) as pair:
                k = 2 * pair
                copies(k * tile_units, 2 * tile_units)
            copies(6 * tile_units, tile_units)

        @block.tensor
        def _(pe):
            pe.wait_ge(const_loaded, 32)
            pe.sem_inc(embedded, 2)
            pe.sem_inc(transposed, 2)

            def embed(par, u0, border=False):
                def transposes(g):
                    u = u0 + g
                    pe.wait_ge(ordered, u + 1)
                    pe.wait_ge(copied_dve, u + 1)
                    pe.wait_ge(copied_act, u + 1)
                    for k in range(KC):
                        last = nc.tensor.transpose(psT[g % 2][:, k // 3, (k % 3) * 128:(k % 3) * 128 + 128],
                                                   patch[g % 2][:, k * 128:(k + 1) * 128], ident[:, :])
                    last.then_inc(transposed, 1)

                def product(g):
                    u = u0 + g
                    pe.wait_ge(copied_dve, u + 3)
                    pe.wait_ge(copied_act, u + 3)
                    pe.wait_ge(staged, u + 1)
                    for rows, m0, m1 in (((1, 0, half), (2, half, 128)) if border else ((0, 0, 128),)):
                        for k in range(KC):
                            off = (g == 0 and k < 3) or (g == GRID - 1 and k >= 3)
                            last = nc.tensor.matmul(psO[g % 2][m0:m1, 0:D], patchT[g % 2][:, k, m0:m1],
                                                    wv[rows][off][:, k, :], start=(k == 0), stop=(k == KC - 1))
                    last.then_inc(embedded, 1)
                transposes(0)
                for g in range(GRID):
                    if g + 1 < GRID:
                        transposes(g + 1)
                    if g == 0:
                        pe.wait_ge(w_ready, 1)
                    product(g)

            with pe.Fori(0, 3, 1) as pair:
                k = 2 * pair
                for par in range(2):
                    embed(par, k * tile_units + par * tile_units)
            pe.wait_ge(border_ready, 1)
            embed(0, 6 * tile_units, border=True)

        @block.vector
        def _(dve):
            dve.sem_inc(copied_dve, 2)
            dve.sem_inc(staged, 2)
            dve.sem_inc(stored[0], 32)
            dve.sem_inc(stored[1], 32)
            dve.wait_ge(w_loaded, 16 * KC)

            every, left, right = slice(0, KC), slice(0, 3), slice(3, KC)
            for dst, groups, chunks in ((wv[0][0], (0, 1, 2, 3, 4), every), (wv[0][1], (0, 1, 2), left),
                                        (wv[0][1], (0, 3, 4), right)):
                src = [wraw[:, chunks, g, :] for g in groups]
                nc.vector.tensor_tensor(dst[:, chunks, :], src[0], src[1], ALU.add)
                for later in src[2:]:
                    dve.drain()
                    nc.vector.tensor_tensor(dst[:, chunks, :], dst[:, chunks, :], later, ALU.add)
            dve.drain().then_inc(w_ready, 1)
            dve.wait_ge(const_loaded, 32)

            def order(par, u0, g):
                dve.wait_ge(transposed, u0 + g + 1)
                src = img[par][:, :].rearrange("p (r n) -> p r n", r=PATCH)[:, :, g * SEG:(g + 1) * SEG]
                dst = patch[g % 2][:, :].rearrange("p (s c r e) -> p s c r e", s=2, c=CH, r=PATCH)
                src = src.rearrange("p r (s e c) -> p s c r e", s=2, c=CH)
                for side in range(2):
                    last = nc.vector.tensor_copy(dst[:, side], src[:, side])
                last.then_inc(ordered, 1)

            def tile(par, u0, stores, loads):
                def copy(g):
                    u = u0 + g
                    dve.wait_ge(transposed, u + 3)
                    dve.wait_ge(embedded, u + 1)
                    nc.vector.tensor_copy(patchT[g % 2][:, 0:3, :].rearrange("p k n -> p (k n)"),
                                          psT[g % 2][:, 0, 0:384]).then_inc(copied_dve, 1)
                dve.wait_ge(img_loaded[par], loads)
                order(par, u0, 0)
                order(par, u0, 1)
                copy(0)
                dve.wait_ge(stored[par], stores)
                for g in range(GRID):
                    if g + 1 < GRID:
                        copy(g + 1)
                    if g + 2 < GRID:
                        order(par, u0, g + 2)
                    dve.wait_ge(embedded, u0 + g + 3)
                    nc.vector.tensor_tensor(stage[par][:, g, :], psO[g % 2][:, 0:D], bias[:, :], ALU.add)\
                      .then_inc(staged, 1)
            with dve.Fori(0, 3, 1) as pair:
                k = 2 * pair
                for par in range(2):
                    tile(par, k * tile_units + par * tile_units, k * 16 + 32, k * 32 + 64)
            tile(0, 6 * tile_units, 3 * 32 + 32, 4 * 64)

        @block.gpsimd
        def _(pool):
            pool.dma_start(idx_all[0][:, :], idx_tok).then_inc(txt_idx, 16)
            pool.dma_start(idx_all[1][:, :], idx_seg).then_inc(txt_idx, 16)
            pool.dma_start(pos_sb[:, :], pos).then_inc(txt_idx, 16)
            pool.wait_ge(txt_idx, 48)
            for i, size in enumerate((tok_table.shape[0], seg_table.shape[0])):
                nc.gpsimd.tensor_copy(idx_f[i][:, :], idx_all[i][:, :])
                pool.drain()
                nc.gpsimd.tensor_scalar(wrap[i][:, :], idx_f[i][:, :], 0.0, float(size), ALU.is_lt, ALU.mult)
                pool.drain()
                nc.gpsimd.tensor_tensor(wrap[i][:, :], wrap[i][:, :], idx_f[i][:, :], ALU.add)
                pool.drain()
                nc.gpsimd.tensor_scalar(wrap[i][:, :], wrap[i][:, :], 0.0, float(size - 1), ALU.max, ALU.min)
                pool.drain()

            def gather(n, par):
                pool.wait_ge(txt_idx, 48)
                for i in range(2):
                    nc.gpsimd.tensor_copy(idx_now[i][par][:, :], wrap[i][:, bass.ds(TB * n, TB)]).then_inc(idx_ready, 1)
                pool.wait_ge(txt_idx, 48)
                pool.wait_ge(idx_ready, 2 * n + 2)
                pool.sem_inc(idx_seen, 1)
                for j in range(TB):
                    for i, (table, rows) in enumerate(((tok_table, tok_rows), (seg_table, seg_rows))):
                        pool.indirect_dma_start(rows[par][:, j, :], None, table,
                                                bass.IndirectOffsetOnAxis(ap=idx_now[i][par][:, j:j + 1], axis=0))\
                            .then_inc(txt_got[par], 16)

            def add(n, par, half):
                pool.wait_ge(txt_idx, 48)
                pool.wait_ge(txt_got[par], 32 * TB * half + 32 * TB)
                nc.gpsimd.tensor_tensor(seg_rows[par][:, :, :], seg_rows[par][:, :, :],
                                        pos_sb[:, :].rearrange("p (o d) -> p o d", o=1).broadcast_to([TXT, TB, D]), ALU.add)\
                    .then_inc(with_pos, 1)
                pool.wait_ge(txt_idx, 48)
                pool.wait_ge(with_pos, n + 1)
                nc.gpsimd.tensor_tensor(txt_sum[par][:, :, :], seg_rows[par][:, :, :], tok_rows[par][:, :, :], ALU.add)\
                    .then_inc(summed, 1)
                pool.wait_ge(txt_idx, 48)
                pool.wait_ge(summed, n + 1)
                pool.dma_start(h[bass.ds(TB * n, TB), 0:TXT, :].rearrange("b t d -> t b d"), txt_sum[par][:, :, :])\
                    .then_inc(txt_out[par], 16)

            def stored_before(par, half):
                pool.wait_ge(txt_idx, 48)
                pool.wait_ge(txt_out[par], 16 * half)
            groups = BATCH // TB
            groups = BATCH // TB
            pool.wait_ge(w_loaded, 16 * KC)
            (top, top_off), (bot, bot_off) = wv[1:]
            every, left, right = slice(0, KC), slice(0, 3), slice(3, KC)
            up, down = (0, half), (half, 128)
            sums = [(top, (0, 1, 2, 3, 4), every, down), (top, (0, 1, 3), every, up),
                    (bot, (0, 1, 2, 3, 4), every, up), (bot, (0, 2, 4), every, down)]
            for side, g_mid, g_top, g_bot in ((left, (0, 1, 2), (0, 1), (0, 2)), (right, (0, 3, 4), (0, 3), (0, 4))):
                sums += [(top_off, g_mid, side, down), (top_off, g_top, side, up),
                         (bot_off, g_mid, side, up), (bot_off, g_bot, side, down)]
            for step in range(GROUPS - 1):
                for dst, groups_in, chunks, (p0, p1) in sums:
                    if step + 1 < len(groups_in):
                        out = dst[p0:p1, chunks, :]
                        so_far = wraw[p0:p1, chunks, groups_in[0], :] if step == 0 else out
                        nc.gpsimd.tensor_tensor(out, so_far, wraw[p0:p1, chunks, groups_in[step + 1], :], ALU.add)
                pool.drain()
            pool.sem_inc(border_ready, 1)
            gather(0, 0)
            gather(1, 1)
            for par in range(2):
                add(par, par, 0)
                gather(par + 2, par)
            with pool.Fori(1, groups // 2 - 1, 1) as pair:
                for par in range(2):
                    stored_before(par, pair)
                    add(2 * pair + par, par, pair)
                    gather(2 * pair + par + 2, par)
            for par in range(2):
                stored_before(par, groups // 2 - 1)
                add(groups - 2 + par, par, groups // 2 - 1)
            for par in range(2):
                pool.wait_ge(txt_out[par], 16 * (groups // 2))


def attention(nc, NB, h, wqkvT, bqkv, woT, bo, sw, swb, ident_in, tri_in, c8_in, tok_in, run_in,
              xs, stack, p_all_d, r_all_d, cnt_d):
    def listed(tail, ln, prep):
        return [m for m in MISC if (tail or m not in TAIL) and (ln or m not in AFTER) and (prep or m not in NEXT)]

    class Use:

        def __init__(self, base, turn, pos):
            fixed = base if isinstance(base, int) else 0
            self.before, self.bank = base + turn + pos, (fixed + turn + pos) % 2
            self.prior = (base + turn + pos) // 2 if isinstance(base, int) else base // 2 + (turn + pos) // 2

    def use(b, name, tail=True, ln=True, prep=True):
        if isinstance(b, str):
            return Use(0, 0, name)
        first = len(START)
        if isinstance(b, int):
            kinds = [(k > 0, k + 2 < NB, k + 1 < NB) for k in range(b)] + [(tail, ln, prep)]
            base = first + sum(len(listed(*k)) for k in kinds[:-1])
            names = TAIL if b == NB else listed(*kinds[-1])
            return Use(base, 0, list(names).index(name))
        u = Use(0, first + len(listed(False, True, True)), MISC.index(name))
        u.before, u.prior = u.before + len(MISC) * (b - 1), u.prior + len(MISC) // 2 * (b - 1)
        return u

    with ExitStack() as ctx:
        def sb(name, shape, dt=fp32):
            return ctx.enter_context(nc.sbuf_tensor(name, shape, dt))

        def sem(name):
            return ctx.enter_context(nc.semaphore(name))

        ident, identb = sb("identB", [128, 128]), sb("identb", [128, 128], bf16)
        w_qkv = sb("w_qkv", [KH + 1, 2, 3 * D])
        w_out = sb("w_out", [KH + 1, 2, D])
        w_sw = sb("w_sw", [KH + 1, 2, E])
        tri, ones = sb("tri", [P, P]), sb("ones", [P, P])
        c8 = sb("c8", [P, QT, E])
        tok_all = sb("tok_all", [P, NB * QT])
        p_all, r_all = sb("p_all", [P, NB * QT]), sb("r_all", [P, NB * QT])
        h_in = [sb(f"h_in{i}", [P, QT, D]) for i in range(2)]
        h_res = [sb(f"h_res{i}", [P, QT, D]) for i in range(2)]
        stats, mv = sb("stats", [P, QT, 6]), sb("mv", [P, QT, 2])
        neg_mean, neg_mean2 = sb("neg_mean", [P, QT]), sb("neg_mean2", [P, QT])
        var_eps, rstd, mhalf = sb("var_eps", [P, QT]), sb("rstd", [P, QT]), sb("mhalf", [P, QT])
        xn = [sb(f"xn{i}", [P, QT, D]) for i in range(2)]
        xnT = sb("xnT", [KH + 1, 2, NTOK])
        qk_f = sb("qk_f", [KH, 4, NTOK])
        qk_r = sb("qk_r", [KH, 4, NTOK])
        parts = sb("parts", [KH, 4, 3, NTOK], bf16)
        Qs = [sb(f"Qs{i}", [KH + 2, HEADS, NTOK], bf16) for i in range(2)]
        Ks = [sb(f"Ks{i}", [KH + 2, HEADS, NTOK], bf16) for i in range(2)]
        V = [sb(f"V{i}", [P, QT, HEADS, 32]) for i in range(2)]
        neg_max = [sb(f"neg_max{i}", [P, QT, HEADS]) for i in range(2)]
        shift = sb("shift", [P, QT, 2, 4], bf16)
        mT = [sb(f"mT{i}", [8, NTOK], bf16) for i in range(GRP)]
        Pr = [sb(f"Pr{i}", [P, NTOK]) for i in range(8)]
        O_sb = [sb(f"O_sb{i}", [128, NTOK]) for i in range(2)]
        inv = sb("inv", [P, QT, 4])
        On = [sb(f"On{i}", [P, QT, D]) for i in range(2)]
        OnT = sb("OnT", [KH + 1, 2, NTOK])
        zeros = sb("zeros", [KH, NTOK])
        neg_mr, neg_mr2 = sb("neg_mr", [P, QT]), sb("neg_mr2", [P, QT])
        row = [sb(f"row{i}", [P, QT, RW]) for i in range(2)]
        stats2, mv2 = sb("stats2", [P, QT, 6]), sb("mv2", [P, QT, 2])
        var_eps2, rstd2 = sb("var_eps2", [P, QT]), sb("rstd2", [P, QT])
        xf = sb("xf", [P, QT, D])
        xfT = sb("xfT", [KH + 1, 2, NTOK])
        lmax, ls, ex = sb("lmax", [P, QT]), sb("ls", [P, QT, E]), sb("ex", [P, QT, E])
        esum, k8, oh = sb("esum", [P, QT]), sb("k8", [P, QT, E]), sb("oh", [P, QT, E])
        prob, r8 = sb("prob", [P, QT]), sb("r8", [P, QT])
        run = sb("run", [P, E])
        place, slotf = sb("place", [P, QT, E]), sb("slotf", [P, QT])
        slot = [sb(f"slot{i}", [P, QT], i32) for i in range(2)]

        psS = [ctx.enter_context(nc.psum_tensor(f"psS{i}", [128, 512], fp32)) for i in range(2)]
        psE = [ctx.enter_context(nc.psum_tensor(f"psE{i}", [128, 512], fp32)) for i in range(3)]
        psO = ctx.enter_context(nc.psum_tensor("psAttn", [128, 512], fp32))
        psM = [ctx.enter_context(nc.psum_tensor(f"psM{i}", [128, 512], fp32)) for i in range(2)]

        const_loaded, prepared = sem("const_loadedB"), sem("prepared")
        h_loaded = [sem(f"h_loaded{i}") for i in range(2)]
        hres_loaded = [sem(f"hres_loaded{i}") for i in range(2)]
        var_ready, rstd_ready, xn_ready = sem("var_ready"), sem("rstd_ready"), sem("xn_ready")
        misc_ready, misc_free = sem("misc_ready"), [sem(f"misc_free{i}") for i in range(2)]
        qk_hi, res_done, mid_done, parts_ready = sem("qk_hi"), sem("res_done"), sem("mid_done"), sem("parts_ready")
        stack_stored, stack_loaded = sem("stack_stored"), sem("stack_loaded")
        scored, maxed, shift_ready = sem("scored"), sem("maxed"), sem("shift_ready")
        shifted, exped, weighted = sem("shifted"), sem("exped"), sem("weighted")
        o_read, o_ready = sem("o_read"), sem("o_ready")
        shift_loaded = [sem(f"shift_loaded{i}") for i in range(GRP)]
        var2_ready, rstd2_ready, xf_ready = sem("var2_ready"), sem("rstd2_ready"), sem("xf_ready")
        h2_ready = sem("h2_ready")
        ls_ready, ex_ready, oh_ready, row_ready = sem("ls_ready"), sem("ex_ready"), sem("oh_ready"), sem("row_ready")
        rows_free = sem("rows_free")
        scattered = [sem(f"scattered{i}") for i in range(2)]
        finished, stacks_seen = sem("finishedB"), sem("stacks_seen")
        block = ctx.enter_context(nc.Block())
        h_v = h.rearrange("b (t p) d -> b p t d", p=P)

        def bodies(eng, body, final):
            body(0, 0, tail=False, ln=True, prep=True)
            with eng.Fori(0, (NB - 4) // 2, 1) as pair:
                body(2 * pair + 1, 1, tail=True, ln=True, prep=True)
                body(2 * pair + 2, 0, tail=True, ln=True, prep=True)
            body(NB - 3, (NB - 3) % 2, tail=True, ln=True, prep=True)
            body(NB - 2, (NB - 2) % 2, tail=True, ln=False, prep=True)
            body(NB - 1, (NB - 1) % 2, tail=True, ln=False, prep=False)
            final(NB, NB % 2)

        def wait_use(eng, u):
            eng.wait_ge(misc_ready, u.before + 1)

        def wait_copied(eng, u):
            eng.wait_ge(misc_free[u.bank], u.prior + 1)

        @block.sync
        def _(sp):
            for dst, src in ((w_qkv[0:KH, 0, :], wqkvT[0:KH, :]), (w_qkv[0:KH, 1, :], wqkvT[KH:D, :]),
                             (w_qkv[KH:KH + 1, 1, :], bqkv.rearrange("(o n) -> o n", o=1)),
                             (ident[:, :], ident_in), 
                             (tri[:, :], tri_in), (c8[:, :, :], c8_in), (tok_all[:, :], tok_in),
                             (run[:, :], run_in), (w_sw[0:KH, 0, :], sw[0:KH, :]), (w_sw[0:KH, 1, :], sw[KH:D, :]),
                             (w_sw[KH:KH + 1, 1, :], swb.rearrange("(o n) -> o n", o=1))):
                sp.dma_start(dst, src).then_inc(const_loaded, 16)
            for dst, src in ((w_out[0:KH, 0, :], woT[0:KH, :]), (w_out[0:KH, 1, :], woT[KH:D, :]),
                             (w_out[KH:KH + 1, 1, :], bo.rearrange("(o n) -> o n", o=1))):
                sp.dma_start(dst, src).then_inc(const_loaded, 16)

            def load_h(b, par):
                sp.dma_start(h_in[par][:, :, :], h_v[bass.ds(b, 1)].rearrange("o p t d -> (o p) t d"))\
                  .then_inc(h_loaded[par], 16)

            def load_res(b, par):
                sp.dma_start(h_res[par][:, :, :], h_v[bass.ds(b, 1)].rearrange("o p t d -> (o p) t d"))\
                  .then_inc(hres_loaded[par], 16)

            def store_parts(n, par):
                for m in range(4):
                    sp.wait_ge(parts_ready, 4 * n + m + 1)
                    dst = stack[par, :, m // 2, KH * (m % 2):KH * (m % 2) + KH, :].rearrange("s r n -> r s n")
                    sp.dma_start(dst, parts[:, m, :, :]).then_inc(stack_stored, 16)

            def load_stacks(n, par):
                sp.wait_ge(stack_stored, 64 * n + 64)
                for s in range(6):
                    for kind, tile, part in ((0, Qs, Q_PART), (1, Ks, K_PART)):
                        src = stack[par, part[s], kind, :, :].rearrange("(h d) n -> d h n", d=HD)
                        sp.dma_start(tile[par][HD * s:HD * s + HD, :, :], src).then_inc(stack_loaded, 16)

            def load_shift(b, par, g, u):
                wait_copied(sp, u)
                for s in range(2):
                    sp.dma_start(Qs[par][KH + s:KH + s + 1, 4 * g:4 * g + 4, :].rearrange("o j n -> o (j n)"),
                                 mT[g][4 * s:4 * s + 4, :]).then_inc(shift_loaded[g], 16)

            load_h(0, 0)
            load_h(1, 1)
            store_parts(0, 0)
            load_stacks(0, 0)
            store_parts(1, 1)
            load_shift(0, 0, 0, use("start", len(START) - 1))

            def body(b, par, tail, ln, prep):
                if prep:
                    if tail:
                        sp.wait_ge(shifted, 36 * b + 3)
                        sp.sem_inc(stacks_seen, 1)
                    load_stacks(b + 1, 1 - par)
                load_shift(b, par, 1, use(b, "MT1", tail, ln, prep))
                if ln:
                    sp.wait_ge(xn_ready, b + 1)
                    load_h(b + 2, par)
                load_shift(b, par, 2, use(b, "MT2", tail, ln, prep))
                if tail:
                    sp.wait_ge(h2_ready, b)
                load_res(b, par)
                if prep:
                    load_shift(b + 1, 1 - par, 0, use(b, "MT0", tail, ln, prep))
                if ln:
                    store_parts(b + 2, par)
            bodies(sp, body, lambda b, par: None)
            sp.wait_ge(finished, 1)
            sp.dma_start(p_all_d, p_all[:, :]).then_inc(finished, 16)
            sp.dma_start(r_all_d, r_all[:, :]).then_inc(finished, 16)
            sp.dma_start(cnt_d, run[:, :]).then_inc(finished, 16)
            sp.wait_ge(finished, 49)
            sp.wait_ge(rows_free, NB + 2)

        @block.tensor
        def _(pe):
            pe.sem_inc(shifted, 3)
            pe.sem_inc(weighted, 2)
            pe.wait_ge(const_loaded, 16 * 14)
            pe.wait_ge(prepared, 2)

            def score(b, par, u):
                g, r = divmod(u, 12)
                qt, j = divmod(r, 4)
                hd = 4 * g + j
                pe.wait_ge(maxed, 36 * b + u + 1)
                nc.tensor.matmul(psS[u % 2][0:P, 0:NTOK], Qs[par][0:KH, hd, P * qt:P * qt + P], Ks[par][0:KH, hd, :],
                                 start=True, stop=True).then_inc(scored, 1)

            def shifted_score(b, par, u):
                g, r = divmod(u, 12)
                kt, j = divmod(r, 4)
                if r == 0:
                    pe.wait_ge(shift_loaded[g], 32 * b + 32)
                pe.wait_ge(exped, 36 * b + u + 1)
                nc.tensor.matmul(psE[u % 3][0:P, 0:NTOK], Ks[par][:, 4 * g + j, P * kt:P * kt + P],
                                 Qs[par][:, 4 * g + j, :], start=True, stop=True).then_inc(shifted, 1)

            def weigh(b, par, m):
                g, kt = divmod(m, 3)
                pe.wait_ge(exped, 36 * b + 4 * m + 7)
                if kt == 0:
                    pe.wait_ge(o_read, 3 * b + g + 1)
                for j in range(4):
                    last = nc.tensor.matmul(psO[32 * j:32 * j + 32, 0:NTOK], V[par][:, kt, 4 * g + j, :],
                                            Pr[(4 * par + 4 * m + j) % 8][:, :], start=(kt == 0), stop=(kt == 2))
                last.then_inc(weighted, 1)

            def transpose_x(ps, src, c):
                for t in range(QT):
                    last = nc.tensor.transpose(ps[0:KH, P * t:P * t + P], src[:, t, KH * c:KH * c + KH], ident[0:P, 0:P])
                return last

            def misc(name, b, par, u, get):
                ps = psM[u.bank]
                if name in ("T0", "T1"):
                    pe.wait_ge(xn_ready, b + 1)
                elif name in ("Q0", "V0"):
                    wait_copied(pe, get("T0"))
                    wait_copied(pe, get("T1"))
                elif name[:2] == "MT":
                    pe.wait_ge(shift_ready, 3 * b + int(name[2]) + 1)
                elif name in ("N0", "N1", "N2"):
                    pe.wait_ge(o_read, 3 * b + int(name[1]) + 2)
                elif name == "ON0":
                    pe.wait_ge(o_ready, 3 * b + 3)
                elif name == "OUT0":
                    wait_copied(pe, get("ON0"))
                    wait_copied(pe, get("ON1"))
                elif name == "X0":
                    pe.wait_ge(xf_ready, b + 1)
                elif name == "LG":
                    wait_copied(pe, get("X0"))
                    wait_copied(pe, get("X1"))
                elif name == "RK":
                    pe.wait_ge(oh_ready, b + 1)
                if not (isinstance(u.prior, int) and u.prior == 0):
                    pe.wait_ge(misc_free[u.bank], u.prior)
                if name[0] == "T":
                    last = transpose_x(ps, xn[par], int(name[1]))
                elif name[0] in "QK":
                    f = (0 if name[0] == "Q" else D) + KH * int(name[1])
                    for c in range(2):
                        last = nc.tensor.matmul(ps[0:KH, 0:NTOK], w_qkv[0:KH + c, c, f:f + KH], xnT[0:KH + c, c, :],
                                                start=(c == 0), stop=(c == 1))
                elif name[0] == "V":
                    for i, t in enumerate(((0, 1), (2,))[int(name[1])]):
                        for c in range(2):
                            last = nc.tensor.matmul(ps[0:P, D * i:D * i + D], xnT[0:KH + c, c, P * t:P * t + P],
                                                    w_qkv[0:KH + c, c, 2 * D:3 * D], start=(c == 0), stop=(c == 1))
                elif name[:2] == "MT":
                    rows = ps[:, :].bitcast(bf16)
                    for t in range(QT):
                        last = nc.tensor.transpose(rows[0:8, P * t + t:P * t + t + P],
                                                   shift[:, t, :, :].rearrange("p s j -> p (s j)"), identb[0:P, 0:P])
                elif name in ("N0", "N1", "N2"):
                    g = int(name[1])
                    for t in range(QT):
                        last = nc.tensor.transpose(ps[0:P, 128 * t:128 * t + 128],
                                                   O_sb[(g + par) % 2][:, P * t:P * t + P], ident[:, :])
                elif name[:2] == "ON":
                    last = transpose_x(ps, On[par], int(name[2]))
                elif name[:3] == "OUT":
                    for i, t in enumerate(((0, 1), (2,))[int(name[3])]):
                        for c in range(2):
                            last = nc.tensor.matmul(ps[0:P, D * i:D * i + D], OnT[0:KH + c, c, P * t:P * t + P],
                                                    w_out[0:KH + c, c, :], start=(c == 0), stop=(c == 1))
                elif name[0] == "X":
                    last = transpose_x(ps, xf, int(name[1]))
                elif name == "LG":
                    for t in range(QT):
                        for c in range(2):
                            last = nc.tensor.matmul(ps[0:P, E * t:E * t + E], xfT[0:KH + c, c, P * t:P * t + P],
                                                    w_sw[0:KH + c, c, :], start=(c == 0), stop=(c == 1))
                else:
                    for t in range(QT + 1):
                        if t < QT:
                            last = nc.tensor.matmul(ps[0:P, E * t:E * t + E], tri[:, :], oh[:, t, :],
                                                    start=True, stop=(t == 0))
                        for before in range(t):
                            last = nc.tensor.matmul(ps[0:P, E * t:E * t + E], ones[:, :], oh[:, before, :],
                                                    start=(t == QT and before == 0), stop=(before == t - 1))
                last.then_inc(misc_ready, 1)

            def start_misc(i, b):
                u = use("start", i)
                base = 0 if i < len(AFTER) + 2 else len(AFTER) + 2
                misc(START[i], b, b, u, lambda name: use("start", base + AFTER.index(name)))
            for i in range(len(START) - 1):
                start_misc(i, 0 if i < len(AFTER) + 2 else 1)
            pe.wait_ge(stack_loaded, 192)
            for k in range(LEAD):
                score(0, 0, 2 * k)
                score(0, 0, 2 * k + 1)
                if k == 6:
                    start_misc(len(START) - 1, 0)

            def body(b, par, tail, ln, prep):
                n = b + 1
                for i in range(SLOTS):
                    k = i + LEAD
                    if k < SLOTS:
                        score(b, par, 2 * k)
                        score(b, par, 2 * k + 1)
                    elif prep:
                        if k == SLOTS:
                            pe.wait_ge(stack_loaded, 192 * n + 192)
                        score(n, 1 - par, 2 * (k - SLOTS))
                        score(n, 1 - par, 2 * (k - SLOTS) + 1)
                    shifted_score(b, par, 2 * i)
                    shifted_score(b, par, 2 * i + 1)
                    if i % 2 == 0:
                        if i:
                            weigh(b, par, i // 2 - 1)
                        elif tail:
                            weigh(b - 1, 1 - par, 8)
                    for name in USES.get(i, ()):
                        if name in TAIL:
                            if tail:
                                misc(name, b - 1, 1 - par, use(b, name, tail, ln, prep),
                                     lambda x: use(b, x, tail, ln, prep))
                        elif name in NEXT:
                            if prep:
                                misc(name, n, 1 - par, use(b, name, tail, ln, prep),
                                     (lambda x: use(b - 1, x)) if tail else
                                     (lambda x: use("start", len(AFTER) + 2 + AFTER.index(x))))
                        elif name in AFTER:
                            if ln:
                                misc(name, b + 2, par, use(b, name, tail, ln, prep), lambda x: use(b, x, tail, ln, prep))
                        else:
                            misc(name, b, par, use(b, name, tail, ln, prep), None)

            def final(b, par):
                weigh(b - 1, 1 - par, 8)
                for name in TAIL:
                    misc(name, b - 1, 1 - par, use(b, name), lambda x: use(b, x))
            bodies(pe, body, final)

        @block.scalar
        def _(act):
            act.sem_inc(exped, 3)
            act.sem_inc(o_read, 1)
            act.wait_ge(prepared, 2)

            def exponent(b, par, u):
                act.wait_ge(shifted, 36 * b + u + 4)
                act.wait_ge(weighted, 9 * b + u // 4 + 1)
                nc.scalar.activation(Pr[(4 * par + u) % 8][:, :], psE[u % 3][0:P, 0:NTOK], ACT.Exp).then_inc(exped, 1)

            def read_group(b, par, g):
                act.wait_ge(weighted, 9 * b + 3 * g + 3 + 2)
                if not (isinstance(b, int) and b == 0 and g < 2):
                    act.wait_ge(o_ready, 3 * b + g - 1)
                nc.scalar.activation(O_sb[(g + par) % 2][:, :], psO[:, 0:NTOK], ACT.Copy).then_inc(o_read, 1)

            def apply(b, src, dst, rs, nmr, ready, done):
                act.wait_ge(ready, b + 1)
                for t in range(QT):
                    last = nc.scalar.activation(dst[:, t, :], src[:, t, 0:D], ACT.Identity, bias=nmr[:, t:t + 1],
                                                scale=rs[:, t:t + 1])
                last.then_inc(done, 1)

            def copy(name, b, par, u):
                ps = psM[u.bank]
                wait_use(act, u)
                free = misc_free[u.bank]
                if name[0] == "T":
                    nc.scalar.activation(xnT[0:KH, int(name[1]), :], ps[0:KH, 0:NTOK], ACT.Copy).then_inc(free, 1)
                elif name[0] in "QK":
                    m = (0 if name[0] == "Q" else 2) + int(name[1])
                    scale = HD ** -0.5 if name[0] == "Q" else 1.0
                    if not (isinstance(b, int) and b == 0):
                        act.wait_ge(stack_stored, 64 * b)
                    nc.scalar.activation(parts[:, m, 0, :], ps[0:KH, 0:NTOK], ACT.Copy, scale=scale).then_inc(qk_hi, 1)
                    nc.scalar.activation(qk_f[:, m, :], ps[0:KH, 0:NTOK], ACT.Copy, scale=scale).then_inc(free, 1)
                elif name[0] == "V":
                    if name == "V0":
                        act.wait_ge(weighted, 2 if isinstance(b, int) and b == 0 else 9 * b - 7)
                    for i, t in enumerate(((0, 1), (2,))[int(name[1])]):
                        last = nc.scalar.activation(V[par][:, t, :, 0:HD],
                                                    ps[0:P, D * i:D * i + D].rearrange("p (h d) -> p h d", d=HD), ACT.Copy)
                    last.then_inc(free, 1)
                elif name[:2] == "MT":
                    rows = ps[:, :].bitcast(bf16)
                    nc.scalar.activation(mT[int(name[2])][:, :].rearrange("p (t n) -> p t n", t=QT),
                                         rows[0:8, 0:QT * (P + 1)].rearrange("p (t n) -> p t n", t=QT)[:, :, 0:P], ACT.Copy)\
                      .then_inc(free, 1)
                elif name[:2] == "ON":
                    nc.scalar.activation(OnT[0:KH, int(name[2]), :], ps[0:KH, 0:NTOK], ACT.Copy).then_inc(free, 1)
                else:
                    nc.scalar.activation(xfT[0:KH, int(name[1]), :], ps[0:KH, 0:NTOK], ACT.Copy).then_inc(free, 1)

            def exp_logits(p):
                act.wait_ge(ls_ready, p + 1)
                nc.scalar.activation(ex[:, :, :], ls[:, :, :], ACT.Exp).then_inc(ex_ready, 1)

            apply(0, h_in[0], xn[0], rstd, neg_mr, rstd_ready, xn_ready)
            apply(1, h_in[1], xn[1], rstd, neg_mr, rstd_ready, xn_ready)
            for i, name in enumerate(START):
                copy(name, 1 if len(AFTER) + 2 <= i < len(START) - 1 else 0, 0, use("start", i))
            mine = ("V0", "V1", "ON0", "ON1", "X0", "X1", "T0", "T1", "Q0", "Q1", "K0", "K1", "MT0", "MT1", "MT2")

            def body(b, par, tail, ln, prep):
                for i in range(SLOTS):
                    exponent(b, par, 2 * i)
                    exponent(b, par, 2 * i + 1)
                    if i == 0 and tail:
                        read_group(b - 1, 1 - par, 2)
                    if i in (6, 12):
                        read_group(b, par, i // 6 - 1)
                    if i == 8 and ln:
                        apply(b + 2, h_in[par], xn[par], rstd, neg_mr, rstd_ready, xn_ready)
                    if i == 9 and tail:
                        apply(b - 1, row[1 - par], xf, rstd2, neg_mr2, rstd2_ready, xf_ready)
                    if i == 13 and tail:
                        exp_logits(b - 1)
                    for name in USES.get(i, ()):
                        if name in mine and (tail or name not in TAIL) and (ln or name not in AFTER) \
                                and (prep or name not in NEXT):
                            of, q = (b - 1, 1 - par) if name in TAIL else (b + 1, 1 - par) if name in NEXT else \
                                (b + 2, par) if name in AFTER else (b, par)
                            copy(name, of, q, use(b, name, tail, ln, prep))

            def final(b, par):
                read_group(b - 1, 1 - par, 2)
                copy("ON0", b - 1, 1 - par, use(b, "ON0"))
                copy("ON1", b - 1, 1 - par, use(b, "ON1"))
                apply(b - 1, row[1 - par], xf, rstd2, neg_mr2, rstd2_ready, xf_ready)
                copy("X0", b - 1, 1 - par, use(b, "X0"))
                copy("X1", b - 1, 1 - par, use(b, "X1"))
                exp_logits(b - 1)
            bodies(act, body, final)

        @block.vector
        def _(dve):
            nc.vector.memset(xnT[KH:KH + 1, 1, :], 1.0)
            nc.vector.memset(xfT[KH:KH + 1, 1, :], 1.0)
            nc.vector.memset(OnT[KH:KH + 1, 1, :], 1.0)
            nc.vector.memset(ones[:, :], 1.0)
            nc.vector.memset(zeros[:, :], 0.0)
            nc.vector.memset(mhalf[:, :], -0.5)
            for i in range(2):
                nc.vector.memset(V[i][:, :, :, :], 1.0)
                nc.vector.memset(Ks[i][KH:KH + 2, :, :], 1.0)
            dve.drain().then_inc(prepared, 1)
            dve.sem_inc(maxed, 2)
            dve.wait_ge(const_loaded, 16 * 14)
            nc.vector.tensor_copy(identb[:, :], ident[:, :])
            dve.drain().then_inc(prepared, 1)

            def maximum(b, par, u):
                g, r = divmod(u, 12)
                qt, j = divmod(r, 4)
                dve.wait_ge(scored, 36 * b + u + 1)
                nc.vector.reduce_max(neg_max[par][:, qt, 4 * g + j:4 * g + j + 1], psS[u % 2][0:P, 0:NTOK], AX.X,
                                     negate=True).then_inc(maxed, 1)

            def split_shift(b, par, g):
                nm = neg_max[par][:, :, 4 * g:4 * g + 4]
                dve.drain()
                nc.vector.tensor_copy(shift[:, :, 0, :], nm)
                dve.drain()
                nc.vector.tensor_tensor(shift[:, :, 1, :], nm, shift[:, :, 0, :], ALU.subtract)
                dve.drain().then_inc(shift_ready, 1)

            def ln_stats(src, st, m, nm, ve, signal):
                for t in range(QT):
                    nc.vector.bn_stats(st[:, t, :], src[:, t, 0:D])
                dve.drain()
                for t in range(QT):
                    nc.vector.bn_aggr(m[:, t, :], st[:, t, :])
                dve.drain()
                nc.vector.tensor_scalar(nm[:, :], m[:, :, 0], -1.0, None, ALU.mult)
                nc.vector.tensor_scalar(ve[:, :], m[:, :, 1], 1e-5, None, ALU.add).then_inc(signal, 1)

            def ln1_stats(b, par):
                dve.drain()
                dve.wait_ge(h_loaded[par], 8 * (b - par) + 16)
                ln_stats(h_in[par], stats, mv, neg_mean, var_eps, var_ready)

            def normalise(b, par, g, u):
                wait_use(dve, u)
                v = psM[u.bank][0:P, 0:QT * 128].rearrange("p (t j r) -> p t j r", t=QT, j=4)
                nc.vector.reciprocal(inv[:, :, :], v[:, :, :, HD])
                dve.drain()
                dst = On[par][:, :, 4 * HD * g:4 * HD * (g + 1)].rearrange("p t (j r) -> p t j r", j=4)
                nc.vector.tensor_tensor(dst, v[:, :, :, 0:HD], inv[:, :, :].rearrange("p t (j o) -> p t j o", o=1)
                                        .broadcast_to([P, QT, 4, HD]), ALU.mult).then_inc(misc_free[u.bank], 1)
                dve.drain().then_inc(o_ready, 1)

            def residual(u, half, p, par):
                if half == 0:
                    dve.wait_ge(hres_loaded[par], 8 * (p - par) + 16)
                    dve.wait_ge(rows_free, p + 1)
                    wait_use(dve, u)
                    nc.vector.tensor_tensor(row[par][:, 0:2, 0:D],
                                            psM[u.bank][0:P, 0:2 * D].rearrange("p (t d) -> p t d", t=2),
                                            h_res[par][:, 0:2, :], ALU.add).then_inc(misc_free[u.bank], 1)
                else:
                    wait_use(dve, u)
                    nc.vector.tensor_tensor(row[par][:, 2, 0:D], psM[u.bank][0:P, 0:D], h_res[par][:, 2, :], ALU.add)\
                      .then_inc(misc_free[u.bank], 1)

            def ln2_stats(p, par):
                dve.drain().then_inc(h2_ready, 1)
                ln_stats(row[par], stats2, mv2, neg_mean2, var_eps2, var2_ready)

            def ln2_columns(p, par):
                dve.wait_ge(rstd2_ready, p + 1)
                nc.vector.tensor_copy(row[par][:, :, D], rstd2[:, :])
                nc.vector.tensor_copy(row[par][:, :, D + 1], mv2[:, :, 0])
                nc.vector.tensor_copy(row[par][:, :, D + 3], tok_all[:, bass.ds(QT * p, QT)])

            def logits(u, p):
                wait_use(dve, u)
                lg = psM[u.bank][0:P, 0:QT * E].rearrange("p (t e) -> p t e", e=E)
                nc.vector.reduce_max(lmax[:, :], lg, AX.X)
                dve.drain()
                nc.vector.tensor_tensor(ls[:, :, :], lg, lmax[:, :].rearrange("p (t o) -> p t o", o=1)
                                        .broadcast_to([P, QT, E]), ALU.subtract).then_inc(misc_free[u.bank], 1)
                dve.drain().then_inc(ls_ready, 1)

            def route(p, par):
                dve.wait_ge(ex_ready, p + 1)
                nc.vector.reduce_sum(esum[:, :], ex[:, :, :], AX.X)
                nc.vector.scalar_tensor_tensor(out=k8[:, :, :], in0=ex[:, :, :], scalar=1.0, in1=c8[:, :, :],
                                               op0=ALU.is_ge, op1=ALU.mult)
                dve.drain()
                nc.vector.reciprocal(prob[:, :], esum[:, :])
                nc.vector.reduce_max(r8[:, :], k8[:, :, :], AX.X)
                dve.drain()
                nc.vector.tensor_copy(row[par][:, :, D + 2], prob[:, :])
                nc.vector.tensor_copy(p_all[:, bass.ds(QT * p, QT)], prob[:, :])
                nc.vector.tensor_copy(r_all[:, bass.ds(QT * p, QT)], r8[:, :])
                nc.vector.tensor_tensor(oh[:, :, :], c8[:, :, :], r8[:, :].rearrange("p (t o) -> p t o", o=1)
                                        .broadcast_to([P, QT, E]), ALU.is_equal)
                dve.drain().then_inc(oh_ready, 1)

            def places(u, p, par):
                wait_use(dve, u)
                psR = psM[u.bank]
                nc.vector.tensor_tensor(place[:, :, :], psR[0:P, 0:QT * E].rearrange("p (t e) -> p t e", e=E),
                                        run[:, :].rearrange("p (o e) -> p o e", o=1).broadcast_to([P, QT, E]), ALU.add)
                dve.drain()
                nc.vector.tensor_tensor(run[:, :], run[:, :], psR[0:P, QT * E:QT * E + E], ALU.add)\
                    .then_inc(misc_free[u.bank], 1)
                nc.vector.tensor_tensor(place[:, :, :], place[:, :, :], oh[:, :, :], ALU.mult)
                dve.drain()
                nc.vector.reduce_sum(slotf[:, :], place[:, :, :], AX.X)
                dve.drain()
                nc.vector.tensor_copy(slot[par][:, :], slotf[:, :])
                dve.drain().then_inc(row_ready, 1)

            for b in range(2):
                if b == 1:
                    dve.wait_ge(xn_ready, 1)
                ln1_stats(b, b)
            for k in range(LEAD):
                maximum(0, 0, 2 * k)
                maximum(0, 0, 2 * k + 1)
                if k == 5:
                    split_shift(0, 0, 0)

            def body(b, par, tail, ln, prep):
                n, p = b + 1, b - 1
                q = 1 - par

                def at(name):
                    return use(b, name, tail, ln, prep)
                for i in range(SLOTS):
                    k = i + LEAD
                    if k < SLOTS:
                        maximum(b, par, 2 * k)
                        maximum(b, par, 2 * k + 1)
                    elif prep:
                        maximum(n, q, 2 * (k - SLOTS))
                        maximum(n, q, 2 * (k - SLOTS) + 1)
                    if i == 1:
                        split_shift(b, par, 1)
                    if i == 2 and tail:
                        normalise(p, q, 2, at("N2"))
                    if i == 5 and ln:
                        ln1_stats(b + 2, par)
                    if i == 6 and tail:
                        residual(at("OUT0"), 0, p, q)
                    if i == 7:
                        split_shift(b, par, 2)
                        if tail:
                            residual(at("OUT1"), 1, p, q)
                            ln2_stats(p, q)
                    if i == 8:
                        normalise(b, par, 0, at("N0"))
                    if i == 10 and tail:
                        ln2_columns(p, q)
                    if i == 13:
                        if prep:
                            split_shift(n, q, 0)
                        if tail:
                            logits(at("LG"), p)
                    if i == 14:
                        normalise(b, par, 1, at("N1"))
                    if i == 15 and tail:
                        route(p, q)
                    if i == 17 and tail:
                        places(at("RK"), p, q)

            def final(b, par):
                p, q = b - 1, 1 - par
                normalise(p, q, 2, use(b, "N2"))
                residual(use(b, "OUT0"), 0, p, q)
                residual(use(b, "OUT1"), 1, p, q)
                ln2_stats(p, q)
                ln2_columns(p, q)
                logits(use(b, "LG"), p)
                route(p, q)
                places(use(b, "RK"), p, q)
            bodies(dve, body, final)
            dve.drain().then_inc(finished, 1)

        @block.gpsimd
        def _(pool):
            pool.wait_ge(prepared, 2)

            def root(b, m, ve, rs, nmr, ready, done):
                pool.wait_ge(ready, b + 1)
                nc.gpsimd.tensor_tensor(rs[:, :], ve[:, :], mhalf[:, :], ALU.pow)
                pool.drain()
                nc.gpsimd.tensor_tensor(nmr[:, :], m[:, :], rs[:, :], ALU.mult).then_inc(done, 1)

            def split(n, at):
                for m, name in enumerate(("Q0", "Q1", "K0", "K1")):
                    pool.wait_ge(qk_hi, 4 * n + m + 1)
                    wait_copied(pool, at(name))
                    nc.gpsimd.tensor_tensor(qk_r[:, m, :], qk_f[:, m, :], parts[:, m, 0, :], ALU.subtract)\
                      .then_inc(res_done, 1)
                    pool.wait_ge(res_done, 4 * n + m + 1)
                    nc.gpsimd.tensor_tensor(parts[:, m, 1, :], qk_r[:, m, :], zeros[:, :], ALU.add).then_inc(mid_done, 1)
                    pool.wait_ge(mid_done, 4 * n + m + 1)
                    nc.gpsimd.tensor_tensor(parts[:, m, 2, :], qk_r[:, m, :], parts[:, m, 1, :], ALU.subtract)\
                      .then_inc(parts_ready, 1)

            pool.sem_inc(rows_free, 2)

            def release(p, par):
                pool.wait_ge(scattered[par], 24 * (p - par) + 48)
                pool.sem_inc(rows_free, 1)

            def scatter(p, par):
                pool.wait_ge(prepared, 2)
                pool.wait_ge(row_ready, p + 1)
                for t in range(QT):
                    pool.indirect_dma_start(xs, bass.IndirectOffsetOnAxis(ap=slot[par][:, t:t + 1], axis=0),
                                            row[par][:, t, :], None).then_inc(scattered[par], 16)
            one = (neg_mean, var_eps, rstd, neg_mr, var_ready, rstd_ready)
            two = (neg_mean2, var_eps2, rstd2, neg_mr2, var2_ready, rstd2_ready)
            root(0, *one)
            root(1, *one)
            split(0, lambda name: use("start", AFTER.index(name)))
            split(1, lambda name: use("start", len(AFTER) + 2 + AFTER.index(name)))

            def body(b, par, tail, ln, prep):
                if ln:
                    root(b + 2, *one)
                if tail:
                    root(b - 1, *two)
                if ln:
                    split(b + 2, lambda name: use(b, name, tail, ln, prep))
                if tail:
                    scatter(b - 1, 1 - par)
                    release(b - 1, 1 - par)

            def final(b, par):
                root(b - 1, *two)
                scatter(b - 1, 1 - par)
                release(b - 1, 1 - par)
            bodies(pool, body, final)


def experts(nc, N, PT, CAPR, NT, xs, p_d, r_d, cnt_d, start_in, tok_in, tile_in, lane_in, neg_in, ident_in,
            w1, b1, w2, b2, out):
    PP = N // PT
    capacity = int(1.25 * N / E)
    RING = 4
    with ExitStack() as ctx:
        def sb(name, shape, dt=fp32):
            return ctx.enter_context(nc.sbuf_tensor(name, shape, dt))

        def sem(name):
            return ctx.enter_context(nc.semaphore(name))

        def ps(name, shape):
            return ctx.enter_context(nc.psum_tensor(name, shape, fp32))

        w1_sb = sb("w1_sb", [KH + 1, 2, E * F])
        w2_sb = sb("w2_sb", [128, FC, E * D])
        b2_sb = sb("b2_sb", [1, E * D])
        ident, one_row = sb("identC", [128, 128]), sb("one_row", [1, 128])
        p_all, r_all, tok = sb("p_allC", [PP, PT]), sb("r_allC", [PP, PT]), sb("tok", [PP, PT])
        mine = sb("mine", [PP, E, PT])
        hit = sb("hit", [PP, E, PT])
        part = sb("part", [PP, E])
        ones = sb("onesC", [PP, 128])
        start, cnt = sb("start", [128, E]), sb("cnt", [128, E])
        thr, step, cand, ok = sb("thr", [128, E]), sb("step", [128, 1]), sb("cand", [128, E]), sb("ok", [128, E])
        room, last_tok = sb("room", [128, E]), sb("last_tok", [128, E])
        tiles_f, tiles_i = sb("tiles_f", [128, E]), sb("tiles_i", [128, E], i32)
        first, end = sb("first", [128, E]), sb("end", [128, E])
        tile_no, lane, eno = sb("tile_no", [128, NT]), sb("lane", [128, 1]), sb("eno", [128, E])
        own, tmp, off = sb("own", [128, E, NT]), sb("tmp", [128, E, NT]), sb("off", [128, E, NT])
        t_base, t_exp, t_valid = sb("t_base", [128, NT]), sb("t_exp", [128, NT]), sb("t_valid", [128, NT])
        t_thr, t_last, t_used = sb("t_thr", [128, NT]), sb("t_last", [128, NT]), sb("t_used", [128, NT])
        base_i, exp_i = sb("base_i", [1, NT], i32), sb("exp_i", [1, NT], i32)
        zero_rows = sb("zero_rows", [128, RW])
        tail_f, tail_i = sb("tail_f", [128, E]), sb("tail_i", [128, E], i32)
        row = [sb(f"rowC{i}", [128, RW]) for i in range(RING)]
        xf = [sb(f"xfC{i}", [128, D]) for i in range(RING)]
        xfT = [sb(f"xfTC{i}", [KH + 1, 2, 128]) for i in range(2)]
        hid = [sb(f"hid{i}", [128, F]) for i in range(2)]
        hidT = [sb(f"hidT{i}", [128, F]) for i in range(2)]
        over, tie, low, keep, kp, dp, val, idm = (sb(n, [128, 1]) for n in
                                                   ("over", "tie", "low", "keep", "kp", "dp", "val", "idm"))
        pre = sb("pre", [128, D])
        res = [sb(f"res{i}", [128, D]) for i in range(RING)]
        dest = [sb(f"dest{i}", [128, 1], i32) for i in range(RING)]
        psC = ps("psC", [128, 512])
        psX, psH, psT = ps("psX", [128, 512]), ps("psH", [128, 2, 512]), ps("psTr", [128, 2, 512])
        psY = [ps(f"psY{i}", [128, 512]) for i in range(2)]

        small_loaded, weights_loaded, cleared = sem("small_loaded"), sem("weights_loaded"), sem("cleared")
        counted, totalled, tails_ready, tails_done, tables = (sem("counted"), sem("totalled"), sem("tails_ready"),
                                                               sem("tails_done"), sem("tables"))
        row_loaded = [sem(f"row_loaded{i}") for i in range(RING)]
        x_ready, x_tr, x_copied = sem("x_ready"), sem("x_tr"), sem("x_copied")
        h_ready, geluped = sem("h_ready"), sem("gelued")
        ht_ready, ht_dve, ht_act = sem("ht_ready"), sem("ht_dve"), sem("ht_act")
        y_ready, combined, dest_ready, out_free = sem("y_ready"), sem("combined"), sem("dest_ready"), sem("out_free")
        rows_seen = sem("rows_seen")
        scat = [sem(f"scat{i}") for i in range(RING)]
        block = ctx.enter_context(nc.Block())
        NSMALL = 10

        @block.sync
        def _(sp):
            for dst, src in ((p_all[:, :], p_d), (r_all[:, :], r_d), (tok[:, :], tok_in),
                             (start[:, :], start_in), (cnt[:, :], cnt_d[0:1, :].broadcast_to([128, E])),
                             (tile_no[:, :], tile_in), (lane[:, :], lane_in), (eno[:, :], neg_in),
                             (ident[:, :], ident_in), (b2_sb[:, :], b2.rearrange("e d -> (e d)").rearrange("(o n) -> o n", o=1))):
                sp.dma_start(dst, src).then_inc(small_loaded, 16)
            for c in range(2):
                sp.dma_start(w1_sb[0:KH, c, :].rearrange("k (e f) -> k e f", e=E),
                             w1[:, KH * c:KH * c + KH, :].rearrange("e k f -> k e f")).then_inc(weights_loaded, 16)
            sp.dma_start(w1_sb[KH:KH + 1, 1, :], b1.rearrange("e f -> (e f)").rearrange("(o n) -> o n", o=1))\
              .then_inc(weights_loaded, 16)
            for e in range(E):
                sp.dma_start(w2_sb[:, :, D * e:D * e + D], w2[e].rearrange("(c p) n -> p c n", p=128))\
                  .then_inc(weights_loaded, 16)
            sp.wait_ge(tables, 1)
            sp.wait_ge(tails_done, 16 * (E + 1))

            def load(t, r):
                base = sp.value_load(base_i[0:1, bass.ds(t, 1)], min_val=0, max_val=E * CAPR)
                sp.dma_start(row[r][:, :], xs[bass.ds(base, 128), :]).then_inc(row_loaded[r], 16)
            for r in range(RING):
                load(r, r)
            with sp.Fori(0, NT // RING - 1, 1) as k:
                for r in range(RING):
                    sp.wait_ge(tables, 1)
                    sp.wait_ge(combined, RING * k + r + 1)
                    load(RING * k + r + RING, r)

        @block.tensor
        def _(pe):
            pe.wait_ge(cleared, 1)
            pe.wait_ge(small_loaded, 16 * NSMALL)

            def total(i):
                pe.wait_ge(counted, i + 1)
                nc.tensor.matmul(psC[:, 0:E], ones[:, :], part[:, :], start=True, stop=True).then_inc(totalled, 1)
            with pe.Fori(0, 27, 1) as i:
                total(i)
            total(27)
            with pe.Fori(28, 43, 1) as i:
                total(i)
            pe.wait_ge(weights_loaded, 16 * 11)
            pe.wait_ge(tables, 1)

            def x_transpose(t, r):
                pe.wait_ge(x_ready, t + 1)
                pe.wait_ge(x_copied, t + 1)
                for c in range(2):
                    last = nc.tensor.transpose(psX[0:KH, 128 * c:128 * c + 128], xf[r][:, KH * c:KH * c + KH], ident[:, :])
                last.then_inc(x_tr, 1)

            def first_layer(t, r):
                e = pe.value_load(exp_i[0:1, bass.ds(t, 1)], min_val=0, max_val=E - 1)
                pe.wait_ge(x_copied, t + 2)
                pe.wait_ge(geluped, t + 1)
                for n in range(2):
                    for c in range(2):
                        last = nc.tensor.matmul(psH[:, n, 0:F // 2], xfT[r % 2][0:KH + c, c, :],
                                                w1_sb[0:KH + c, c, bass.ds(e * F + n * (F // 2), F // 2)],
                                                start=(c == 0), stop=(c == 1))
                last.then_inc(h_ready, 1)

            def hid_transpose(t, r):
                pe.wait_ge(geluped, t + 2)
                pe.wait_ge(ht_dve, t + 1)
                pe.wait_ge(ht_act, t + 1)
                for f in range(FC):
                    last = nc.tensor.transpose(psT[:, f // 3, 128 * (f % 3):128 * (f % 3) + 128],
                                               hid[r % 2][:, 128 * f:128 * f + 128], ident[:, :])
                last.then_inc(ht_ready, 1)

            def second_layer(t, r):
                e = pe.value_load(exp_i[0:1, bass.ds(t, 1)], min_val=0, max_val=E - 1)
                pe.wait_ge(ht_dve, t + 2)
                pe.wait_ge(ht_act, t + 2)
                for f in range(FC):
                    nc.tensor.matmul(psY[r % 2][:, 0:D], hidT[r % 2][:, 128 * f:128 * f + 128],
                                     w2_sb[:, f, bass.ds(e * D, D)], start=(f == 0), stop=False)
                nc.tensor.matmul(psY[r % 2][:, 0:D], one_row[:, :], b2_sb[:, bass.ds(e * D, D)], start=False, stop=True)\
                  .then_inc(y_ready, 1)
            x_transpose(0, 0)
            first_layer(0, 0)
            x_transpose(1, 1)
            with pe.Fori(0, NT // RING - 1, 1) as k:
                for r in range(RING):
                    t = RING * k + r
                    first_layer(t + 1, (r + 1) % RING)
                    hid_transpose(t, r)
                    x_transpose(t + 2, (r + 2) % RING)
                    second_layer(t, r)
            for t in range(NT - RING, NT):
                r = t % RING
                if t + 1 < NT:
                    first_layer(t + 1, (r + 1) % RING)
                hid_transpose(t, r)
                if t + 2 < NT:
                    x_transpose(t + 2, (r + 2) % RING)
                second_layer(t, r)

        @block.scalar
        def _(act):
            act.sem_inc(x_copied, 1)
            act.sem_inc(geluped, 1)
            act.sem_inc(ht_act, 1)
            act.wait_ge(cleared, 1)

            def x_copy(t, r):
                act.wait_ge(x_tr, t + 1)
                nc.scalar.activation(xfT[r % 2][0:KH, :, :], psX[0:KH, 0:256].rearrange("p (c n) -> p c n", c=2), ACT.Copy)\
                  .then_inc(x_copied, 1)

            def gelu(t, r):
                act.wait_ge(h_ready, t + 1)
                nc.scalar.activation(hid[r % 2][:, :].rearrange("p (n f) -> p n f", n=2), psH[:, :, 0:F // 2], ACT.Gelu)\
                   .then_inc(geluped, 1)

            def hid_copy(t, r):
                act.wait_ge(ht_ready, t + 1)
                nc.scalar.activation(hidT[r % 2][:, 384:768], psT[:, 1, 0:384], ACT.Copy).then_inc(ht_act, 1)
            x_copy(0, 0)
            gelu(0, 0)
            x_copy(1, 1)
            with act.Fori(0, NT // RING - 1, 1) as k:
                for r in range(RING):
                    t = RING * k + r
                    gelu(t + 1, r + 1)
                    hid_copy(t, r)
                    x_copy(t + 2, r + 2)
            for t in range(NT - RING, NT):
                if t + 1 < NT:
                    gelu(t + 1, t + 1)
                hid_copy(t, t)
                if t + 2 < NT:
                    x_copy(t + 2, t)

        @block.vector
        def _(dve):
            nc.vector.memset(one_row[:, :], 1.0)
            nc.vector.memset(ones[:, :], 1.0)
            nc.vector.memset(zero_rows[:, :], 0.0)
            nc.vector.memset(thr[:, :], 0.0)
            nc.vector.memset(last_tok[:, :], 0.0)
            nc.vector.memset(step[:, :], 0.5)
            for i in range(2):
                nc.vector.memset(xfT[i][KH:KH + 1, 1, :], 1.0)
            dve.drain().then_inc(cleared, 1)
            dve.sem_inc(ht_dve, 1)
            dve.wait_ge(small_loaded, 16 * NSMALL)

            def bc(a, n=NT):
                return a[:, :].rearrange("p (e o) -> p e o", o=1).broadcast_to([a.shape[0], E, n])

            def bt(a):
                return a[:, :].rearrange("p (o n) -> p o n", o=1).broadcast_to([128, E, NT])
            tt, ts = nc.vector.tensor_tensor, nc.vector.tensor_scalar
            ts(tail_f[:, :], cnt[:, :], lane[:, 0:1], None, ALU.add)
            tt(cnt[:, :], cnt[:, :], start[:, :], ALU.subtract)
            dve.drain()
            nc.vector.tensor_copy(tail_i[:, :], tail_f[:, :])
            dve.drain().then_inc(tails_ready, 1)
            ts(tiles_f[:, :], cnt[:, :], 1.0 / 128, 127.0 / 128 - 0.498, ALU.mult, ALU.add)
            dve.drain()
            nc.vector.tensor_copy(tiles_i[:, :], tiles_f[:, :])
            dve.drain()
            nc.vector.tensor_copy(end[:, :], tiles_i[:, :])
            dve.drain()
            for e in range(1, E):
                tt(end[:, e:e + 1], end[:, e:e + 1], end[:, e - 1:e], ALU.add)
                dve.drain()
            tt(first[:, :], end[:, :], tiles_i[:, :], ALU.subtract)
            dve.drain()
            tt(own[:, :, :], bt(tile_no), bc(first), ALU.is_ge)
            tt(tmp[:, :, :], bt(tile_no), bc(end), ALU.is_ge)
            tt(off[:, :, :], bt(tile_no), bc(first), ALU.subtract)
            dve.drain()
            tt(own[:, :, :], own[:, :, :], tmp[:, :, :], ALU.subtract)
            ts(off[:, :, :], off[:, :, :], 128.0, None, ALU.mult)
            dve.drain()

            def table(dst, value):
                tt(tmp[:, :, :], own[:, :, :], value, ALU.mult)
                dve.drain()
                nc.vector.reduce_sum(dst[:, :], tmp[:, :, :].rearrange("p e n -> p n e"), AX.X)
                dve.drain()
            nc.vector.reduce_sum(t_used[:, :], own[:, :, :].rearrange("p e n -> p n e"), AX.X)
            table(t_exp, bc(eno))
            table(t_base, bc(start))
            table(t_valid, off[:, :, :])
            tt(t_base[:, :], t_base[:, :], t_valid[:, :], ALU.add)
            ts(t_used[:, :], t_used[:, :], -float(E * CAPR), float(E * CAPR), ALU.mult, ALU.add)
            dve.drain()
            tt(t_base[:, :], t_base[:, :], t_used[:, :], ALU.add)
            dve.drain()
            nc.vector.tensor_copy(base_i[:, :], t_base[0:1, :])
            nc.vector.tensor_copy(exp_i[:, :], t_exp[0:1, :])
            dve.drain().then_inc(tables, 1)
            tt(off[:, :, :], bc(cnt), off[:, :, :], ALU.subtract)
            dve.drain()
            table(t_valid, off[:, :, :])
            for e in range(E):
                nc.vector.scalar_tensor_tensor(out=mine[:, e, :], in0=r_all[:, :], scalar=float(E - e), in1=p_all[:, :],
                                               op0=ALU.is_equal, op1=ALU.mult)
            dve.drain()

            def count(i, than, op):
                tt(hit[:, :, :], mine[:, :, :], than[0:PP, :].rearrange("p (e o) -> p e o", o=1).broadcast_to([PP, E, PT]), op)
                dve.drain()
                nc.vector.reduce_sum(part[:, :], hit[:, :, :], AX.X).then_inc(counted, 1)
                dve.wait_ge(totalled, i + 1)
            with dve.Fori(0, 27, 1) as i:
                ts(cand[:, :], thr[:, :], step[:, 0:1], None, ALU.add)
                dve.drain()
                count(i, cand, ALU.is_ge)
                ts(ok[:, :], psC[:, 0:E], float(capacity), None, ALU.is_ge)
                dve.drain()
                nc.vector.scalar_tensor_tensor(out=thr[:, :], in0=ok[:, :], scalar=step[:, 0:1], in1=thr[:, :],
                                               op0=ALU.mult, op1=ALU.add)
                dve.drain()
                ts(step[:, :], step[:, :], 0.5, None, ALU.mult)
                dve.drain()
            count(27, thr, ALU.is_gt)
            ts(room[:, :], psC[:, 0:E], -1.0, float(capacity), ALU.mult, ALU.add)
            tt(hit[:, :, :], mine[:, :, :], thr[0:PP, :].rearrange("p (e o) -> p e o", o=1).broadcast_to([PP, E, PT]),
               ALU.not_equal)
            dve.drain()
            ts(hit[:, :, :], hit[:, :, :], 2.0 ** 20, None, ALU.mult)
            nc.vector.memset(step[:, :], 2.0 ** 14)
            dve.drain()
            tt(mine[:, :, :], hit[:, :, :], tok[:, :].rearrange("p (o n) -> p o n", o=1).broadcast_to([PP, E, PT]), ALU.add)
            dve.drain()
            with dve.Fori(28, 43, 1) as i:
                ts(cand[:, :], last_tok[:, :], step[:, 0:1], None, ALU.add)
                dve.drain()
                count(i, cand, ALU.is_lt)
                tt(ok[:, :], psC[:, 0:E], room[:, :], ALU.is_le)
                dve.drain()
                nc.vector.scalar_tensor_tensor(out=last_tok[:, :], in0=ok[:, :], scalar=step[:, 0:1], in1=last_tok[:, :],
                                               op0=ALU.mult, op1=ALU.add)
                dve.drain()
                ts(step[:, :], step[:, :], 0.5, None, ALU.mult)
                dve.drain()
            table(t_thr, bc(thr))
            table(t_last, bc(last_tok))

            def normalise(t, r, rounds):
                dve.wait_ge(row_loaded[r], rounds)
                ts(xf[r][:, :], row[r][:, 0:D], row[r][:, D + 1:D + 2], row[r][:, D:D + 1], ALU.subtract, ALU.mult)\
                    .then_inc(x_ready, 1)

            def decide(t, r):
                p, tk = row[r][:, D + 2:D + 3], row[r][:, D + 3:D + 4]
                col = bass.ds(t, 1)
                tt(over[:, :], p, t_thr[:, col], ALU.is_gt)
                tt(tie[:, :], p, t_thr[:, col], ALU.is_equal)
                tt(low[:, :], tk, t_last[:, col], ALU.is_lt)
                tt(val[:, :], lane[:, :], t_valid[:, col], ALU.is_lt)
                dve.drain()
                tt(tie[:, :], tie[:, :], low[:, :], ALU.mult)
                nc.vector.scalar_tensor_tensor(out=idm[:, :], in0=tk, scalar=-float(NOWHERE), in1=val[:, :],
                                               op0=ALU.add, op1=ALU.mult)
                dve.drain()
                tt(keep[:, :], over[:, :], tie[:, :], ALU.max)
                dve.wait_ge(out_free, t + 1)
                ts(dest[r][:, :], idm[:, :], float(NOWHERE), None, ALU.add)
                dve.drain()
                tt(kp[:, :], keep[:, :], p, ALU.mult)
                dve.drain()
                tt(dp[:, :], p, kp[:, :], ALU.subtract)
                dve.drain()
                nc.vector.scalar_tensor_tensor(out=pre[:, :], in0=xf[r][:, :], scalar=dp[:, 0:1], in1=row[r][:, 0:D],
                                               op0=ALU.mult, op1=ALU.add)
                dve.drain()

            def hid_copy(t, r):
                dve.wait_ge(ht_ready, t + 1)
                nc.vector.tensor_copy(hidT[r % 2][:, 0:384], psT[:, 0, 0:384]).then_inc(ht_dve, 1)

            def combine(t, r):
                dve.wait_ge(y_ready, t + 1)
                nc.vector.scalar_tensor_tensor(out=res[r][:, :], in0=psY[r % 2][:, 0:D], scalar=kp[:, 0:1], in1=pre[:, :],
                                               op0=ALU.mult, op1=ALU.add).then_inc(combined, 1)
                dve.drain()
            for t in range(2):
                normalise(t, t, 16)
            with dve.Fori(0, NT // RING - 1, 1) as k:
                for r in range(RING):
                    t = RING * k + r
                    hid_copy(t, r)
                    normalise(t + 2, (r + 2) % RING, 16 * k + (16 if r < 2 else 32))
                    decide(t, r)
                    combine(t, r)
            for t in range(NT - RING, NT):
                r = t % RING
                hid_copy(t, r)
                if t + 2 < NT:
                    normalise(t + 2, (r + 2) % RING, 16 * (NT // RING))
                decide(t, r)
                combine(t, r)

        @block.gpsimd
        def _(pool):
            pool.sem_inc(out_free, 4)
            pool.wait_ge(tails_ready, 1)
            pool.dma_start(xs[E * CAPR:E * CAPR + 128, :], zero_rows[:, :]).then_inc(tails_done, 16)
            for e in range(E):
                pool.indirect_dma_start(xs, bass.IndirectOffsetOnAxis(ap=tail_i[:, e:e + 1], axis=0),
                                        zero_rows[:, :], None).then_inc(tails_done, 16)

            def write(t, r, done):
                pool.wait_ge(combined, t + 1)
                pool.sem_inc(rows_seen, 1)
                pool.indirect_dma_start(out, bass.IndirectOffsetOnAxis(ap=dest[r][:, 0:1], axis=0), res[r][:, :], None,
                                        bounds_check=N - 1, oob_is_err=False).then_inc(scat[r], 16)
                pool.wait_ge(scat[r], done)
                pool.sem_inc(out_free, 1)
            with pool.Fori(0, NT // RING, 1) as k:
                for r in range(RING):
                    write(RING * k + r, r, 16 * k + 16)


ROWS_PER_EXPERT = BATCH * NTOK + 128
TILES = -(-BATCH * NTOK // 128) + E
TILES += -TILES % 4


def _constants():
    place = np.arange(TXT, dtype=np.float32)[:, None]
    dim = np.arange(D, dtype=np.float32)[None, :]
    angle = place / np.power(np.float32(10000.0), np.floor(dim / 2) * 2 / np.float32(D)).astype(np.float32)
    here = np.arange(NTOK).reshape(QT, P).T
    outside = np.where(here < TXT, here + NIMG, here - TXT)
    tok = outside[:, None, :] + NTOK * np.arange(BATCH)[None, :, None]
    start = np.arange(E, dtype=np.float32) * ROWS_PER_EXPERT

    def on(a, n):
        return np.ascontiguousarray(np.broadcast_to(a, (n,) + a.shape)).astype(np.float32)
    return {
        "pos": np.where(np.arange(D) % 2 == 0, np.sin(angle), np.cos(angle)).astype(np.float32),
        "ident": np.eye(128, dtype=np.float32),
        "before": np.triu(np.ones((P, P), np.float32), 1),
        "c8": on(np.broadcast_to(E - np.arange(E, dtype=np.float32), (QT, E)), P),
        "tok": tok.reshape(P, BATCH * QT).astype(np.float32),
        "start": on(start, 128),
        "tile_no": on(np.arange(TILES), 128),
        "lane": np.arange(128, dtype=np.float32)[:, None].copy(),
        "expert_no": on(np.arange(E), 128),
    }


def build(nc, t, out):
    def scratch(name, shape, dt=fp32):
        return nc.dram_tensor(name, shape, dt, kind="Internal").ap()
    h = scratch("h_rows", (BATCH, NTOK, D))
    xs = scratch("routed_rows", (E * ROWS_PER_EXPERT + 128, RW))
    stack = scratch("qk_parts", (2, 3, 2, D, NTOK), bf16)
    p_all, r_all = scratch("p_rows", (P, BATCH * QT)), scratch("r_rows", (P, BATCH * QT))
    counts = scratch("counts", (P, E))
    patch_embed(nc, t["x"], t["L0_tok_W"], t["L0_tok_b"], t["x_txt"], t["mask_BS_i2_0"], t["L0_txt_token_table"],
                t["L0_txt_segm_table"], t["pos"], t["ident"], h)
    attention(nc, BATCH, h, t["L0_attn_w_qkv"], t["L0_attn_b_qkv"], t["L0_attn_w_out"], t["L0_attn_b_out"],
              t["L0_ffn_switch_w"], t["L0_ffn_switch_b"], t["ident"], t["before"], t["c8"],
              t["tok"], t["start"][0:P, :], xs, stack, p_all, r_all, counts)
    experts(nc, BATCH * NTOK, BATCH * QT, ROWS_PER_EXPERT, TILES, xs, p_all, r_all, counts, t["start"], t["tok"],
            t["tile_no"], t["lane"], t["expert_no"], t["ident"], t["L0_ffn_w1"], t["L0_ffn_b1"], t["L0_ffn_w2"],
            t["L0_ffn_b2"], out)


def kernel(**inputs):
    import concourse.bacc as bacc
    from concourse.bass_utils import run_bass_kernel_spmd

    nc = bacc.Bacc("TRN2", target_bir_lowering=False, num_devices=1)
    laid = dict(inputs)
    for name in ("x_txt", "mask_BS_i2_0", "L0_attn_w_qkv", "L0_attn_w_out"):
        laid[name] = np.asarray(inputs[name]).T
    laid.update(_constants())
    arrays, tensors = {}, {}
    for name, a in laid.items():
        a = np.ascontiguousarray(a)
        arrays["in_" + name] = a
        tensors[name] = nc.dram_tensor("in_" + name, a.shape, mybir.dt.from_np(a.dtype), kind="ExternalInput").ap()
    out = nc.dram_tensor("out_rows", (BATCH * NTOK, D), fp32, kind="ExternalOutput").ap()
    build(nc, tensors, out)
    r = run_bass_kernel_spmd(nc, [arrays], core_ids=[0])
    return r.results[0]["out_rows"].reshape(BATCH, NTOK, D)
```

```python
import numpy as np
import concourse.bass as bass
from concourse import mybir
from contextlib import ExitStack

fp32 = mybir.dt.float32
bf16 = mybir.dt.bfloat16
i32 = mybir.dt.int32
ALU = mybir.AluOpType
ACT = mybir.ActivationFunctionType
AX = mybir.AxisListType

BATCH = 64
IMG = 224
PATCH = 16
GRID = IMG // PATCH
CH = 3
D = 192
TXT = 77
NIMG = GRID * GRID
NTOK = TXT + NIMG
GROUPS = 5
ROW = IMG * CH
SEG = PATCH * CH
KC = 6
TB = 4
HEADS, HD = 12, 16
QT = 3
P = NTOK // QT
KH = D // 2
GRP = 3
E = 8
RW = D + 4
LEAD = 10
SLOTS = 18
TAIL = ("N2", "ON0", "ON1", "OUT0", "OUT1", "X0", "X1", "LG", "RK")
NEXT = ("V0", "V1", "MT0")
AFTER = ("T0", "T1", "Q0", "Q1", "K0", "K1")
USES = {0: ("V0",), 1: ("V1",), 2: ("MT1",), 3: ("N2",), 4: ("ON0", "ON1"), 5: ("T0", "T1"), 6: ("Q0", "OUT0"),
        7: ("Q1", "OUT1"), 8: ("MT2",), 9: ("N0", "K0"), 11: ("K1",), 12: ("X0", "X1"), 13: ("LG",), 14: ("MT0",),
        15: ("N1",), 16: ("RK",)}
MISC = tuple(name for i in sorted(USES) for name in USES[i])
START = AFTER + ("V0", "V1") + AFTER + ("MT0",)
F = 768
FC = F // 128
NOWHERE = 1000000
P_STEPS = 27
T_STEPS = 15


def patch_embed(nc, x, W, tok_b, idx_tok, idx_seg, tok_table, seg_table, pos, ident_in, h):
    half = 64
    tile_units = GRID
    with ExitStack() as ctx:
        def sb(name, shape, dt=fp32):
            return ctx.enter_context(nc.sbuf_tensor(name, shape, dt))

        def sem(name):
            return ctx.enter_context(nc.semaphore(name))

        img = [sb(f"img{i}", [128, PATCH * ROW]) for i in range(2)]
        wraw = sb("wraw", [128, KC, GROUPS, D])
        wv = [[sb(f"w_{r}_{c}", [128, KC, D]) for c in ("all", "off")] for r in ("mid", "top", "bottom")]
        patch = [sb(f"patch{i}", [128, KC * 128]) for i in range(2)]
        patchT = [sb(f"patchT{i}", [128, KC, 128]) for i in range(2)]
        stage = [sb(f"stage{i}", [128, GRID, D]) for i in range(2)]
        bias = sb("tok_bias", [128, D])
        ident = sb("identA", [128, 128])
        psT = [ctx.enter_context(nc.psum_tensor(f"psT{i}", [128, 2, 512], fp32)) for i in range(2)]
        psO = [ctx.enter_context(nc.psum_tensor(f"psO{i}", [128, 512], fp32)) for i in range(2)]
        idx_all = [sb(f"idx_all{i}", [TXT, BATCH], i32) for i in range(2)]
        idx_f = [sb(f"idx_f{i}", [TXT, BATCH]) for i in range(2)]
        wrap = [sb(f"idx_wrapped{i}", [TXT, BATCH]) for i in range(2)]
        idx_now = [[sb(f"idx_now{i}{j}", [TXT, TB], i32) for j in range(2)] for i in range(2)]
        tok_rows = [sb(f"tok_rows{i}", [TXT, TB, D]) for i in range(2)]
        seg_rows = [sb(f"seg_rows{i}", [TXT, TB, D]) for i in range(2)]
        txt_sum = [sb(f"txt_sum{i}", [TXT, TB, D]) for i in range(2)]
        pos_sb = sb("pos_sb", [TXT, D])

        w_loaded, const_loaded, w_ready = sem("w_loaded"), sem("const_loaded"), sem("w_ready")
        img_loaded = [sem(f"img_loaded{i}") for i in range(2)]
        ordered, transposed = sem("ordered"), sem("transposed")
        copied_dve, copied_act = sem("copied_dve"), sem("copied_act")
        embedded, staged = sem("embedded"), sem("staged")
        stored = [sem(f"stored{i}") for i in range(2)]
        txt_idx, idx_ready, with_pos, summed = sem("txt_idx"), sem("idx_ready"), sem("with_pos"), sem("summed")
        txt_got = [sem(f"txt_got{i}") for i in range(2)]
        txt_out = [sem(f"txt_out{i}") for i in range(2)]
        border_ready, idx_seen = sem("border_ready"), sem("idx_seen")
        block = ctx.enter_context(nc.Block())

        h_rows = h.rearrange("b t d -> b (t d)")

        def out_rows(gy):
            return h_rows[:, bass.ds((TXT + gy * GRID) * D, GRID * D)]

        x_rows = x.rearrange("b (gy r) w c -> gy b (r w c)", gy=GRID)

        @block.sync
        def _(sp):
            def load(par, gys):
                for i, gy in enumerate(gys):
                    for q in range(2):
                        n = PATCH * ROW // 2
                        src = x_rows[bass.ds(gy, 1), :, q * n:(q + 1) * n].rearrange("o b n -> (o b) n")
                        sp.dma_start(img[par][i * half:(i + 1) * half, q * n:(q + 1) * n], src)\
                          .then_inc(img_loaded[par], 16)

            def store(par, gys):
                for i, gy in enumerate(gys):
                    sp.dma_start(out_rows(gy), stage[par][i * half:(i + 1) * half, :, :]
                                 .rearrange("p g d -> p (g d)")).then_inc(stored[par], 16)

            load(0, (1, 2))
            sp.wait_ge(w_loaded, 16 * KC)
            load(1, (3, 4))
            with sp.Fori(0, 2, 1) as pair:
                k = 2 * pair
                for par in range(2):
                    sp.wait_ge(w_ready, 1)
                    sp.wait_ge(ordered, (k + par) * tile_units + tile_units)
                    load(par, (2 * k + 2 * par + 5, 2 * k + 2 * par + 6))
                    sp.wait_ge(w_ready, 1)
                    sp.wait_ge(staged, (k + par) * tile_units + tile_units + 2)
                    store(par, (2 * k + 2 * par + 1, 2 * k + 2 * par + 2))
            sp.wait_ge(ordered, 5 * tile_units)
            load(0, (0, GRID - 1))
            sp.wait_ge(staged, 5 * tile_units + 2)
            store(0, (9, 10))
            sp.wait_ge(staged, 6 * tile_units + 2)
            store(1, (11, 12))
            sp.wait_ge(staged, 7 * tile_units + 2)
            store(0, (0, GRID - 1))
            sp.wait_ge(stored[0], 4 * 32 + 32)
            sp.wait_ge(stored[1], 3 * 32 + 32)

        @block.scalar
        def _(act):
            act.dma_start(ident[:, :], ident_in).then_inc(const_loaded, 16)
            act.dma_start(bias[:, :], tok_b.rearrange("(o n) -> o n", o=1).broadcast_to([128, D]))\
               .then_inc(const_loaded, 16)
            wrows = W.rearrange("(py s e g c) n -> s c py e g n", py=PATCH, s=2, g=GROUPS, c=CH)
            for k in range(KC):
                act.dma_start(wraw[:, k, :, :], wrows[k // CH, k % CH]).then_inc(w_loaded, 16)
            act.sem_inc(copied_act, 2)

            def copies(u0, n):
                for i in range(n):
                    act.wait_ge(transposed, u0 + i + 3)
                    act.wait_ge(embedded, u0 + i + 1)
                    nc.scalar.activation(patchT[i % 2][:, 3:6, :].rearrange("p k n -> p (k n)"),
                                         psT[i % 2][:, 1, 0:384], ACT.Copy).then_inc(copied_act, 1)
            with act.Fori(0, 3, 1) as pair:
                k = 2 * pair
                copies(k * tile_units, 2 * tile_units)
            copies(6 * tile_units, tile_units)

        @block.tensor
        def _(pe):
            pe.wait_ge(const_loaded, 32)
            pe.sem_inc(embedded, 2)
            pe.sem_inc(transposed, 2)

            def embed(par, u0, border=False):
                def transposes(g):
                    u = u0 + g
                    pe.wait_ge(ordered, u + 1)
                    pe.wait_ge(copied_dve, u + 1)
                    pe.wait_ge(copied_act, u + 1)
                    for k in range(KC):
                        last = nc.tensor.transpose(psT[g % 2][:, k // 3, (k % 3) * 128:(k % 3) * 128 + 128],
                                                   patch[g % 2][:, k * 128:(k + 1) * 128], ident[:, :])
                    last.then_inc(transposed, 1)

                def product(g):
                    u = u0 + g
                    pe.wait_ge(copied_dve, u + 3)
                    pe.wait_ge(copied_act, u + 3)
                    pe.wait_ge(staged, u + 1)
                    for rows, m0, m1 in (((1, 0, half), (2, half, 128)) if border else ((0, 0, 128),)):
                        for k in range(KC):
                            off = (g == 0 and k < 3) or (g == GRID - 1 and k >= 3)
                            last = nc.tensor.matmul(psO[g % 2][m0:m1, 0:D], patchT[g % 2][:, k, m0:m1],
                                                    wv[rows][off][:, k, :], start=(k == 0), stop=(k == KC - 1))
                    last.then_inc(embedded, 1)
                transposes(0)
                for g in range(GRID):
                    if g + 1 < GRID:
                        transposes(g + 1)
                    if g == 0:
                        pe.wait_ge(w_ready, 1)
                    product(g)

            with pe.Fori(0, 3, 1) as pair:
                k = 2 * pair
                for par in range(2):
                    embed(par, k * tile_units + par * tile_units)
            pe.wait_ge(border_ready, 1)
            embed(0, 6 * tile_units, border=True)

        @block.vector
        def _(dve):
            dve.sem_inc(copied_dve, 2)
            dve.sem_inc(staged, 2)
            dve.sem_inc(stored[0], 32)
            dve.sem_inc(stored[1], 32)
            dve.wait_ge(w_loaded, 16 * KC)

            every, left, right = slice(0, KC), slice(0, 3), slice(3, KC)
            for dst, groups, chunks in ((wv[0][0], (0, 1, 2, 3, 4), every), (wv[0][1], (0, 1, 2), left),
                                        (wv[0][1], (0, 3, 4), right)):
                src = [wraw[:, chunks, g, :] for g in groups]
                nc.vector.tensor_tensor(dst[:, chunks, :], src[0], src[1], ALU.add)
                for later in src[2:]:
                    dve.drain()
                    nc.vector.tensor_tensor(dst[:, chunks, :], dst[:, chunks, :], later, ALU.add)
            dve.drain().then_inc(w_ready, 1)
            dve.wait_ge(const_loaded, 32)

            def order(par, u0, g):
                dve.wait_ge(transposed, u0 + g + 1)
                src = img[par][:, :].rearrange("p (r n) -> p r n", r=PATCH)[:, :, g * SEG:(g + 1) * SEG]
                dst = patch[g % 2][:, :].rearrange("p (s c r e) -> p s c r e", s=2, c=CH, r=PATCH)
                src = src.rearrange("p r (s e c) -> p s c r e", s=2, c=CH)
                for side in range(2):
                    last = nc.vector.tensor_copy(dst[:, side], src[:, side])
                last.then_inc(ordered, 1)

            def tile(par, u0, stores, loads):
                def copy(g):
                    u = u0 + g
                    dve.wait_ge(transposed, u + 3)
                    dve.wait_ge(embedded, u + 1)
                    nc.vector.tensor_copy(patchT[g % 2][:, 0:3, :].rearrange("p k n -> p (k n)"),
                                          psT[g % 2][:, 0, 0:384]).then_inc(copied_dve, 1)
                dve.wait_ge(img_loaded[par], loads)
                order(par, u0, 0)
                order(par, u0, 1)
                copy(0)
                dve.wait_ge(stored[par], stores)
                for g in range(GRID):
                    if g + 1 < GRID:
                        copy(g + 1)
                    if g + 2 < GRID:
                        order(par, u0, g + 2)
                    dve.wait_ge(embedded, u0 + g + 3)
                    nc.vector.tensor_tensor(stage[par][:, g, :], psO[g % 2][:, 0:D], bias[:, :], ALU.add)\
                      .then_inc(staged, 1)
            with dve.Fori(0, 3, 1) as pair:
                k = 2 * pair
                for par in range(2):
                    tile(par, k * tile_units + par * tile_units, k * 16 + 32, k * 32 + 64)
            tile(0, 6 * tile_units, 3 * 32 + 32, 4 * 64)

        @block.gpsimd
        def _(pool):
            pool.dma_start(idx_all[0][:, :], idx_tok).then_inc(txt_idx, 16)
            pool.dma_start(idx_all[1][:, :], idx_seg).then_inc(txt_idx, 16)
            pool.dma_start(pos_sb[:, :], pos).then_inc(txt_idx, 16)
            pool.wait_ge(txt_idx, 48)
            for i, size in enumerate((tok_table.shape[0], seg_table.shape[0])):
                nc.gpsimd.tensor_copy(idx_f[i][:, :], idx_all[i][:, :])
                pool.drain()
                nc.gpsimd.tensor_scalar(wrap[i][:, :], idx_f[i][:, :], 0.0, float(size), ALU.is_lt, ALU.mult)
                pool.drain()
                nc.gpsimd.tensor_tensor(wrap[i][:, :], wrap[i][:, :], idx_f[i][:, :], ALU.add)
                pool.drain()
                nc.gpsimd.tensor_scalar(wrap[i][:, :], wrap[i][:, :], 0.0, float(size - 1), ALU.max, ALU.min)
                pool.drain()

            def gather(n, par):
                pool.wait_ge(txt_idx, 48)
                for i in range(2):
                    nc.gpsimd.tensor_copy(idx_now[i][par][:, :], wrap[i][:, bass.ds(TB * n, TB)]).then_inc(idx_ready, 1)
                pool.wait_ge(txt_idx, 48)
                pool.wait_ge(idx_ready, 2 * n + 2)
                pool.sem_inc(idx_seen, 1)
                for j in range(TB):
                    for i, (table, rows) in enumerate(((tok_table, tok_rows), (seg_table, seg_rows))):
                        pool.indirect_dma_start(rows[par][:, j, :], None, table,
                                                bass.IndirectOffsetOnAxis(ap=idx_now[i][par][:, j:j + 1], axis=0))\
                            .then_inc(txt_got[par], 16)

            def add(n, par, half):
                pool.wait_ge(txt_idx, 48)
                pool.wait_ge(txt_got[par], 32 * TB * half + 32 * TB)
                nc.gpsimd.tensor_tensor(seg_rows[par][:, :, :], seg_rows[par][:, :, :],
                                        pos_sb[:, :].rearrange("p (o d) -> p o d", o=1).broadcast_to([TXT, TB, D]), ALU.add)\
                    .then_inc(with_pos, 1)
                pool.wait_ge(txt_idx, 48)
                pool.wait_ge(with_pos, n + 1)
                nc.gpsimd.tensor_tensor(txt_sum[par][:, :, :], seg_rows[par][:, :, :], tok_rows[par][:, :, :], ALU.add)\
                    .then_inc(summed, 1)
                pool.wait_ge(txt_idx, 48)
                pool.wait_ge(summed, n + 1)
                pool.dma_start(h[bass.ds(TB * n, TB), 0:TXT, :].rearrange("b t d -> t b d"), txt_sum[par][:, :, :])\
                    .then_inc(txt_out[par], 16)

            def stored_before(par, half):
                pool.wait_ge(txt_idx, 48)
                pool.wait_ge(txt_out[par], 16 * half)
            groups = BATCH // TB
            groups = BATCH // TB
            pool.wait_ge(w_loaded, 16 * KC)
            (top, top_off), (bot, bot_off) = wv[1:]
            every, left, right = slice(0, KC), slice(0, 3), slice(3, KC)
            up, down = (0, half), (half, 128)
            sums = [(top, (0, 1, 2, 3, 4), every, down), (top, (0, 1, 3), every, up),
                    (bot, (0, 1, 2, 3, 4), every, up), (bot, (0, 2, 4), every, down)]
            for side, g_mid, g_top, g_bot in ((left, (0, 1, 2), (0, 1), (0, 2)), (right, (0, 3, 4), (0, 3), (0, 4))):
                sums += [(top_off, g_mid, side, down), (top_off, g_top, side, up),
                         (bot_off, g_mid, side, up), (bot_off, g_bot, side, down)]
            for step in range(GROUPS - 1):
                for dst, groups_in, chunks, (p0, p1) in sums:
                    if step + 1 < len(groups_in):
                        out = dst[p0:p1, chunks, :]
                        so_far = wraw[p0:p1, chunks, groups_in[0], :] if step == 0 else out
                        nc.gpsimd.tensor_tensor(out, so_far, wraw[p0:p1, chunks, groups_in[step + 1], :], ALU.add)
                pool.drain()
            pool.sem_inc(border_ready, 1)
            gather(0, 0)
            gather(1, 1)
            for par in range(2):
                add(par, par, 0)
                gather(par + 2, par)
            with pool.Fori(1, groups // 2 - 1, 1) as pair:
                for par in range(2):
                    stored_before(par, pair)
                    add(2 * pair + par, par, pair)
                    gather(2 * pair + par + 2, par)
            for par in range(2):
                stored_before(par, groups // 2 - 1)
                add(groups - 2 + par, par, groups // 2 - 1)
            for par in range(2):
                pool.wait_ge(txt_out[par], 16 * (groups // 2))


def attention(nc, NB, h, wqkvT, bqkv, woT, bo, sw, swb, ident_in, tri_in, c8_in, tok_in, run_in,
              xs, stack, p_all_d, r_all_d, cnt_d):
    def listed(tail, ln, prep):
        return [m for m in MISC if (tail or m not in TAIL) and (ln or m not in AFTER) and (prep or m not in NEXT)]

    class Use:

        def __init__(self, base, turn, pos):
            fixed = base if isinstance(base, int) else 0
            self.before, self.bank = base + turn + pos, (fixed + turn + pos) % 2
            self.prior = (base + turn + pos) // 2 if isinstance(base, int) else base // 2 + (turn + pos) // 2

    def use(b, name, tail=True, ln=True, prep=True):
        if isinstance(b, str):
            return Use(0, 0, name)
        first = len(START)
        if isinstance(b, int):
            kinds = [(k > 0, k + 2 < NB, k + 1 < NB) for k in range(b)] + [(tail, ln, prep)]
            base = first + sum(len(listed(*k)) for k in kinds[:-1])
            names = TAIL if b == NB else listed(*kinds[-1])
            return Use(base, 0, list(names).index(name))
        u = Use(0, first + len(listed(False, True, True)), MISC.index(name))
        u.before, u.prior = u.before + len(MISC) * (b - 1), u.prior + len(MISC) // 2 * (b - 1)
        return u

    with ExitStack() as ctx:
        def sb(name, shape, dt=fp32):
            return ctx.enter_context(nc.sbuf_tensor(name, shape, dt))

        def sem(name):
            return ctx.enter_context(nc.semaphore(name))

        ident, identb = sb("identB", [128, 128]), sb("identb", [128, 128], bf16)
        w_qkv = sb("w_qkv", [128, 2, 3 * D])
        w_qk = sb("w_qk", [128, 2, 4, KH])
        w_out = sb("w_out", [128, 2, D])
        w_sw = sb("w_sw", [128, 2, E])
        tri, ones = sb("tri", [P, P]), sb("ones", [P, P])
        c8 = sb("c8", [P, QT, E])
        tok_all = sb("tok_all", [P, NB * QT])
        p_all, r_all = sb("p_all", [P, NB * QT]), sb("r_all", [P, NB * QT])
        h_in = [sb(f"h_in{i}", [P, QT, D]) for i in range(2)]
        h_res = [sb(f"h_res{i}", [P, QT, D]) for i in range(2)]
        stats, mv = sb("stats", [P, QT, 6]), sb("mv", [P, QT, 2])
        neg_mean, neg_mean2 = sb("neg_mean", [P, QT]), sb("neg_mean2", [P, QT])
        neg_mr, neg_mr2 = sb("neg_mr", [P, QT]), sb("neg_mr2", [P, QT])
        var_eps, rstd, mhalf = sb("var_eps", [P, QT]), sb("rstd", [P, QT]), sb("mhalf", [P, QT])
        xn = [sb(f"xn{i}", [P, QT, D]) for i in range(2)]
        xnT = sb("xnT", [128, 2, NTOK])
        qk_f = sb("qk_f", [KH, 4, NTOK])
        qk_r = sb("qk_r", [KH, 4, NTOK])
        parts = sb("parts", [KH, 4, 3, NTOK], bf16)
        Qs = [sb(f"Qs{i}", [128, HEADS, NTOK], bf16) for i in range(2)]
        Ks = [sb(f"Ks{i}", [128, HEADS, NTOK], bf16) for i in range(2)]
        V = [sb(f"V{i}", [128, QT, HEADS, 32]) for i in range(2)]
        neg_max = [sb(f"neg_max{i}", [P, QT, HEADS]) for i in range(2)]
        shift = sb("shift", [P, QT, 2, 4], bf16)
        mT = [sb(f"mT{i}", [8, NTOK], bf16) for i in range(GRP)]
        Pr = [sb(f"Pr{i}", [128, NTOK]) for i in range(12)]
        O_sb = [sb(f"O_sb{i}", [128, NTOK]) for i in range(2)]
        inv = sb("inv", [P, QT, 4])
        On = [sb(f"On{i}", [P, QT, D]) for i in range(2)]
        OnT = sb("OnT", [128, 2, NTOK])
        zeros = sb("zeros", [KH, NTOK])
        row = [sb(f"row{i}", [P, QT, RW]) for i in range(2)]
        stats2, mv2 = sb("stats2", [P, QT, 6]), sb("mv2", [P, QT, 2])
        var_eps2, rstd2 = sb("var_eps2", [P, QT]), sb("rstd2", [P, QT])
        xf = sb("xf", [P, QT, D])
        xfT = sb("xfT", [128, 2, NTOK])
        lmax, ls, ex = sb("lmax", [P, QT]), sb("ls", [P, QT, E]), sb("ex", [P, QT, E])
        esum, k8, oh = sb("esum", [P, QT]), sb("k8", [P, QT, E]), sb("oh", [P, QT + 1, E])
        run = sb("run", [P, E])
        place, slotf = sb("place", [P, QT, E]), sb("slotf", [P, QT])
        slot = [sb(f"slot{i}", [P, QT], i32) for i in range(2)]

        psS = [ctx.enter_context(nc.psum_tensor(f"psS{i}", [128, 512], fp32)) for i in range(3)]
        psE = [ctx.enter_context(nc.psum_tensor(f"psE{i}", [128, 512], fp32)) for i in range(2)]
        psO = ctx.enter_context(nc.psum_tensor("psAttn", [128, 512], fp32))
        psM = [ctx.enter_context(nc.psum_tensor(f"psM{i}", [128, 512], fp32)) for i in range(2)]

        weights_cleared, const_loaded, prepared = sem("weights_cleared"), sem("const_loadedB"), sem("prepared")
        h_loaded = [sem(f"h_loaded{i}") for i in range(2)]
        hres_loaded = [sem(f"hres_loaded{i}") for i in range(2)]
        var_ready, rstd_ready, xn_ready = sem("var_ready"), sem("rstd_ready"), sem("xn_ready")
        misc_ready, misc_free = sem("misc_ready"), [sem(f"misc_free{i}") for i in range(2)]
        qk_hi, res_done, mid_done, parts_ready = sem("qk_hi"), sem("res_done"), sem("mid_done"), sem("parts_ready")
        stack_stored, stack_loaded = sem("stack_stored"), sem("stack_loaded")
        scored, maxed, shift_ready = sem("scored"), sem("maxed"), sem("shift_ready")
        shifted, exped, weighted = sem("shifted"), sem("exped"), sem("weighted")
        o_read, o_ready = sem("o_read"), sem("o_ready")
        shift_loaded = [sem(f"shift_loaded{i}") for i in range(GRP)]
        var2_ready, rstd2_ready, xf_ready = sem("var2_ready"), sem("rstd2_ready"), sem("xf_ready")
        scale_ready, scale2_ready, columns_ready = sem("scale_ready"), sem("scale2_ready"), sem("columns_ready")
        rows_seen, padded = sem("rows_seenB"), sem("padded")
        h2_ready = sem("h2_ready")
        ls_ready, ex_ready, oh_ready, row_ready = sem("ls_ready"), sem("ex_ready"), sem("oh_ready"), sem("row_ready")
        rows_free = sem("rows_free")
        scattered = [sem(f"scattered{i}") for i in range(2)]
        finished, stacks_seen = sem("finishedB"), sem("stacks_seen")
        block = ctx.enter_context(nc.Block())
        h_v = h.rearrange("b (t p) d -> b p t d", p=P)

        def bodies(eng, body, final, first=1):
            def alone(b):
                body(b, b % 2, tail=b > 0, ln=b + 2 < NB, prep=b + 1 < NB)
            pairs = (NB - 3 - first) // 2
            for b in range(first):
                alone(b)
            with eng.Fori(0, pairs, 1) as pair:
                for b in (first, first + 1):
                    body(2 * pair + b, b % 2, tail=True, ln=True, prep=True)
            for b in range(first + 2 * pairs, NB):
                alone(b)
            final(NB, NB % 2)

        def wait_use(eng, u):
            eng.wait_ge(misc_ready, u.before + 1)

        def wait_copied(eng, u):
            eng.wait_ge(misc_free[u.bank], u.prior + 1)

        @block.sync
        def _(sp):
            def load_h(b, par):
                sp.dma_start(h_in[par][:, :, :], h_v[bass.ds(b, 1)].rearrange("o p t d -> (o p) t d"))\
                  .then_inc(h_loaded[par], 16)

            load_h(0, 0)
            load_h(1, 1)
            sp.wait_ge(weights_cleared, 1)
            for dst, src in ((w_qkv[0:KH, 0, :], wqkvT[0:KH, :]), (w_qkv[0:KH, 1, :], wqkvT[KH:D, :]),
                             (w_qkv[KH:KH + 1, 1, :], bqkv.rearrange("(o n) -> o n", o=1)),
                             (ident[:, :], ident_in), 
                             (tri[:, :], tri_in), (c8[:, :, :], c8_in), (tok_all[:, :], tok_in),
                             (run[:, :], run_in), (w_sw[0:KH, 0, :], sw[0:KH, :]), (w_sw[0:KH, 1, :], sw[KH:D, :]),
                             (w_sw[KH:KH + 1, 1, :], swb.rearrange("(o n) -> o n", o=1))):
                sp.dma_start(dst, src).then_inc(const_loaded, 16)
            for dst, src in ((w_out[0:KH, 0, :], woT[0:KH, :]), (w_out[0:KH, 1, :], woT[KH:D, :]),
                             (w_out[KH:KH + 1, 1, :], bo.rearrange("(o n) -> o n", o=1))):
                sp.dma_start(dst, src).then_inc(const_loaded, 16)

            def load_res(b, par):
                sp.dma_start(h_res[par][:, :, :], h_v[bass.ds(b, 1)].rearrange("o p t d -> (o p) t d"))\
                  .then_inc(hres_loaded[par], 16)

            def store_parts(n, par):
                for m in range(4):
                    sp.wait_ge(parts_ready, 4 * n + m + 1)
                    dst = stack[par, m].rearrange("s r n -> r s n")
                    sp.dma_start(dst, parts[:, m, :, :]).then_inc(stack_stored, 16)

            def load_stacks(n, par):
                sp.wait_ge(stack_stored, 64 * n + 64)
                for half in range(2):
                    for at, many, part in ((0, 3, 0), (3, 2, 1)):
                        src = stack[par, half, part:part + 1].rearrange("s (d h) n -> s d (h n)", d=HD)
                        sp.dma_start(Qs[par][HD * at:HD * (at + many), 6 * half:6 * half + 6, :]
                                     .rearrange("p h n -> p (h n)"), src.broadcast_to([many, HD, 6 * NTOK]))\
                          .then_inc(stack_loaded, 16)
                for kind, at, many, part in ((0, 5, 1, 2), (1, 0, 3, 0), (1, 3, 2, 0), (1, 5, 1, 0)):
                    src = stack[par, 2 * kind:2 * kind + 2, part:part + many].rearrange("a s (d h) n -> (s d) a (h n)", d=HD)
                    sp.dma_start((Qs, Ks)[kind][par][HD * at:HD * (at + many), :, :]
                                 .rearrange("p (a h) n -> p a (h n)", a=2), src).then_inc(stack_loaded, 16)

            def load_shift(b, par, g, u):
                wait_copied(sp, u)
                sp.dma_start(Qs[par][KH:KH + 2, 4 * g:4 * g + 4, :], mT[g][:, :]).then_inc(shift_loaded[g], 16)

            store_parts(0, 0)
            load_stacks(0, 0)
            sp.wait_ge(xn_ready, 1)
            load_h(2, 0)
            store_parts(1, 1)
            sp.wait_ge(padded, 1)
            load_shift(0, 0, 0, use("start", len(START) - 1))

            def body(b, par, tail, ln, prep):
                if prep:
                    if tail:
                        sp.wait_ge(shifted, 36 * b + 3)
                        sp.sem_inc(stacks_seen, 1)
                    load_stacks(b + 1, 1 - par)
                load_shift(b, par, 1, use(b, "MT1", tail, ln, prep))
                if not isinstance(b, int) or b + 3 < NB:
                    sp.wait_ge(xn_ready, b + 2)
                    load_h(b + 3, 1 - par)
                load_shift(b, par, 2, use(b, "MT2", tail, ln, prep))
                if tail:
                    sp.wait_ge(h2_ready, b)
                load_res(b, par)
                if prep:
                    load_shift(b + 1, 1 - par, 0, use(b, "MT0", tail, ln, prep))
                if ln:
                    store_parts(b + 2, par)
            bodies(sp, body, lambda b, par: None)
            sp.wait_ge(finished, 1)
            sp.dma_start(p_all_d, p_all[:, :]).then_inc(finished, 16)
            sp.dma_start(r_all_d, r_all[:, :]).then_inc(finished, 16)
            sp.dma_start(cnt_d, run[:, :]).then_inc(finished, 16)
            sp.wait_ge(finished, 49)
            sp.wait_ge(rows_free, NB + 2)

        @block.tensor
        def _(pe):
            pe.sem_inc(shifted, 3)
            pe.sem_inc(weighted, 3)
            pe.wait_ge(const_loaded, 16 * 14)
            pe.wait_ge(prepared, 3)

            def score(b, par, u):
                g, r = divmod(u, 12)
                qt, j = divmod(r, 4)
                hd = 4 * g + j
                pe.wait_ge(maxed, 36 * b + u + 1)
                nc.tensor.matmul(psS[u % 3][0:P, 0:NTOK], Qs[par][0:KH, hd, P * qt:P * qt + P], Ks[par][0:KH, hd, :],
                                 start=True, stop=True).then_inc(scored, 1)

            def shifted_score(b, par, u):
                g, r = divmod(u, 12)
                kt, j = divmod(r, 4)
                if r == 0:
                    pe.wait_ge(shift_loaded[g], 16 * b + 16)
                pe.wait_ge(exped, 36 * b + u + 1)
                nc.tensor.matmul(psE[u % 2][0:P, 0:NTOK], Ks[par][:, 4 * g + j, P * kt:P * kt + P],
                                 Qs[par][:, 4 * g + j, :], start=True, stop=True).then_inc(shifted, 1)

            def weigh(b, par, m):
                g, kt = divmod(m, 3)
                pe.wait_ge(exped, 36 * b + 4 * m + 6)
                if kt == 0:
                    pe.wait_ge(o_read, 3 * b + g + 1)
                for j in range(4):
                    last = nc.tensor.matmul(psO[32 * j:32 * j + 32, 0:NTOK], V[par][:, kt, 4 * g + j, :],
                                            Pr[(4 * m + j) % 12][:, :], start=(kt == 0), stop=(kt == 2))
                last.then_inc(weighted, 1)

            def transpose_x(ps, src, c):
                for t in range(QT):
                    last = nc.tensor.transpose(ps[0:KH, P * t:P * t + P], src[:, t, KH * c:KH * c + KH], ident[0:P, 0:P])
                return last

            def misc(name, b, par, u, get):
                ps = psM[u.bank]

                def wait_sources(*uses):
                    for source in uses:
                        if source.bank != u.bank:
                            wait_copied(pe, source)
                if name in ("T0", "T1"):
                    pe.wait_ge(xn_ready, b + 1)
                elif name in ("Q0", "V0"):
                    wait_sources(get("T0"), get("T1"))
                elif name[:2] == "MT":
                    pe.wait_ge(shift_ready, 3 * b + int(name[2]) + 1)
                elif name in ("N0", "N1", "N2"):
                    pe.wait_ge(o_read, 3 * b + int(name[1]) + 2)
                elif name == "ON0":
                    pe.wait_ge(o_ready, 3 * b + 3)
                elif name == "OUT0":
                    wait_sources(get("ON0"), get("ON1"))
                elif name == "X0":
                    pe.wait_ge(xf_ready, b + 2)
                elif name == "LG":
                    wait_sources(get("X0"), get("X1"))
                elif name == "RK":
                    pe.wait_ge(oh_ready, b + 1)
                if not (isinstance(u.prior, int) and u.prior == 0):
                    pe.wait_ge(misc_free[u.bank], u.prior)
                if name[0] == "T":
                    last = transpose_x(ps, xn[par], int(name[1]))
                elif name[0] in "QK":
                    m = (0 if name[0] == "Q" else 2) + int(name[1])
                    for c in range(2):
                        last = nc.tensor.matmul(ps[0:KH, 0:NTOK], w_qk[:, c, m, :], xnT[:, c, :],
                                                start=(c == 0), stop=(c == 1))
                elif name[0] == "V":
                    for i, t in enumerate(((0, 1), (2,))[int(name[1])]):
                        for c in range(2):
                            last = nc.tensor.matmul(ps[0:P, D * i:D * i + D], xnT[:, c, P * t:P * t + P],
                                                    w_qkv[:, c, 2 * D:3 * D], start=(c == 0), stop=(c == 1))
                elif name[:2] == "MT":
                    rows = ps[:, :].bitcast(bf16)
                    for t in range(QT):
                        last = nc.tensor.transpose(rows[0:8, P * t + t:P * t + t + P],
                                                   shift[:, t, :, :].rearrange("p s j -> p (s j)"), identb[0:P, 0:P])
                elif name in ("N0", "N1", "N2"):
                    g = int(name[1])
                    for t in range(QT):
                        last = nc.tensor.transpose(ps[0:P, 128 * t:128 * t + 128],
                                                   O_sb[(g + par) % 2][:, P * t:P * t + P], ident[:, :])
                elif name[:2] == "ON":
                    last = transpose_x(ps, On[par], int(name[2]))
                elif name[:3] == "OUT":
                    for i, t in enumerate(((0, 1), (2,))[int(name[3])]):
                        for c in range(2):
                            last = nc.tensor.matmul(ps[0:P, D * i:D * i + D], OnT[:, c, P * t:P * t + P],
                                                    w_out[:, c, :], start=(c == 0), stop=(c == 1))
                elif name[0] == "X":
                    last = transpose_x(ps, xf, int(name[1]))
                elif name == "LG":
                    for t in range(QT):
                        for c in range(2):
                            last = nc.tensor.matmul(ps[0:P, E * t:E * t + E], xfT[:, c, P * t:P * t + P],
                                                    w_sw[:, c, :], start=(c == 0), stop=(c == 1))
                else:
                    nc.tensor.matmul(ps[0:P, 0:E * (QT + 1)], tri[:, :], oh[:, :, :], start=True, stop=False)
                    for t in range(QT):
                        last = nc.tensor.matmul(ps[0:P, E * (t + 1):E * (QT + 1)], ones[:, :],
                                                oh[:, t:t + 1, :].broadcast_to([P, QT - t, E]),
                                                start=False, stop=(t == QT - 1))
                last.then_inc(misc_ready, 1)

            def start_misc(i, b):
                u = use("start", i)
                base = 0 if i < len(AFTER) + 2 else len(AFTER) + 2
                misc(START[i], b, b, u, lambda name: use("start", base + AFTER.index(name)))
            for i in range(len(START) - 1):
                start_misc(i, 0 if i < len(AFTER) + 2 else 1)
            pe.wait_ge(padded, 1)
            pe.wait_ge(stack_loaded, 128)
            for k in range(LEAD):
                score(0, 0, 2 * k)
                score(0, 0, 2 * k + 1)
                if k == 6:
                    start_misc(len(START) - 1, 0)

            def body(b, par, tail, ln, prep):
                n = b + 1
                for i in range(SLOTS):
                    k = i + LEAD
                    if k < SLOTS:
                        score(b, par, 2 * k)
                        score(b, par, 2 * k + 1)
                    elif prep:
                        if k == SLOTS:
                            pe.wait_ge(stack_loaded, 128 * n + 128)
                        score(n, 1 - par, 2 * (k - SLOTS))
                        score(n, 1 - par, 2 * (k - SLOTS) + 1)
                    shifted_score(b, par, 2 * i)
                    shifted_score(b, par, 2 * i + 1)
                    if i == 1 and tail:
                        weigh(b - 1, 1 - par, 8)
                    elif i % 2 and i > 1:
                        weigh(b, par, i // 2 - 1)
                    for name in USES.get(i, ()):
                        if name in TAIL:
                            if tail:
                                misc(name, b - 1, 1 - par, use(b, name, tail, ln, prep),
                                     lambda x: use(b, x, tail, ln, prep))
                        elif name in NEXT:
                            if prep:
                                misc(name, n, 1 - par, use(b, name, tail, ln, prep),
                                     (lambda x: use(b - 1, x)) if tail else
                                     (lambda x: use("start", len(AFTER) + 2 + AFTER.index(x))))
                        elif name in AFTER:
                            if ln:
                                misc(name, b + 2, par, use(b, name, tail, ln, prep), lambda x: use(b, x, tail, ln, prep))
                        else:
                            misc(name, b, par, use(b, name, tail, ln, prep), None)

            def final(b, par):
                weigh(b - 1, 1 - par, 8)
                for name in TAIL:
                    misc(name, b - 1, 1 - par, use(b, name), lambda x: use(b, x))
            bodies(pe, body, final)

        @block.scalar
        def _(act):
            act.sem_inc(exped, 2)
            act.sem_inc(xf_ready, 1)
            act.sem_inc(o_read, 1)
            act.wait_ge(prepared, 3)

            def exponent(b, par, u):
                act.wait_ge(shifted, 36 * b + u + 4)
                act.wait_ge(weighted, 9 * b + u // 4 + 1)
                nc.scalar.activation(Pr[u % 12][0:P, :], psE[u % 2][0:P, 0:NTOK], ACT.Exp).then_inc(exped, 1)

            def read_group(b, par, g):
                act.wait_ge(weighted, 9 * b + 3 * g + 3 + 3)
                if not (isinstance(b, int) and b == 0 and g < 2):
                    act.wait_ge(o_ready, 3 * b + g - 1)
                nc.scalar.activation(O_sb[(g + par) % 2][:, :], psO[:, 0:NTOK], ACT.Copy).then_inc(o_read, 1)

            def apply(b, src, dst, rs, nmr, ready, done):
                act.wait_ge(ready, b + 1)
                for t in range(QT):
                    last = nc.scalar.activation(dst[:, t, :], src[:, t, 0:D], ACT.Identity, bias=nmr[:, t:t + 1],
                                                scale=rs[:, t:t + 1])
                last.then_inc(done, 1)

            def apply1(b, par):
                apply(b, h_in[par], xn[par], rstd, neg_mr, scale_ready, xn_ready)

            def apply2(b, par):
                apply(b, row[par], xf, rstd2, neg_mr2, scale2_ready, xf_ready)

            def copy(name, b, par, u):
                ps = psM[u.bank]
                wait_use(act, u)
                free = misc_free[u.bank]
                if name[0] == "T":
                    nc.scalar.activation(xnT[0:KH, int(name[1]), :], ps[0:KH, 0:NTOK], ACT.Copy).then_inc(free, 1)
                elif name[0] in "QK":
                    m = (0 if name[0] == "Q" else 2) + int(name[1])
                    scale = HD ** -0.5 if name[0] == "Q" else 1.0
                    if not (isinstance(b, int) and b == 0):
                        act.wait_ge(stack_stored, 64 * b)
                    nc.scalar.activation(parts[:, m, 0, :], ps[0:KH, 0:NTOK], ACT.Copy, scale=scale).then_inc(qk_hi, 1)
                    nc.scalar.activation(qk_f[:, m, :], ps[0:KH, 0:NTOK], ACT.Copy, scale=scale).then_inc(free, 1)
                elif name[0] == "V":
                    if name == "V0":
                        act.wait_ge(weighted, 3 if isinstance(b, int) and b == 0 else 9 * b - 6)
                    for i, t in enumerate(((0, 1), (2,))[int(name[1])]):
                        last = nc.scalar.activation(V[par][0:P, t, :, 0:HD],
                                                    ps[0:P, D * i:D * i + D].rearrange("p (h d) -> p h d", d=HD), ACT.Copy)
                    last.then_inc(free, 1)
                elif name[:2] == "MT":
                    rows = ps[:, :].bitcast(bf16)
                    nc.scalar.activation(mT[int(name[2])][:, :].rearrange("p (t n) -> p t n", t=QT),
                                         rows[0:8, 0:QT * (P + 1)].rearrange("p (t n) -> p t n", t=QT)[:, :, 0:P], ACT.Copy)\
                      .then_inc(free, 1)
                elif name[:2] == "ON":
                    nc.scalar.activation(OnT[0:KH, int(name[2]), :], ps[0:KH, 0:NTOK], ACT.Copy).then_inc(free, 1)
                else:
                    nc.scalar.activation(xfT[0:KH, int(name[1]), :], ps[0:KH, 0:NTOK], ACT.Copy).then_inc(free, 1)

            def exp_logits(p):
                act.wait_ge(ls_ready, p + 1)
                nc.scalar.activation(ex[:, :, :], ls[:, :, :], ACT.Exp).then_inc(ex_ready, 1)

            apply1(0, 0)
            apply1(1, 1)
            for i, name in enumerate(START):
                copy(name, 1 if len(AFTER) + 2 <= i < len(START) - 1 else 0, 0, use("start", i))
            mine = ("V0", "V1", "ON0", "ON1", "X0", "X1", "T0", "T1", "Q0", "Q1", "K0", "K1", "MT0", "MT1", "MT2")

            def body(b, par, tail, ln, prep):
                def read(i, now):
                    for name in USES.get(i, ()):
                        if name in mine and (name[:2] == "MT") == now and (tail or name not in TAIL) \
                                and (ln or name not in AFTER) and (prep or name not in NEXT):
                            of, q = (b - 1, 1 - par) if name in TAIL else (b + 1, 1 - par) if name in NEXT else \
                                (b + 2, par) if name in AFTER else (b, par)
                            copy(name, of, q, use(b, name, tail, ln, prep))
                for i in range(SLOTS):
                    if i == 2 and tail:
                        read_group(b - 1, 1 - par, 2)
                    if i in (8, 14):
                        read_group(b, par, int(i == 14))
                    if i == 4 and ln:
                        apply1(b + 2, par)
                    if i == 11 and tail:
                        apply2(b - 1, 1 - par)
                    if i == 15 and tail:
                        exp_logits(b - 1)
                    read(i - 1, False)
                    exponent(b, par, 2 * i)
                    exponent(b, par, 2 * i + 1)
                    read(i, True)

            def final(b, par):
                read_group(b - 1, 1 - par, 2)
                copy("ON0", b - 1, 1 - par, use(b, "ON0"))
                copy("ON1", b - 1, 1 - par, use(b, "ON1"))
                apply2(b - 1, 1 - par)
                copy("X0", b - 1, 1 - par, use(b, "X0"))
                copy("X1", b - 1, 1 - par, use(b, "X1"))
                exp_logits(b - 1)
            bodies(act, body, final)

        @block.vector
        def _(dve):
            for w in (w_qkv, w_out, w_sw):
                nc.vector.memset(w[:, :, :], 0.0)
            dve.drain().then_inc(weights_cleared, 1)
            for x in (xnT, xfT, OnT):
                nc.vector.memset(x[:, :, :], 0.0)
            dve.drain()
            for x in (xnT, xfT, OnT):
                nc.vector.memset(x[KH:KH + 1, 1, :], 1.0)
            nc.vector.memset(ones[:, :], 1.0)
            nc.vector.memset(oh[:, QT, :], 0.0)
            nc.vector.memset(zeros[:, :], 0.0)
            nc.vector.memset(mhalf[:, :], -0.5)
            dve.drain().then_inc(prepared, 1)
            dve.sem_inc(maxed, 3)
            dve.wait_ge(const_loaded, 16 * 14)
            nc.vector.tensor_copy(identb[:, :], ident[:, :])
            for c in range(2):
                for m in range(4):
                    nc.vector.tensor_copy(w_qk[:, c, m, :].rearrange("p (d h) -> p d h", d=HD),
                                          w_qkv[:, c, KH * m:KH * m + KH].rearrange("p (h d) -> p d h", d=HD))
            dve.drain().then_inc(prepared, 1)

            def maximum(b, par, u):
                g, r = divmod(u, 12)
                qt, j = divmod(r, 4)
                dve.wait_ge(scored, 36 * b + u + 1)
                nc.vector.reduce_max(neg_max[par][:, qt, 4 * g + j:4 * g + j + 1], psS[u % 3][0:P, 0:NTOK], AX.X,
                                     negate=True).then_inc(maxed, 1)

            def split_shift(b, par, g):
                nm = neg_max[par][:, :, 4 * g:4 * g + 4]
                dve.drain()
                nc.vector.tensor_copy(shift[:, :, 0, :], nm)
                dve.drain()
                nc.vector.tensor_tensor(shift[:, :, 1, :], nm, shift[:, :, 0, :], ALU.subtract)
                dve.drain().then_inc(shift_ready, 1)

            def ln_sums(st, m, nm, ve, signal):
                for t in range(QT):
                    nc.vector.bn_aggr(m[:, t, :], st[:, t, :])
                dve.drain()
                nc.vector.tensor_scalar(nm[:, :], m[:, :, 0], -1.0, None, ALU.mult)
                nc.vector.tensor_scalar(ve[:, :], m[:, :, 1], 1e-5, None, ALU.add).then_inc(signal, 1)

            def ln1_stats(b, par):
                dve.drain()
                if not isinstance(b, int) or b > 0:
                    dve.wait_ge(xn_ready, b)
                dve.wait_ge(h_loaded[par], 8 * (b - par) + 16)
                for t in range(QT):
                    nc.vector.bn_stats(stats[:, t, :], h_in[par][:, t, :])
                dve.drain()

            def ln1_sums():
                ln_sums(stats, mv, neg_mean, var_eps, var_ready)

            def normalise(b, par, g, u):
                wait_use(dve, u)
                v = psM[u.bank][0:P, 0:QT * 128].rearrange("p (t j r) -> p t j r", t=QT, j=4)
                nc.vector.reciprocal(inv[:, :, :], v[:, :, :, HD])
                dve.drain()
                dst = On[par][:, :, 4 * HD * g:4 * HD * (g + 1)].rearrange("p t (j r) -> p t j r", j=4)
                nc.vector.tensor_tensor(dst, v[:, :, :, 0:HD], inv[:, :, :].rearrange("p t (j o) -> p t j o", o=1)
                                        .broadcast_to([P, QT, 4, HD]), ALU.mult).then_inc(misc_free[u.bank], 1)
                dve.drain().then_inc(o_ready, 1)

            def residual(u, half, p, par):
                if half == 0:
                    dve.wait_ge(hres_loaded[par], 8 * (p - par) + 16)
                    dve.wait_ge(rows_free, p + 1)
                    wait_use(dve, u)
                    nc.vector.tensor_tensor(row[par][:, 0:2, 0:D],
                                            psM[u.bank][0:P, 0:2 * D].rearrange("p (t d) -> p t d", t=2),
                                            h_res[par][:, 0:2, :], ALU.add).then_inc(misc_free[u.bank], 1)
                else:
                    wait_use(dve, u)
                    nc.vector.tensor_tensor(row[par][:, 2, 0:D], psM[u.bank][0:P, 0:D], h_res[par][:, 2, :], ALU.add)\
                      .then_inc(misc_free[u.bank], 1)

            def ln2_stats(p, par):
                dve.drain().then_inc(h2_ready, 1)
                dve.wait_ge(xf_ready, p + 1)
                dve.wait_ge(columns_ready, p + 1)
                for t in range(QT):
                    nc.vector.bn_stats(stats2[:, t, :], row[par][:, t, 0:D])
                dve.drain()

            def ln2_sums():
                ln_sums(stats2, mv2, neg_mean2, var_eps2, var2_ready)

            def logits(u, p):
                wait_use(dve, u)
                lg = psM[u.bank][0:P, 0:QT * E].rearrange("p (t e) -> p t e", e=E)
                nc.vector.reduce_max(lmax[:, :], lg, AX.X)
                dve.drain()
                nc.vector.tensor_tensor(ls[:, :, :], lg, lmax[:, :].rearrange("p (t o) -> p t o", o=1)
                                        .broadcast_to([P, QT, E]), ALU.subtract).then_inc(misc_free[u.bank], 1)
                dve.drain().then_inc(ls_ready, 1)

            def route(p, par):
                dve.wait_ge(ex_ready, p + 1)
                nc.vector.reduce_sum(esum[:, :], ex[:, :, :], AX.X)
                nc.vector.scalar_tensor_tensor(out=k8[:, :, :], in0=ex[:, :, :], scalar=1.0, in1=c8[:, :, :],
                                               op0=ALU.is_ge, op1=ALU.mult)
                dve.drain()
                cols = bass.ds(QT * p, QT)
                nc.vector.reciprocal(p_all[:, cols], esum[:, :])
                nc.vector.reduce_max(r_all[:, cols], k8[:, :, :], AX.X)
                dve.drain()
                nc.vector.tensor_copy(row[par][:, :, D + 2], p_all[:, cols])
                nc.vector.tensor_tensor(oh[:, 0:QT, :], c8[:, :, :], r_all[:, cols].rearrange("p (t o) -> p t o", o=1)
                                        .broadcast_to([P, QT, E]), ALU.is_equal)
                dve.drain().then_inc(oh_ready, 1)

            def places(u, p, par):
                wait_use(dve, u)
                psR = psM[u.bank]
                nc.vector.tensor_tensor(place[:, :, :], psR[0:P, 0:QT * E].rearrange("p (t e) -> p t e", e=E),
                                        run[:, :].rearrange("p (o e) -> p o e", o=1).broadcast_to([P, QT, E]), ALU.add)
                dve.drain()
                nc.vector.tensor_tensor(run[:, :], run[:, :], psR[0:P, QT * E:QT * E + E], ALU.add)\
                    .then_inc(misc_free[u.bank], 1)
                nc.vector.tensor_tensor(place[:, :, :], place[:, :, :], oh[:, 0:QT, :], ALU.mult)
                dve.drain()
                nc.vector.reduce_sum(slotf[:, :], place[:, :, :], AX.X)
                dve.drain()
                nc.vector.tensor_copy(slot[par][:, :], slotf[:, :])
                dve.drain().then_inc(row_ready, 1)

            for b in range(2):
                ln1_stats(b, b)
                ln1_sums()
            for i in range(2):
                nc.vector.memset(Qs[i][KH:128, :, :], 0.0)
                nc.vector.memset(Ks[i][KH:128, :, :], 0.0)
            dve.drain()
            for i in range(2):
                nc.vector.memset(Ks[i][KH:KH + 2, :, :], 1.0)
            dve.drain().then_inc(padded, 1)
            for k in range(LEAD):
                maximum(0, 0, 2 * k)
                maximum(0, 0, 2 * k + 1)
                if k == 5:
                    split_shift(0, 0, 0)

            def body(b, par, tail, ln, prep):
                n, p = b + 1, b - 1
                q = 1 - par

                def at(name):
                    return use(b, name, tail, ln, prep)
                for i in range(SLOTS):
                    if i == 4 and tail:
                        normalise(p, q, 2, at("N2"))
                    if i == 7 and tail:
                        residual(at("OUT0"), 0, p, q)
                    if i == 8 and tail:
                        residual(at("OUT1"), 1, p, q)
                    if i == 10:
                        normalise(b, par, 0, at("N0"))
                    k = i + LEAD
                    if k < SLOTS:
                        maximum(b, par, 2 * k)
                        maximum(b, par, 2 * k + 1)
                    elif prep:
                        maximum(n, q, 2 * (k - SLOTS))
                        maximum(n, q, 2 * (k - SLOTS) + 1)
                    if i == 1 and ln:
                        ln1_stats(b + 2, par)
                    if i == 1:
                        split_shift(b, par, 1)
                    if i == 1 and ln:
                        ln1_sums()
                    if i == 7:
                        split_shift(b, par, 2)
                    if i == 9 and tail:
                        ln2_stats(p, q)
                    if i == 9 and tail:
                        ln2_sums()
                    if i == 13 and prep:
                        split_shift(n, q, 0)
                    if i == 13 and tail:
                        logits(at("LG"), p)
                    if i == 15 and tail:
                        route(p, q)
                    if i == 16:
                        normalise(b, par, 1, at("N1"))
                    if i == 17 and tail:
                        places(at("RK"), p, q)

            def final(b, par):
                p, q = b - 1, 1 - par
                normalise(p, q, 2, use(b, "N2"))
                residual(use(b, "OUT0"), 0, p, q)
                residual(use(b, "OUT1"), 1, p, q)
                ln2_stats(p, q)
                ln2_sums()
                logits(use(b, "LG"), p)
                route(p, q)
                places(use(b, "RK"), p, q)
            bodies(dve, body, final)
            dve.drain().then_inc(finished, 1)

        @block.gpsimd
        def _(pool):
            for p in Pr:
                nc.gpsimd.memset(p[:, :], 0.0)
            for i in range(2):
                nc.gpsimd.memset(V[i][:, :, :, :], 1.0)
            pool.drain().then_inc(prepared, 1)
            pool.wait_ge(prepared, 3)

            def root(b, nm, ve, rs, nmr, ready, rooted, done):
                pool.wait_ge(ready, b + 1)
                nc.gpsimd.tensor_tensor(rs[:, :], ve[:, :], mhalf[:, :], ALU.pow).then_inc(rooted, 1)
                pool.wait_ge(rooted, b + 1)
                nc.gpsimd.tensor_tensor(nmr[:, :], nm[:, :], rs[:, :], ALU.mult).then_inc(done, 1)

            def root1(b):
                root(b, neg_mean, var_eps, rstd, neg_mr, var_ready, rstd_ready, scale_ready)

            def root2(b, par):
                root(b, neg_mean2, var_eps2, rstd2, neg_mr2, var2_ready, rstd2_ready, scale2_ready)
                nc.gpsimd.tensor_copy(row[par][:, :, D], rstd2[:, :])
                nc.gpsimd.tensor_copy(row[par][:, :, D + 1], mv2[:, :, 0])
                nc.gpsimd.tensor_copy(row[par][:, :, D + 3], tok_all[:, bass.ds(QT * b, QT)]).then_inc(columns_ready, 1)

            def split(n, at, names):
                for name in names:
                    m = ("Q0", "Q1", "K0", "K1").index(name)
                    pool.wait_ge(qk_hi, 4 * n + m + 1)
                    wait_copied(pool, at(name))
                    nc.gpsimd.tensor_tensor(qk_r[:, m, :], qk_f[:, m, :], parts[:, m, 0, :], ALU.subtract)\
                      .then_inc(res_done, 1)
                    pool.wait_ge(res_done, 4 * n + m + 1)
                    nc.gpsimd.tensor_tensor(parts[:, m, 1, :], qk_r[:, m, :], zeros[:, :], ALU.add).then_inc(mid_done, 1)
                    pool.wait_ge(mid_done, 4 * n + m + 1)
                    nc.gpsimd.tensor_tensor(parts[:, m, 2, :], qk_r[:, m, :], parts[:, m, 1, :], ALU.subtract)\
                      .then_inc(parts_ready, 1)

            pool.sem_inc(rows_free, 2)
            pool.sem_inc(columns_ready, 1)

            def release(p, par):
                pool.wait_ge(scattered[par], 24 * (p - par) + 48)
                pool.sem_inc(rows_free, 1)

            def scatter(p, par):
                pool.wait_ge(prepared, 3)
                pool.wait_ge(columns_ready, p + 2)
                pool.wait_ge(row_ready, p + 1)
                pool.sem_inc(rows_seen, 1)
                for t in range(QT):
                    pool.indirect_dma_start(xs, bass.IndirectOffsetOnAxis(ap=slot[par][:, t:t + 1], axis=0),
                                            row[par][:, t, :], None).then_inc(scattered[par], 16)
            root1(0)
            root1(1)
            names = ("Q0", "Q1", "K0", "K1")
            split(0, lambda name: use("start", AFTER.index(name)), names)
            split(1, lambda name: use("start", len(AFTER) + 2 + AFTER.index(name)), names)

            def body(b, par, tail, ln, prep):
                def at(name):
                    return use(b, name, tail, ln, prep)
                if ln:
                    root1(b + 2)
                if not isinstance(b, int) or b > 1:
                    release(b - 2, par)
                if ln:
                    split(b + 2, at, names[0:2])
                if tail:
                    root2(b - 1, 1 - par)
                if ln:
                    split(b + 2, at, names[2:4])
                if tail:
                    scatter(b - 1, 1 - par)

            def final(b, par):
                release(b - 2, par)
                root2(b - 1, 1 - par)
                scatter(b - 1, 1 - par)
                release(b - 1, 1 - par)
            bodies(pool, body, final, first=2)


def experts(nc, N, CAPR, NT, xs, p_d, r_d, cnt_d, start_in, tok_in, tile_in, lane_in, eno_in, label_in,
            block_in, first_in, steps_in, ident_in,
            w1, b1, w2, b2, out):
    SHARE = 128 // E
    PT = N // SHARE
    capacity = int(1.25 * N / E)
    RING, GROUP = 8, 4
    with ExitStack() as ctx:
        def sb(name, shape, dt=fp32):
            return ctx.enter_context(nc.sbuf_tensor(name, shape, dt))

        def sem(name):
            return ctx.enter_context(nc.semaphore(name))

        def ps(name, shape):
            return ctx.enter_context(nc.psum_tensor(name, shape, fp32))

        w1_sb = sb("w1_sb", [128, 2, E * F])
        w2_sb = sb("w2_sb", [128, FC, E * D])
        b2_f, b2_r, b2_split = sb("b2_f", [1, E * D]), sb("b2_r", [1, E * D]), sb("b2_split", [1, 3, E * D], bf16)
        b2_sb = sb("b2_sb", [3, E * D], bf16)
        ident, one_row = sb("identC", [128, 128]), sb("one_row", [3, 128], bf16)
        p_all, r_all, tok = sb("p_allC", [128, PT]), sb("r_allC", [128, PT]), sb("tok", [128, PT])
        mine, hit = sb("mine", [128, PT]), sb("hit", [128, PT])
        part, ones = sb("part", [128, 1]), sb("onesC", [128, 128])
        same_expert, first_of, label = sb("same_expert", [128, 128]), sb("first_of", [128, E]), sb("label", [128, 1])
        start, cnt = sb("start", [128, E]), sb("cnt", [128, E])
        thr, moved, cand = (sb(n, [128, 1]) for n in ("thr", "moved", "cand"))
        steps = sb("steps", [128, P_STEPS + T_STEPS + 2])
        room, last_tok, found = sb("room", [128, 1]), sb("last_tok", [128, 1]), sb("found", [128, 2, E])
        expert_thr = sb("expert_thr", [128, 2, E])
        tiles_f, tiles_i = sb("tiles_f", [128, E]), sb("tiles_i", [128, E], i32)
        first, end = sb("first", [128, E]), sb("end", [128, E])
        tile_no, lane, eno = sb("tile_no", [128, NT]), sb("lane", [128, 1]), sb("eno", [128, E])
        own, tmp, off = sb("own", [128, E, NT]), sb("tmp", [128, E, NT]), sb("off", [128, E, NT])
        t_base, t_exp, t_valid = sb("t_base", [128, NT]), sb("t_exp", [128, NT]), sb("t_valid", [128, NT])
        t_thr, t_last, t_used = sb("t_thr", [128, NT]), sb("t_last", [128, NT]), sb("t_used", [128, NT])
        base_i, exp_i = sb("base_i", [1, NT], i32), sb("exp_i", [1, NT], i32)
        zero_rows = sb("zero_rows", [128, RW])
        tail_f, tail_i = sb("tail_f", [128, E]), sb("tail_i", [128, E], i32)
        row = [sb(f"rowC{i}", [128, GROUP, RW]) for i in range(2)]
        xf = [sb(f"xfC{i}", [128, D]) for i in range(RING)]
        xfT = [sb(f"xfTC{i}", [128, 2, 128]) for i in range(2)]
        hid = [sb(f"hid{i}", [128, F]) for i in range(2)]
        hidT = [sb(f"hidT{i}", [128, F]) for i in range(2)]
        over, tie, low, keep, val, idm = (sb(n, [128, GROUP]) for n in ("over", "tie", "low", "keep", "val", "idm"))
        kp, dp = ([sb(f"{n}{i}", [128, GROUP]) for i in range(2)] for n in ("kp", "dp"))
        pre = [sb(f"pre{i}", [128, D]) for i in range(2)]
        res = [sb(f"res{i}", [128, D]) for i in range(RING)]
        dest = [sb(f"dest{i}", [128, GROUP], i32) for i in range(2)]
        psC = ps("psC", [128, 512])
        psX, psH, psT = ps("psX", [128, 512]), ps("psH", [128, 2, 512]), ps("psTr", [128, 2, 512])
        psY = [ps(f"psY{i}", [128, 512]) for i in range(2)]

        small_loaded, weights_loaded, cleared = sem("small_loaded"), sem("weights_loaded"), sem("cleared")
        counted, totalled, tails_ready, tails_done, tables = (sem("counted"), sem("totalled"), sem("tails_ready"),
                                                               sem("tails_done"), sem("tables"))
        row_loaded = [sem(f"row_loaded{i}") for i in range(RING)]
        x_ready, x_tr, x_copied = sem("x_ready"), sem("x_tr"), sem("x_copied")
        h_ready, geluped = sem("h_ready"), sem("gelued")
        ht_ready, ht_dve, ht_act = sem("ht_ready"), sem("ht_dve"), sem("ht_act")
        y_ready, combined = sem("y_ready"), sem("combined")
        rows_seen, b2_parts, pads_cleared = (sem("rows_seen"), sem("b2_parts"),
                                                       sem("pads_cleared"))
        scat = [sem(f"scat{i}") for i in range(RING)]
        block = ctx.enter_context(nc.Block())
        NSMALL = 14

        @block.sync
        def _(sp):
            def shares(a):
                return a.rearrange("p (o n) -> o (p n)", o=1).rearrange("o (s n) -> o s n", s=SHARE)\
                        .broadcast_to([E, SHARE, PT])
            for dst, src in ((p_all[:, :], shares(p_d)), (r_all[:, :], shares(r_d)), (tok[:, :], shares(tok_in)),
                             (start[:, :], start_in), (cnt[:, :], cnt_d[0:1, :].broadcast_to([128, E])),
                             (tile_no[:, :], tile_in), (lane[:, :], lane_in), (eno[:, :], eno_in),
                             (label[:, :], label_in), (same_expert[:, :], block_in), (first_of[:, :], first_in),
                             (steps[:, :], steps_in), (ident[:, :], ident_in),
                             (b2_f[:, :], b2.rearrange("(o e) d -> o (e d)", o=1))):
                sp.dma_start(dst, src).then_inc(small_loaded, 16)
            for c in range(2):
                sp.dma_start(w1_sb[0:KH, c, :].rearrange("k (e f) -> k e f", e=E),
                             w1[:, KH * c:KH * c + KH, :].rearrange("e k f -> k e f")).then_inc(weights_loaded, 16)
            sp.wait_ge(pads_cleared, 1)
            sp.dma_start(w1_sb[KH:KH + 1, 1, :], b1.rearrange("e f -> (e f)").rearrange("(o n) -> o n", o=1))\
              .then_inc(weights_loaded, 16)
            for e in range(E):
                sp.dma_start(w2_sb[:, :, D * e:D * e + D], w2[e].rearrange("(c p) n -> p c n", p=128))\
                  .then_inc(weights_loaded, 16)
            sp.wait_ge(b2_parts, 1)
            sp.dma_start(b2_sb[:, :], b2_split[:, :, :]).then_inc(weights_loaded, 16)
            sp.wait_ge(tables, 1)
            sp.wait_ge(tails_done, 16 * (E + 1))

            def load(t, r):
                base = sp.value_load(base_i[0:1, bass.ds(t, 1)], min_val=0, max_val=E * CAPR)
                sp.dma_start(row[r // GROUP][:, r % GROUP, :], xs[bass.ds(base, 128), :]).then_inc(row_loaded[r], 16)
            for r in range(RING):
                load(r, r)
            with sp.Fori(0, NT // RING - 1, 1) as k:
                for r in range(RING):
                    sp.wait_ge(tables, 1)
                    sp.wait_ge(combined, RING * k + r + 1)
                    load(RING * k + r + RING, r)

        @block.tensor
        def _(pe):
            pe.wait_ge(cleared, 1)
            pe.wait_ge(small_loaded, 16 * NSMALL)

            def total(i):
                pe.wait_ge(counted, i + 1)
                nc.tensor.matmul(psC[:, 0:1], same_expert[:, :], part[:, :], start=True, stop=True).then_inc(totalled, 1)
            with pe.Fori(0, P_STEPS // 3, 1) as k:
                for i in range(3):
                    total(3 * k + i)
            total(P_STEPS)
            with pe.Fori(0, T_STEPS // 3, 1) as k:
                for i in range(3):
                    total(3 * k + P_STEPS + 1 + i)
            pe.wait_ge(counted, P_STEPS + T_STEPS + 2)
            nc.tensor.matmul(psC[:, 0:2 * E], ones[:, :], found[:, :, :], start=True, stop=True).then_inc(totalled, 1)
            pe.wait_ge(weights_loaded, 16 * 12)
            pe.wait_ge(tables, 1)

            def x_transpose(t, r):
                pe.wait_ge(x_ready, t + 1)
                pe.wait_ge(x_copied, t + 1)
                for c in range(2):
                    last = nc.tensor.transpose(psX[0:KH, 128 * c:128 * c + 128], xf[r][:, KH * c:KH * c + KH], ident[:, :])
                last.then_inc(x_tr, 1)

            def first_layer(t, r):
                e = pe.value_load(exp_i[0:1, bass.ds(t, 1)], min_val=0, max_val=E - 1)
                pe.wait_ge(x_copied, t + 2)
                pe.wait_ge(geluped, t + 1)
                for n in range(2):
                    for c in range(2):
                        last = nc.tensor.matmul(psH[:, n, 0:F // 2], xfT[r % 2][:, c, :],
                                                w1_sb[:, c, bass.ds(e * F + n * (F // 2), F // 2)],
                                                start=(c == 0), stop=(c == 1))
                last.then_inc(h_ready, 1)

            def hid_transpose(t, r):
                pe.wait_ge(geluped, t + 2)
                pe.wait_ge(ht_dve, t + 1)
                pe.wait_ge(ht_act, t + 1)
                for f in range(FC):
                    last = nc.tensor.transpose(psT[:, f // 3, 128 * (f % 3):128 * (f % 3) + 128],
                                               hid[r % 2][:, 128 * f:128 * f + 128], ident[:, :])
                last.then_inc(ht_ready, 1)

            def second_layer(t, r):
                e = pe.value_load(exp_i[0:1, bass.ds(t, 1)], min_val=0, max_val=E - 1)
                pe.wait_ge(ht_dve, t + 2)
                pe.wait_ge(ht_act, t + 2)
                for f in range(FC):
                    nc.tensor.matmul(psY[r % 2][:, 0:D], hidT[r % 2][:, 128 * f:128 * f + 128],
                                     w2_sb[:, f, bass.ds(e * D, D)], start=(f == 0), stop=False)
                nc.tensor.matmul(psY[r % 2][:, 0:D], one_row[:, :], b2_sb[:, bass.ds(e * D, D)], start=False, stop=True)\
                  .then_inc(y_ready, 1)
            x_transpose(0, 0)
            first_layer(0, 0)
            x_transpose(1, 1)

            def step(t, r):
                hid_transpose(t, r)
                if not isinstance(t, int) or t + 1 < NT:
                    first_layer(t + 1, (r + 1) % RING)
                if not isinstance(t, int) or t + 2 < NT:
                    x_transpose(t + 2, (r + 2) % RING)
                second_layer(t, r)
            with pe.Fori(0, NT // RING - 1, 1) as k:
                for r in range(RING):
                    step(RING * k + r, r)
            for t in range(NT - RING, NT):
                step(t, t % RING)

        @block.scalar
        def _(act):
            act.sem_inc(x_copied, 1)
            act.sem_inc(geluped, 1)
            act.sem_inc(ht_act, 1)
            act.wait_ge(cleared, 1)

            def x_copy(t, r):
                act.wait_ge(x_tr, t + 1)
                nc.scalar.activation(xfT[r % 2][0:KH, :, :], psX[0:KH, 0:256].rearrange("p (c n) -> p c n", c=2), ACT.Copy)\
                  .then_inc(x_copied, 1)

            def gelu(t, r):
                act.wait_ge(h_ready, t + 1)
                nc.scalar.activation(hid[r % 2][:, :].rearrange("p (n f) -> p n f", n=2), psH[:, :, 0:F // 2], ACT.Gelu)\
                   .then_inc(geluped, 1)

            def hid_copy(t, r):
                act.wait_ge(ht_ready, t + 1)
                nc.scalar.activation(hidT[r % 2][:, 384:768], psT[:, 1, 0:384], ACT.Copy).then_inc(ht_act, 1)
            x_copy(0, 0)
            gelu(0, 0)
            x_copy(1, 1)

            def step(t, r):
                hid_copy(t, r)
                if not isinstance(t, int) or t + 1 < NT:
                    gelu(t + 1, r + 1)
                if not isinstance(t, int) or t + 2 < NT:
                    x_copy(t + 2, r)
            with act.Fori(0, NT // RING - 1, 1) as k:
                for r in range(RING):
                    step(RING * k + r, r)
            for t in range(NT - RING, NT):
                step(t, t % RING)

        @block.vector
        def _(dve):
            nc.vector.memset(one_row[:, :], 1.0)
            nc.vector.memset(ones[:, :], 1.0)
            nc.vector.memset(zero_rows[:, :], 0.0)
            nc.vector.memset(thr[:, :], 0.0)
            nc.vector.memset(last_tok[:, :], 0.0)
            nc.vector.memset(cand[:, :], 0.5)
            nc.vector.memset(moved[:, :], 0.0)
            for i in range(2):
                nc.vector.memset(xfT[i][:, :, :], 0.0)
            dve.drain()
            for i in range(2):
                nc.vector.memset(xfT[i][KH:KH + 1, 1, :], 1.0)
            dve.drain().then_inc(cleared, 1)
            dve.sem_inc(ht_dve, 1)
            dve.wait_ge(small_loaded, 16 * NSMALL)

            def bc(a, n=NT):
                return a[:, 0:E].rearrange("p (e o) -> p e o", o=1).broadcast_to([a.shape[0], E, n])

            def bt(a):
                return a[:, :].rearrange("p (o n) -> p o n", o=1).broadcast_to([128, E, NT])
            tt, ts = nc.vector.tensor_tensor, nc.vector.tensor_scalar
            ts(tail_f[:, :], cnt[:, :], lane[:, 0:1], None, ALU.add)
            tt(cnt[:, :], cnt[:, :], start[:, :], ALU.subtract)
            dve.drain()
            nc.vector.tensor_copy(tail_i[:, :], tail_f[:, :])
            dve.drain().then_inc(tails_ready, 1)
            ts(tiles_f[:, :], cnt[:, :], 1.0 / 128, 127.0 / 128 - 0.498, ALU.mult, ALU.add)
            dve.drain()
            nc.vector.tensor_copy(tiles_i[:, :], tiles_f[:, :])
            dve.drain()
            nc.vector.tensor_copy(end[:, :], tiles_i[:, :])
            dve.drain()
            for e in range(1, E):
                tt(end[:, e:e + 1], end[:, e:e + 1], end[:, e - 1:e], ALU.add)
                dve.drain()
            tt(first[:, :], end[:, :], tiles_i[:, :], ALU.subtract)
            dve.drain()
            tt(own[:, :, :], bt(tile_no), bc(first), ALU.is_ge)
            tt(tmp[:, :, :], bt(tile_no), bc(end), ALU.is_ge)
            tt(off[:, :, :], bt(tile_no), bc(first), ALU.subtract)
            dve.drain()
            tt(own[:, :, :], own[:, :, :], tmp[:, :, :], ALU.subtract)
            ts(off[:, :, :], off[:, :, :], 128.0, None, ALU.mult)
            dve.drain()

            def table(dst, value):
                tt(tmp[:, :, :], own[:, :, :], value, ALU.mult)
                dve.drain()
                nc.vector.reduce_sum(dst[:, :], tmp[:, :, :].rearrange("p e n -> p n e"), AX.X)
                dve.drain()
            nc.vector.reduce_sum(t_used[:, :], own[:, :, :].rearrange("p e n -> p n e"), AX.X)
            table(t_exp, bc(eno))
            table(t_base, bc(start))
            table(t_valid, off[:, :, :])
            tt(t_base[:, :], t_base[:, :], t_valid[:, :], ALU.add)
            ts(t_used[:, :], t_used[:, :], -float(E * CAPR), float(E * CAPR), ALU.mult, ALU.add)
            dve.drain()
            tt(t_base[:, :], t_base[:, :], t_used[:, :], ALU.add)
            dve.drain()
            nc.vector.tensor_copy(base_i[:, :], t_base[0:1, :])
            nc.vector.tensor_copy(exp_i[:, :], t_exp[0:1, :])
            dve.drain().then_inc(tables, 1)
            tt(off[:, :, :], bc(cnt), off[:, :, :], ALU.subtract)
            dve.drain()
            table(t_valid, off[:, :, :])
            nc.vector.scalar_tensor_tensor(out=mine[:, :], in0=r_all[:, :], scalar=label[:, 0:1], in1=p_all[:, :],
                                           op0=ALU.is_equal, op1=ALU.mult)
            dve.drain()

            def count(i, than, op):
                ts(hit[:, :], mine[:, :], than[:, 0:1], 0.0, op, ALU.add, accum_out=part[:, :]).then_inc(counted, 1)

            def search(i, value, op, room_op, limit):
                count(i, cand, op)
                tt(value[:, :], value[:, :], moved[:, :], ALU.add)
                dve.drain()
                dve.wait_ge(totalled, i + 1)
                nc.vector.scalar_tensor_tensor(out=moved[:, :], in0=psC[:, 0:1], scalar=limit,
                                               in1=steps[:, bass.ds(i, 1)], op0=room_op, op1=ALU.mult)
                dve.drain()
                nc.vector.scalar_tensor_tensor(out=cand[:, :], in0=moved[:, :], scalar=value[:, 0:1],
                                               in1=steps[:, bass.ds(i + 1, 1)], op0=ALU.add, op1=ALU.add)
                dve.drain()
            with dve.Fori(0, P_STEPS // 3, 1) as k:
                for i in range(3):
                    search(3 * k + i, thr, ALU.is_ge, ALU.is_ge, float(capacity))
            tt(thr[:, :], thr[:, :], moved[:, :], ALU.add)
            dve.drain()
            count(P_STEPS, thr, ALU.is_gt)
            dve.wait_ge(totalled, P_STEPS + 1)
            ts(room[:, :], psC[:, 0:1], -1.0, float(capacity), ALU.mult, ALU.add)
            ts(hit[:, :], mine[:, :], thr[:, 0:1], 2.0 ** 20, ALU.not_equal, ALU.mult)
            nc.vector.tensor_copy(cand[:, :], steps[:, P_STEPS + 1:P_STEPS + 2])
            nc.vector.memset(moved[:, :], 0.0)
            dve.drain()
            tt(mine[:, :], hit[:, :], tok[:, :], ALU.add)
            dve.drain()
            with dve.Fori(0, T_STEPS // 3, 1) as k:
                for i in range(3):
                    search(3 * k + P_STEPS + 1 + i, last_tok, ALU.is_lt, ALU.is_le, room[:, 0:1])
            tt(last_tok[:, :], last_tok[:, :], moved[:, :], ALU.add)
            dve.drain()
            for i, value in enumerate((thr, last_tok)):
                ts(found[:, i, :], first_of[:, :], value[:, 0:1], None, ALU.mult)
            dve.drain().then_inc(counted, 1)
            dve.wait_ge(totalled, P_STEPS + T_STEPS + 2)
            nc.vector.tensor_copy(expert_thr[:, :, :], psC[:, 0:2 * E].rearrange("p (i e) -> p i e", i=2))
            dve.drain()
            table(t_thr, bc(expert_thr[:, 0, :]))
            table(t_last, bc(expert_thr[:, 1, :]))

            def normalise(t, r, loads):
                if loads is not None:
                    dve.wait_ge(row_loaded[r], loads)
                src = row[r // GROUP][:, r % GROUP, :]
                ts(xf[r][:, :], src[:, 0:D], src[:, D + 1:D + 2], src[:, D:D + 1], ALU.subtract, ALU.mult)\
                    .then_inc(x_ready, 1)

            def decide(g, half, scattered):
                for j in range(GROUP):
                    dve.wait_ge(row_loaded[GROUP * half + j], 16 * scattered + 16)
                p, tk = row[half][:, :, D + 2], row[half][:, :, D + 3]
                cols = bass.ds(GROUP * g, GROUP)
                tt(over[:, :], p, t_thr[:, cols], ALU.is_gt)
                tt(tie[:, :], p, t_thr[:, cols], ALU.is_equal)
                tt(low[:, :], tk, t_last[:, cols], ALU.is_lt)
                tt(val[:, :], lane[:, :].broadcast_to([128, GROUP]), t_valid[:, cols], ALU.is_lt)
                ts(idm[:, :], tk, -float(NOWHERE), None, ALU.add)
                dve.drain()
                tt(tie[:, :], tie[:, :], low[:, :], ALU.mult)
                tt(idm[:, :], idm[:, :], val[:, :], ALU.mult)
                dve.drain()
                tt(keep[:, :], over[:, :], tie[:, :], ALU.max)
                if not (isinstance(scattered, int) and scattered == 0):
                    for j in range(GROUP):
                        dve.wait_ge(scat[GROUP * half + j], 16 * scattered)
                ts(dest[half][:, :], idm[:, :], float(NOWHERE), None, ALU.add)
                dve.drain()
                tt(kp[half][:, :], keep[:, :], p, ALU.mult)
                dve.drain()
                tt(dp[half][:, :], p, kp[half][:, :], ALU.subtract)
                dve.drain()

            def hid_copy(t, r):
                dve.wait_ge(ht_ready, t + 1)
                nc.vector.tensor_copy(hidT[r % 2][:, 0:384], psT[:, 0, 0:384]).then_inc(ht_dve, 1)

            def dropped(t, r):
                half, j = divmod(r, GROUP)
                nc.vector.scalar_tensor_tensor(out=pre[r % 2][:, :], in0=xf[r][:, :], scalar=dp[half][:, j:j + 1],
                                               in1=row[half][:, j, 0:D], op0=ALU.mult, op1=ALU.add)
                dve.drain()

            def combine(t, r):
                half, j = divmod(r, GROUP)
                dve.wait_ge(y_ready, t + 1)
                nc.vector.scalar_tensor_tensor(out=res[r][:, :], in0=psY[r % 2][:, 0:D], scalar=kp[half][:, j:j + 1],
                                               in1=pre[r % 2][:, :], op0=ALU.mult, op1=ALU.add).then_inc(combined, 1)

            def step_ring(k, first, last):
                for r in range(RING):
                    t = RING * k + r
                    hid_copy(t, r)
                    if not (first and r == 0):
                        combine(t - 1, (r - 1) % RING)
                    if not (last and r + 2 >= RING):
                        normalise(t + 2, (r + 2) % RING, 16 * k + (16 if r + 2 < RING else 32))
                    dropped(t, r)
                    if r == 1:
                        decide(2 * k + 1, 1, k)
                    if r == GROUP + 1 and not last:
                        decide(2 * k + 2, 0, k + 1)
            for t in range(2):
                normalise(t, t, 16)
            decide(0, 0, 0)
            step_ring(0, True, False)
            with dve.Fori(1, NT // RING - 1, 1) as k:
                step_ring(k, False, False)
            step_ring(NT // RING - 1, False, True)
            combine(NT - 1, RING - 1)

        @block.gpsimd
        def _(pool):
            nc.gpsimd.memset(w1_sb[KH:128, :, :], 0.0)
            pool.drain().then_inc(pads_cleared, 1)
            pool.wait_ge(tails_ready, 1)
            pool.dma_start(xs[E * CAPR:E * CAPR + 128, :], zero_rows[:, :]).then_inc(tails_done, 16)
            for e in range(E):
                pool.indirect_dma_start(xs, bass.IndirectOffsetOnAxis(ap=tail_i[:, e:e + 1], axis=0),
                                        zero_rows[:, :], None).then_inc(tails_done, 16)

            nc.gpsimd.tensor_copy(b2_split[:, 0, :], b2_f[:, :])
            pool.drain()
            nc.gpsimd.tensor_tensor(b2_r[:, :], b2_f[:, :], b2_split[:, 0, :], ALU.subtract)
            pool.drain()
            nc.gpsimd.tensor_copy(b2_split[:, 1, :], b2_r[:, :])
            pool.drain()
            nc.gpsimd.tensor_tensor(b2_split[:, 2, :], b2_r[:, :], b2_split[:, 1, :], ALU.subtract)
            pool.drain().then_inc(b2_parts, 1)

            def write(t, r):
                pool.wait_ge(combined, t + 1)
                pool.sem_inc(rows_seen, 1)
                pool.indirect_dma_start(out, bass.IndirectOffsetOnAxis(ap=dest[r // GROUP][:, r % GROUP:r % GROUP + 1],
                                                                       axis=0), res[r][:, :], None,
                                        bounds_check=N - 1, oob_is_err=False).then_inc(scat[r], 16)
            with pool.Fori(0, NT // RING, 1) as k:
                for r in range(RING):
                    write(RING * k + r, r)
            for r in range(RING):
                pool.wait_ge(scat[r], 16 * (NT // RING))


ROWS_PER_EXPERT = BATCH * NTOK + 128
TILES = (BATCH * NTOK + 127 * E) // 128
TILES += -TILES % 8


def _constants():
    place = np.arange(TXT, dtype=np.float32)[:, None]
    dim = np.arange(D, dtype=np.float32)[None, :]
    angle = place / np.power(np.float32(10000.0), np.floor(dim / 2) * 2 / np.float32(D)).astype(np.float32)
    here = np.arange(NTOK).reshape(QT, P).T
    outside = np.where(here < TXT, here + NIMG, here - TXT)
    tok = outside[:, None, :] + NTOK * np.arange(BATCH)[None, :, None]
    start = np.arange(E, dtype=np.float32) * ROWS_PER_EXPERT

    def on(a, n):
        return np.ascontiguousarray(np.broadcast_to(a, (n,) + a.shape)).astype(np.float32)
    return {
        "pos": np.where(np.arange(D) % 2 == 0, np.sin(angle), np.cos(angle)).astype(np.float32),
        "ident": np.eye(128, dtype=np.float32),
        "before": np.triu(np.ones((P, P), np.float32), 1),
        "c8": on(np.broadcast_to(E - np.arange(E, dtype=np.float32), (QT, E)), P),
        "tok": tok.reshape(P, BATCH * QT).astype(np.float32),
        "start": on(start, 128),
        "tile_no": on(np.arange(TILES), 128),
        "lane": np.arange(128, dtype=np.float32)[:, None].copy(),
        "expert_no": on(np.arange(E), 128),
        "label": (E - np.arange(128) * E // 128).astype(np.float32)[:, None],
        "steps": on(2.0 ** np.concatenate([-np.arange(1, P_STEPS + 2), T_STEPS - 1 - np.arange(T_STEPS + 1)]), 128),
        "same_expert": np.kron(np.eye(E), np.ones((128 // E, 128 // E))).astype(np.float32),
        "first_of": (np.arange(128)[:, None] == 128 // E * np.arange(E)).astype(np.float32),
    }


def build(nc, t, out):
    def scratch(name, shape, dt=fp32):
        return nc.dram_tensor(name, shape, dt, kind="Internal").ap()
    h = scratch("h_rows", (BATCH, NTOK, D))
    xs = scratch("routed_rows", (E * ROWS_PER_EXPERT + 128, RW))
    stack = scratch("qk_parts", (2, 4, 3, KH, NTOK), bf16)
    p_all, r_all = scratch("p_rows", (P, BATCH * QT)), scratch("r_rows", (P, BATCH * QT))
    counts = scratch("counts", (P, E))
    patch_embed(nc, t["x"], t["L0_tok_W"], t["L0_tok_b"], t["x_txt"], t["mask_BS_i2_0"], t["L0_txt_token_table"],
                t["L0_txt_segm_table"], t["pos"], t["ident"], h)
    attention(nc, BATCH, h, t["L0_attn_w_qkv"], t["L0_attn_b_qkv"], t["L0_attn_w_out"], t["L0_attn_b_out"],
              t["L0_ffn_switch_w"], t["L0_ffn_switch_b"], t["ident"], t["before"], t["c8"],
              t["tok"], t["start"][0:P, :], xs, stack, p_all, r_all, counts)
    experts(nc, BATCH * NTOK, ROWS_PER_EXPERT, TILES, xs, p_all, r_all, counts, t["start"], t["tok"],
            t["tile_no"], t["lane"], t["expert_no"], t["label"], t["same_expert"],
            t["first_of"], t["steps"], t["ident"], t["L0_ffn_w1"], t["L0_ffn_b1"], t["L0_ffn_w2"],
            t["L0_ffn_b2"], out)


def kernel(**inputs):
    import concourse.bacc as bacc
    from concourse.bass_utils import run_bass_kernel_spmd

    nc = bacc.Bacc("TRN2", target_bir_lowering=False, num_devices=1)
    laid = dict(inputs)
    for name in ("x_txt", "mask_BS_i2_0", "L0_attn_w_qkv", "L0_attn_w_out"):
        laid[name] = np.asarray(inputs[name]).T
    laid.update(_constants())
    arrays, tensors = {}, {}
    for name, a in laid.items():
        a = np.ascontiguousarray(a)
        arrays["in_" + name] = a
        tensors[name] = nc.dram_tensor("in_" + name, a.shape, mybir.dt.from_np(a.dtype), kind="ExternalInput").ap()
    out = nc.dram_tensor("out_rows", (BATCH * NTOK, D), fp32, kind="ExternalOutput").ap()
    build(nc, tensors, out)
    r = run_bass_kernel_spmd(nc, [arrays], core_ids=[0])
    return r.results[0]["out_rows"].reshape(BATCH, NTOK, D)
```
